# Optimizing a Trainium2 kernel written in Bass

```python
import numpy as np
import jax
import jax.numpy as jnp

def _softmax(x, axis=-1):
    return jax.nn.softmax(x, axis=axis)

def _gelu(x):
    return jax.nn.gelu(x, approximate=True)

def _silu(x):
    return jax.nn.silu(x)

def _sigmoid(x):
    return jax.nn.sigmoid(x)

def _layernorm(x, axis=-1, eps=1e-05):
    m = jnp.mean(x, axis=axis, keepdims=True)
    v = jnp.var(x, axis=axis, keepdims=True)
    return (x - m) / jnp.sqrt(v + eps)

def _scatter_add(tgt, idx, src, axis=0):
    return tgt.at[idx].add(src)

def _segment_sum(src, seg, n):
    return jax.ops.segment_sum(src, seg, n)
kernel_name = 'mk_hybrid_d1_jaxref_r8_a5180d'

def setup_inputs(seed: int=0):
    np.random.seed(seed)
    _w = jnp.asarray

    def _L0_attn_a_setup():
        import jax, jax.numpy as jnp
        import numpy as np
        EPS = 1e-05

        def _ln(x, g, b):
            m = jnp.mean(x, axis=-1, keepdims=True)
            v = jnp.mean((x - m) ** 2, axis=-1, keepdims=True)
            return (x - m) * jax.lax.rsqrt(v + EPS) * g + b

        def _forward(x, ln_attn_g, ln_attn_b, Wq, bq, Wk, bk, Wv, bv, ln_conv_g, ln_conv_b, conv_w, conv_b, ln_boom_g, ln_boom_b, Wb, bb, Wu, bu):
            B, S, D = x.shape
            K = conv_w.shape[-1]
            G = D // conv_w.shape[1]
            h = _ln(x, ln_conv_g, ln_conv_b)
            hc = jnp.transpose(h, (0, 2, 1))
            hc = jnp.pad(hc, ((0, 0), (0, 0), (K - 1, 0)))
            conv = jax.lax.conv_general_dilated(hc, conv_w, window_strides=(1,), padding='VALID', dimension_numbers=('NCH', 'OIH', 'NCH'), feature_group_count=G)
            conv = conv + conv_b[None, :, None]
            x = x + jnp.transpose(conv, (0, 2, 1))
            h = _ln(x, ln_attn_g, ln_attn_b)
            q = jnp.einsum('bsd,ed->bse', h, Wq) + bq
            k = jnp.einsum('bsd,ed->bse', h, Wk) + bk
            v = jnp.einsum('bsd,ed->bse', h, Wv) + bv
            scale = jnp.arange(1, S + 1, dtype=x.dtype)[None, :, None]
            pooled_q = jnp.cumsum(q, axis=1) / scale
            pooled_k = jnp.cumsum(pooled_q * k, axis=1) / scale
            x = x + pooled_k * v
            h = _ln(x, ln_boom_g, ln_boom_b)
            h = jax.nn.gelu(jnp.einsum('bsd,ed->bse', h, Wb) + bb, approximate=False)
            h = jnp.einsum('bse,de->bsd', h, Wu) + bu
            return x + h
        key = jax.random.key(seed)
        ks = jax.random.split(key, 8)
        B, S, D, K, G = (4, 256, 128, 4, 4)
        w = lambda k, shape: jax.random.normal(k, shape, jnp.float32) * 0.02
        return {'hidden_states': jax.random.normal(ks[0], (B, S, D), jnp.float32), 'attention_mask': jnp.ones((B, S), jnp.int32), 'ln_attn_g': jnp.ones((D,), jnp.float32), 'ln_attn_b': jnp.zeros((D,), jnp.float32), 'Wq': w(ks[1], (D, D)), 'bq': jnp.zeros((D,), jnp.float32), 'Wk': w(ks[2], (D, D)), 'bk': jnp.zeros((D,), jnp.float32), 'Wv': w(ks[3], (D, D)), 'bv': jnp.zeros((D,), jnp.float32), 'ln_conv_g': jnp.ones((D,), jnp.float32), 'ln_conv_b': jnp.zeros((D,), jnp.float32), 'conv_w': w(ks[4], (D, D // G, K)), 'conv_b': jnp.zeros((D,), jnp.float32), 'ln_boom_g': jnp.ones((D,), jnp.float32), 'ln_boom_b': jnp.zeros((D,), jnp.float32), 'Wb': w(ks[5], (4 * D, D)), 'bb': jnp.zeros((4 * D,), jnp.float32), 'Wu': w(ks[6], (D, 4 * D)), 'bu': jnp.zeros((D,), jnp.float32)}
    _L0_attn_a_in = _L0_attn_a_setup()

    def _L0_attn_b_setup():
        import jax, jax.numpy as jnp
        import numpy as np
        NUM_HEADS = 16
        N_EMBD = 128

        def alibi_bias(num_heads: int, seq_len: int) -> jnp.ndarray:
            pos = jnp.arange(seq_len, dtype=jnp.float32)
            dgrid = pos[None, :] - pos[:, None]
            slopes = 2.0 ** (-8.0 / num_heads * (jnp.arange(num_heads, dtype=jnp.float32) + 1.0))
            bias = slopes[:, None, None] * dgrid[None, :, :]
            return jnp.where(dgrid[None, :, :] > 0, -jnp.inf, bias)
        key = jax.random.key(seed)
        k1, k2, k3 = jax.random.split(key, 3)
        B, L, E = (2, 256, N_EMBD)
        x = jax.random.normal(k1, (B, L, E), dtype=jnp.float32)
        w_in = jax.random.normal(k2, (3 * E, E), dtype=jnp.float32) * 0.02
        w_out = jax.random.normal(k3, (E, E), dtype=jnp.float32) * 0.02
        return {'x': x, 'w_in': w_in, 'w_out': w_out}
    _L0_attn_b_in = _L0_attn_b_setup()

    def _L0_ffn_setup():
        import jax, jax.numpy as jnp
        import numpy as np
        NUM_EXPERTS = 8
        HIDDEN = 128
        FFN = 512
        BATCH = 2
        SEQ = 256
        key = jax.random.key(seed)
        k_x, k_g, k_u, k_d = jax.random.split(key, 4)
        scale_in = 1.0 / np.sqrt(HIDDEN)
        scale_mid = 1.0 / np.sqrt(FFN)
        return {'hidden_states': jax.random.normal(k_x, (BATCH, SEQ, HIDDEN), dtype=jnp.float32), 'Wg': jax.random.normal(k_g, (NUM_EXPERTS, HIDDEN, FFN), dtype=jnp.float32) * scale_in, 'Wu': jax.random.normal(k_u, (NUM_EXPERTS, HIDDEN, FFN), dtype=jnp.float32) * scale_in, 'Wd': jax.random.normal(k_d, (NUM_EXPERTS, FFN, HIDDEN), dtype=jnp.float32) * scale_mid}
    _L0_ffn_in = _L0_ffn_setup()
    _d = {'L0_attn_a_hidden_states': _L0_attn_a_in['hidden_states'], 'L0_attn_a_attention_mask': _L0_attn_a_in['attention_mask'], 'L0_attn_a_ln_attn_g': _L0_attn_a_in['ln_attn_g'], 'L0_attn_a_ln_attn_b': _L0_attn_a_in['ln_attn_b'], 'L0_attn_a_Wq': _L0_attn_a_in['Wq'], 'L0_attn_a_bq': _L0_attn_a_in['bq'], 'L0_attn_a_Wk': _L0_attn_a_in['Wk'], 'L0_attn_a_bk': _L0_attn_a_in['bk'], 'L0_attn_a_Wv': _L0_attn_a_in['Wv'], 'L0_attn_a_bv': _L0_attn_a_in['bv'], 'L0_attn_a_ln_conv_g': _L0_attn_a_in['ln_conv_g'], 'L0_attn_a_ln_conv_b': _L0_attn_a_in['ln_conv_b'], 'L0_attn_a_conv_w': _L0_attn_a_in['conv_w'], 'L0_attn_a_conv_b': _L0_attn_a_in['conv_b'], 'L0_attn_a_ln_boom_g': _L0_attn_a_in['ln_boom_g'], 'L0_attn_a_ln_boom_b': _L0_attn_a_in['ln_boom_b'], 'L0_attn_a_Wb': _L0_attn_a_in['Wb'], 'L0_attn_a_bb': _L0_attn_a_in['bb'], 'L0_attn_a_Wu': _L0_attn_a_in['Wu'], 'L0_attn_a_bu': _L0_attn_a_in['bu'], 'L0_attn_b_w_in': _L0_attn_b_in['w_in'], 'L0_attn_b_w_out': _L0_attn_b_in['w_out'], 'L0_ffn_Wg': _L0_ffn_in['Wg'], 'L0_ffn_Wu': _L0_ffn_in['Wu'], 'L0_ffn_Wd': _L0_ffn_in['Wd']}
    _x0 = _d['L0_attn_a_hidden_states']
    _d['L0_attn_a_hidden_states'] = jax.random.normal(jax.random.fold_in(jax.random.key(seed), 1), (4, 1024, 128), dtype=_x0.dtype)
    del _x0
    return _d

def reference(L0_attn_a_hidden_states, L0_attn_a_attention_mask, L0_attn_a_ln_attn_g, L0_attn_a_ln_attn_b, L0_attn_a_Wq, L0_attn_a_bq, L0_attn_a_Wk, L0_attn_a_bk, L0_attn_a_Wv, L0_attn_a_bv, L0_attn_a_ln_conv_g, L0_attn_a_ln_conv_b, L0_attn_a_conv_w, L0_attn_a_conv_b, L0_attn_a_ln_boom_g, L0_attn_a_ln_boom_b, L0_attn_a_Wb, L0_attn_a_bb, L0_attn_a_Wu, L0_attn_a_bu, L0_attn_b_w_in, L0_attn_b_w_out, L0_ffn_Wg, L0_ffn_Wu, L0_ffn_Wd):

    def _L0_attn_a_ref(hidden_states, attention_mask, ln_attn_g, ln_attn_b, Wq, bq, Wk, bk, Wv, bv, ln_conv_g, ln_conv_b, conv_w, conv_b, ln_boom_g, ln_boom_b, Wb, bb, Wu, bu):
        import jax, jax.numpy as jnp
        import numpy as np
        EPS = 1e-05

        def _ln(x, g, b):
            m = jnp.mean(x, axis=-1, keepdims=True)
            v = jnp.mean((x - m) ** 2, axis=-1, keepdims=True)
            return (x - m) * jax.lax.rsqrt(v + EPS) * g + b

        def _forward(x, ln_attn_g, ln_attn_b, Wq, bq, Wk, bk, Wv, bv, ln_conv_g, ln_conv_b, conv_w, conv_b, ln_boom_g, ln_boom_b, Wb, bb, Wu, bu):
            B, S, D = x.shape
            K = conv_w.shape[-1]
            G = D // conv_w.shape[1]
            h = _ln(x, ln_conv_g, ln_conv_b)
            hc = jnp.transpose(h, (0, 2, 1))
            hc = jnp.pad(hc, ((0, 0), (0, 0), (K - 1, 0)))
            conv = jax.lax.conv_general_dilated(hc, conv_w, window_strides=(1,), padding='VALID', dimension_numbers=('NCH', 'OIH', 'NCH'), feature_group_count=G)
            conv = conv + conv_b[None, :, None]
            x = x + jnp.transpose(conv, (0, 2, 1))
            h = _ln(x, ln_attn_g, ln_attn_b)
            q = jnp.einsum('bsd,ed->bse', h, Wq) + bq
            k = jnp.einsum('bsd,ed->bse', h, Wk) + bk
            v = jnp.einsum('bsd,ed->bse', h, Wv) + bv
            scale = jnp.arange(1, S + 1, dtype=x.dtype)[None, :, None]
            pooled_q = jnp.cumsum(q, axis=1) / scale
            pooled_k = jnp.cumsum(pooled_q * k, axis=1) / scale
            x = x + pooled_k * v
            h = _ln(x, ln_boom_g, ln_boom_b)
            h = jax.nn.gelu(jnp.einsum('bsd,ed->bse', h, Wb) + bb, approximate=False)
            h = jnp.einsum('bse,de->bsd', h, Wu) + bu
            return x + h
        return _forward(hidden_states, ln_attn_g, ln_attn_b, Wq, bq, Wk, bk, Wv, bv, ln_conv_g, ln_conv_b, conv_w, conv_b, ln_boom_g, ln_boom_b, Wb, bb, Wu, bu)

    def _L0_attn_b_ref(x, w_in, w_out):
        import jax, jax.numpy as jnp
        import numpy as np
        NUM_HEADS = 16
        N_EMBD = 128

        def alibi_bias(num_heads: int, seq_len: int) -> jnp.ndarray:
            pos = jnp.arange(seq_len, dtype=jnp.float32)
            dgrid = pos[None, :] - pos[:, None]
            slopes = 2.0 ** (-8.0 / num_heads * (jnp.arange(num_heads, dtype=jnp.float32) + 1.0))
            bias = slopes[:, None, None] * dgrid[None, :, :]
            return jnp.where(dgrid[None, :, :] > 0, -jnp.inf, bias)
        B, L, E = x.shape
        H = NUM_HEADS
        D = E // H
        qkv = jnp.einsum('ble,fe->blf', x, w_in)
        q, k, v = jnp.split(qkv, 3, axis=-1)

        def to_heads(t):
            return t.reshape(B, L, H, D).transpose(0, 2, 1, 3)
        q, k, v = (to_heads(q), to_heads(k), to_heads(v))
        scale = 1.0 / jnp.sqrt(jnp.asarray(D, dtype=x.dtype))
        scores = jnp.einsum('bhqd,bhkd->bhqk', q, k) * scale
        scores = scores + alibi_bias(H, L)[None]
        attn = jax.nn.softmax(scores, axis=-1)
        ctx = jnp.einsum('bhqk,bhkd->bhqd', attn, v)
        ctx = ctx.transpose(0, 2, 1, 3).reshape(B, L, E)
        return jnp.einsum('ble,fe->blf', ctx, w_out)

    def _L0_ffn_ref(hidden_states, Wg, Wu, Wd):
        import jax, jax.numpy as jnp
        import numpy as np
        NUM_EXPERTS = 8
        HIDDEN = 128
        FFN = 512
        BATCH = 2
        SEQ = 256
        B, S, H = hidden_states.shape
        x = hidden_states.reshape(-1, H)

        def expert_step(acc, w):
            wg, wu, wd = w
            h = jax.nn.silu(x @ wg) * (x @ wu)
            return (acc + h @ wd, None)
        acc, _ = jax.lax.scan(expert_step, jnp.zeros_like(x), (Wg, Wu, Wd))
        return acc.reshape(B, S, H)
    x = L0_attn_a_hidden_states
    x = x + _L0_attn_a_ref(_layernorm(x, axis=-1), L0_attn_a_attention_mask, L0_attn_a_ln_attn_g, L0_attn_a_ln_attn_b, L0_attn_a_Wq, L0_attn_a_bq, L0_attn_a_Wk, L0_attn_a_bk, L0_attn_a_Wv, L0_attn_a_bv, L0_attn_a_ln_conv_g, L0_attn_a_ln_conv_b, L0_attn_a_conv_w, L0_attn_a_conv_b, L0_attn_a_ln_boom_g, L0_attn_a_ln_boom_b, L0_attn_a_Wb, L0_attn_a_bb, L0_attn_a_Wu, L0_attn_a_bu)
    x = x + _L0_ffn_ref(_layernorm(x, axis=-1), L0_ffn_Wg, L0_ffn_Wu, L0_ffn_Wd)
    x = x + _L0_attn_b_ref(_layernorm(x, axis=-1), L0_attn_b_w_in, L0_attn_b_w_out)
    x = x + _L0_ffn_ref(_layernorm(x, axis=-1), L0_ffn_Wg, L0_ffn_Wu, L0_ffn_Wd)
    return x

_drawn_inputs = setup_inputs


def setup_inputs(seed=0):
    import zlib

    import numpy as np

    out = dict(_drawn_inputs(seed))
    spreads = {'L0_attn_a_ln_attn_g': (1.0, 0.6),
     'L0_attn_a_ln_attn_b': (0.0, 0.8),
     'L0_attn_a_bq': (0.0, 0.8),
     'L0_attn_a_bk': (0.0, 0.8),
     'L0_attn_a_bv': (0.0, 0.8),
     'L0_attn_a_ln_conv_g': (1.0, 0.2),
     'L0_attn_a_ln_conv_b': (0.0, 0.54),
     'L0_attn_a_conv_b': (0.0, 0.1),
     'L0_attn_a_ln_boom_g': (1.0, 0.6),
     'L0_attn_a_ln_boom_b': (0.0, 2.0),
     'L0_attn_a_bb': (0.0, 2.0),
     'L0_attn_a_bu': (0.0, 0.782)}
    factors = {'L0_attn_a_Wq': 8.0,
     'L0_attn_a_Wk': 8.0,
     'L0_attn_a_Wv': 8.0,
     'L0_attn_b_w_in': 8.0,
     'L0_attn_b_w_out': 8.0,
     'L0_attn_a_Wb': 5.616,
     'L0_attn_a_Wu': 3.559}
    for name, (base, spread) in spreads.items():
        noise = np.random.default_rng([zlib.crc32(name.encode()), seed]).standard_normal(out[name].shape)
        drawn = base * np.exp(spread * noise) if base else spread * noise
        out[name] = jnp.asarray(drawn.astype(out[name].dtype))
    for name, factor in factors.items():
        out[name] = (out[name] * factor).astype(out[name].dtype)
    return out
```

```python
from contextlib import ExitStack

import concourse.bass as bass
import numpy as np
from concourse import mybir

F32 = mybir.dt.float32
F32R = mybir.dt.float32r
BF16 = mybir.dt.bfloat16
I32 = mybir.dt.int32
BF16_NP = mybir.dt.np(BF16)
ALU = mybir.AluOpType
ACT = mybir.ActivationFunctionType
AX = mybir.AxisListType

P = 128
D = 128
B, S = 4, 1024
TOK = B * S
NT = 512
TILES = TOK // NT
SUB = NT // P
BLK = S // P
EPS = 1e-5
TAPS, GROUPS = 4, 4
GW = D // GROUPS
EXPERTS, FFN = 8, 512
CH = EXPERTS * FFN // P
WCOLS = EXPERTS * FFN
HEADS, HD = 16, 8
HG = 4
NG = HEADS // HG
UNITS = B * NG
PARTS = 3
QK_ROWS = PARTS * PARTS * HD
AL_ROWS = 12
K1 = QK_ROWS + AL_ROWS
K2 = K1 + PARTS
MROWS = HG * SUB
SCALE = float(np.float32(1.0) / np.sqrt(np.float32(HD)))
STEPS = [(c, j) for c in range(2) for j in range(SUB * c + SUB)]
NST = len(STEPS) * HG
JOBS = [(h, i) for c in range(2) for h in range(HG) for i in range(SUB * c, SUB * c + SUB)]
JOBS_AFTER = [0, 0, 0, 0, 4, 6, 6, 4, 3, 3, 3, 3]
NEG = -1e30

(R_CONV_G, R_CONV_B, R_CONV_BIAS, R_ATTN_G, R_ATTN_B, R_BQ, R_BK, R_BV, R_BOOM_G, R_BOOM_B, R_BB,
 R_BU) = (0, 1, 2, 3, 4, 5, 6, 7, 8, 9, 10, 14)
PAR_ROWS = 15
T_Q, T_K, T_V, T_BOOM, T_DOWN, T_CONV, T_IN, T_OUT = 0, 1, 2, 3, 7, 11, 15, 18
T_COUNT = 19


def build(nc, ap):
    x_in, out = ap["hidden"], ap["out"]
    with ExitStack() as ctx:
        def sb(name, shape, dt=F32, stack=ctx):
            return stack.enter_context(nc.sbuf_tensor(name, shape, dt))

        def sem(name):
            return ctx.enter_context(nc.semaphore(name))

        x = sb("x", [P, (SUB + TOK // P) * P])
        w_hi = [sb(f"w_hi{m}", [P, WCOLS], F32R) for m in range(3)]
        w_lo = [sb(f"w_lo{m}", [P, WCOLS], F32R) for m in range(3)]
        xn_hi = sb("xn_hi", [P, 2, NT], F32R)
        xn_lo = sb("xn_lo", [P, 2, NT], F32R)
        ident = sb("ident", [P, P])
        identb = sb("identb", [P, P], BF16)
        mask_qk = sb("mask_qk", [P, P], BF16)
        mask_kq = sb("mask_kq", [P, P], BF16)
        par = sb("par", [P, PAR_ROWS])
        win_hi = sb("win_hi", [P, 3 * D], F32R)
        win_lo = sb("win_lo", [P, 3 * D], F32R)
        wout = sb("wout", [P, D])
        half = sb("half", [P, BLK])
        eps = sb("eps", [P, BLK])
        zeros = sb("zeros", [P, BLK])
        zcol = sb("zcol", [P, 1])
        fence = sb("fence", [P, 1])
        st = sb("st", [P, BLK, 6])
        mv = sb("mv", [P, BLK, 2])
        lnw = sb("lnw", [P, 8, BLK])
        ntok = sb("ntok", [P, NT])

        ps = ctx.enter_context(nc.psum_tensor("ps", [P, 8, NT], F32))

        with ExitStack() as pa:
            raw = [sb(f"raw{m}", [P, S], F32, pa) for m in range(3)]
            wt = sb("wt", [P, T_IN * P], F32, pa)
            prow = sb("prow", [PAR_ROWS, P], F32, pa)
            wraw = sb("wraw", [P, 15 * P], F32, pa)
            convraw = sb("convraw", [P, GW * TAPS], F32, pa)
            convx = sb("convx", [P, TAPS, P], F32, pa)
            rinv = sb("rinv", [P, S], F32, pa)
            a0_tok = sb("a0_tok", [P, S], F32, pa)
            hc_tok = sb("hc_tok", [P, S], F32, pa)
            a0T = sb("a0T", [P, S], F32, pa)
            hT = sb("hT", [P, TAPS - 1 + S], F32, pa)
            h2T = sb("h2T", [P, S], F32, pa)
            cq = sb("cq", [P, S], F32, pa)
            pq = sb("pq", [P, S], F32, pa)
            gel = sb("gel", [P, 2, NT], F32, pa)
        with ExitStack() as pf:
            sg = sb("sg", [P, 2, NT], F32, pf)
            hid = sb("hid", [P, 4, NT], F32, pf)
            h_hi = sb("h_hi", [P, 2, NT], F32R, pf)
            h_lo = sb("h_lo", [P, 2, NT], F32R, pf)
            yS = sb("yS", [P, NT], F32, pf)
        with ExitStack() as pt:
            qs = [sb(f"qs{i}", [K2, HG, S], BF16, pt) for i in range(2)]
            ks = [sb(f"ks{i}", [K2, HG, S], BF16, pt) for i in range(2)]
            vp = sb("vp", [P, 2, BLK, HG, 32], F32, pt)
            v_tok = sb("v_tok", [P, BLK, D], F32, pt)
            pr = sb("pr", [P, 2, HG, NT], F32, pt)
            ctxt = sb("ctxt", [P, BLK, D], F32, pt)
            rl = sb("rl", [P, SUB, HG], F32, pt)
            negm = sb("negm", [P, 2, MROWS], F32, pt)
            mpart = sb("mpart", [MROWS, PARTS, P], BF16, pt)
            mres = sb("mres", [MROWS, 2, P], F32, pt)
        with ExitStack() as pp:
            qkp = sb("qkp", [P, TILES, 2, PARTS, NT], BF16, pp)
            qkr = sb("qkr", [P, 2, 2, NT], F32, pp)
            v_out = sb("v_out", [P, TILES, NT], F32, pp)

        qkd = [nc.dram_tensor(n, (PARTS, D, TOK), BF16, kind="Internal").ap() for n in ("qd", "kd")]
        vd = nc.dram_tensor("vd", (TOK, D), F32, kind="Internal").ap()
        md = nc.dram_tensor("md", (2, 2, PARTS, MROWS, P), BF16, kind="Internal").ap()

        names = """x_loaded small_loaded zeros pool_setup conv_loaded
            wraw_T wt_ready par_T par_ready rinv_ready
            raw_loaded split_hi split_lo
            a_st a_mv a_pool a_tokd a_toka a_T a_copyD a_hT a_conv a_a1 a_T5 a_st5 a_mv5 a_n5 a_n5d
            a_T7 a_h2 a_qkv a_d8 a_a2 a_T9 a_st9 a_mv9 a_n9 a_n9d a_T10 a_h3 a_up a_gel a_dn a_y a_T13
            a_x1 stored""".split()
        s = {n: sem(n) for n in names}
        FF_NAMES = "st mv rs norm xT xhi xlo gate up silu prod hhi hlo dn y_done y_out yT xadd".split()
        FS = [{n: sem(f"ff{layer}_{n}") for n in FF_NAMES} for layer in range(2)]
        PREP_NAMES = "st mv rs norm xT xhi xlo qk v first rest second third vcopy stored".split()
        G = {n: sem(f"prep_{n}") for n in PREP_NAMES}
        ATT_NAMES = """init v_loaded loaded0 loaded1 vp scores exp pv o_out oT onorm ctx job reduced mT m_split
            m_parts m_stored m_loaded cT c_out proj xadd""".split()
        T = {n: sem(f"att_{n}") for n in ATT_NAMES}
        block = ctx.enter_context(nc.Block())

        def bank(n):
            return ps[:, n, :]

        def xs(blk, n=1):
            return x[:, bass.ds(blk * P + NT, n * P)]

        def col(r):
            return par[:, r:r + 1]

        def W(slot, n=1):
            return wt[:, slot * P:(slot + n) * P]

        x_blk = x_in.rearrange("b s d -> (b s) d").rearrange("(n p) d -> p n d", p=P)
        o_blk = out.rearrange("b s d -> (b s) d").rearrange("(n p) d -> p n d", p=P)

        SMALL_ROWS = [("ln_conv_g", R_CONV_G), ("ln_conv_b", R_CONV_B), ("conv_b", R_CONV_BIAS),
                      ("ln_attn_g", R_ATTN_G), ("ln_attn_b", R_ATTN_B), ("bq", R_BQ), ("bk", R_BK),
                      ("bv", R_BV), ("ln_boom_g", R_BOOM_G), ("ln_boom_b", R_BOOM_B), ("bu", R_BU)]
        SMALL_MATS = [("Wq", T_Q), ("Wk", T_K), ("Wv", T_V)]
        N_SMALL = len(SMALL_ROWS) + 1 + len(SMALL_MATS) + 4

        def load_small(q):
            q.dma_start(convraw[:], ap["conv_w"].rearrange("o i k -> o (i k)")).then_inc(s["conv_loaded"], 16)
            for n, r in SMALL_ROWS:
                q.dma_start(prow[r:r + 1, :], ap[n].rearrange("(a d) -> a d", a=1)).then_inc(s["small_loaded"], 16)
            q.dma_start(prow[R_BB:R_BB + 4, :], ap["bb"].rearrange("(a d) -> a d", a=4)).then_inc(s["small_loaded"], 16)
            for n, t in SMALL_MATS:
                q.dma_start(wraw[:, t * P:(t + 1) * P], ap[n]).then_inc(s["small_loaded"], 16)
            q.dma_start(wraw[:, T_BOOM * P:(T_BOOM + 4) * P].rearrange("p (c d) -> p c d", c=4),
                        ap["Wb"].rearrange("(c p) d -> p c d", p=P)).then_inc(s["small_loaded"], 16)
            q.dma_start(wraw[:, T_DOWN * P:(T_DOWN + 4) * P], ap["Wu"]).then_inc(s["small_loaded"], 16)
            q.dma_start(wraw[:, 11 * P:14 * P].rearrange("p (c d) -> p c d", c=3),
                        ap["w_in"].rearrange("(c p) d -> p c d", p=P)).then_inc(s["small_loaded"], 16)
            q.dma_start(wraw[:, 14 * P:15 * P], ap["w_out"]).then_inc(s["small_loaded"], 16)

        ffn_src = [ap["Wg"].rearrange("e d f -> d e f"), ap["Wu8"].rearrange("e d f -> d e f"),
                   ap["Wd"].rearrange("e (m p) d -> p (e m) d", p=P)]

        def store_qkv(sp):
            with sp.Fori(0, TILES) as t:
                sp.wait_ge(G["third"], t * 2 + 2)
                sp.wait_ge(G["second"], t * 2 + 2)
                sp.wait_ge(G["first"], t * 2 + 2)
                for m in range(2):
                    sp.dma_start(qkd[m].rearrange("i f t -> f i t")[:, :, bass.ds(t * NT, NT)],
                                 qkp[:, bass.ds(t, 1), m, :, :].rearrange("p a i t -> p (a i) t")
                                 ).then_inc(G["stored"], 16)
                sp.wait_ge(G["vcopy"], t + 1)
                sp.dma_start(vd.rearrange("(n p) d -> p n d", p=P)[:, bass.ds(t * SUB, SUB), :],
                             v_out[:, bass.ds(t, 1), :].rearrange("p a (n d) -> p (a n) d", d=D)
                             ).then_inc(G["stored"], 16)
            sp.wait_ge(G["stored"], 16 * 3 * TILES)

        def attention_loads(sp):
            def load_unit(b, g):
                hs, tok, slot = slice(g * HG, (g + 1) * HG), bass.ds(b * S, S), g % 2
                got = T[f"loaded{slot}"]
                q_rows = qkd[0].rearrange("i (d h) t -> i d h t", h=HEADS)
                k_rows = qkd[1].rearrange("j (d h) t -> (j d) h t", h=HEADS)
                for i in range(PARTS):
                    r = i * PARTS * HD
                    sp.dma_start(ks[slot][r:r + PARTS * HD], k_rows[:, hs, tok]).then_inc(got, 16)
                    for j in range(PARTS):
                        sp.dma_start(qs[slot][r + j * HD:r + (j + 1) * HD], q_rows[i, :, hs, tok]).then_inc(got, 16)
                sp.dma_start(qs[slot][QK_ROWS:K1], ap["al_q"][:, hs, :]).then_inc(got, 16)
                sp.dma_start(ks[slot][QK_ROWS:K2], ap["al_k"][:, hs, :]).then_inc(got, 16)

            def load_v(b):
                sp.dma_start(v_tok[:], vd.rearrange("(n p) d -> p n d", p=P)[:, bass.ds(b * BLK, BLK), :]
                             ).then_inc(T["v_loaded"], 16)

            def load_max(e, slot, c):
                sp.wait_ge(T["m_parts"], e * 3 + 3)
                sp.dma_start(md[slot, c].rearrange("i r q -> r i q"), mpart[:]).then_inc(T["m_stored"], 16)
                sp.wait_ge(T["m_stored"], e * 16 + 16)
                sp.dma_start(qs[slot][K1:K2, :, c * NT:(c + 1) * NT],
                             md[slot, c].rearrange("i (h n) q -> i h (n q)", h=HG)).then_inc(T["m_loaded"], 16)

            load_unit(0, 0)
            load_v(0)
            load_unit(0, 1)
            load_max(0, 0, 0)

            def batch(b, last):
                for g in range(NG):
                    n = b * NG + g
                    load_max(n * 2 + 1, g % 2, 1)
                    if g == NG - 2 and not last:
                        sp.wait_ge(T["vp"], n + 2)
                        load_v(b + 1)
                    if not (last and g == NG - 1):
                        load_max(n * 2 + 2, (g + 1) % 2, 0)
                    if not (last and g >= NG - 2):
                        sp.wait_ge(T["scores"], n * NST + NST)
                        load_unit(b + (g + 2) // NG, (g + 2) % NG)

            with sp.Fori(0, B - 1) as b:
                batch(b, False)
            batch(B - 1, True)

        def w_in_blocks(dst):
            for m, src in enumerate((bank(3)[:, 3 * P:4 * P], bank(4)[:, 0:P], bank(4)[:, P:2 * P])):
                to = dst[:, m * D:(m + 1) * D]
                if m < 2:
                    to, src = to.rearrange("p (d h) -> p h d", h=HEADS), src.rearrange("p (h d) -> p h d", h=HEADS)
                yield to, src

        def part(t, m, i):
            return qkp[:, bass.ds(t, 1), m, i, :].rearrange("p a n -> p (a n)")

        @block.sync
        def _(sp):
            for b in range(B):
                sp.dma_start(x[:, (SUB + b * BLK) * P:(SUB + b * BLK + BLK) * P].rearrange("p (n d) -> p n d", d=D),
                             x_blk[:, b * BLK:(b + 1) * BLK, :]).then_inc(s["x_loaded"], 16)
            with sp.Fori(0, B) as b:
                sp.wait_ge(s["split_lo"], b * 3 + 1)
                for m in range(3):
                    n = 2 if m < 2 else BLK
                    sp.dma_start(raw[m][:, :].rearrange("p (n f) -> p n f", n=n),
                                 ffn_src[m][:, bass.ds(b * n, n), :]).then_inc(s["raw_loaded"], 16)
            sp.wait_ge(s["a_x1"], TILES)
            store_qkv(sp)
            attention_loads(sp)
            sp.wait_ge(T["xadd"], 2 * B)
            sp.wait_ge(FS[1]["xadd"], TILES + 1)
            sp.dma_start(o_blk, x[:, NT:].rearrange("p (n d) -> p n d", d=D)).then_inc(s["stored"], 16)
            sp.wait_ge(s["stored"], 16)

        @block.gpsimd
        def _(pool):
            g = nc.gpsimd
            steps = [0]

            def setup(ins):
                steps[0] += 1
                ins.then_inc(s["pool_setup"], 1)
                pool.wait_ge(s["pool_setup"], steps[0])

            setup(g.memset(ident[:], 0.0))
            setup(g.affine_select(out=ident[:], in_=ident[:], compare_op=ALU.not_equal, fill=1.0, base=0,
                                  pattern=[[-1, P]], channel_multiplier=1))
            setup(g.memset(convx[:], 0.0))
            pool.wait_ge(s["conv_loaded"], 16)
            for gr in range(GROUPS):
                r = slice(gr * GW, (gr + 1) * GW)
                setup(g.tensor_copy(convx[r, :, gr * GW:(gr + 1) * GW],
                                    convraw[r, :].rearrange("o (i k) -> o k i", k=TAPS)))
            setup(g.iota(rinv[:].bitcast(I32), pattern=[[1, S]], base=1, channel_multiplier=0))
            setup(g.memset(half[:], -0.5))
            setup(g.memset(eps[:], EPS))
            g.memset(zeros[:], 0.0).then_inc(s["split_lo"], 1)
            pool.wait_ge(s["split_lo"], 1)
            setup(g.memset(hT[:, 0:TAPS - 1], 0.0))
            setup(g.tensor_copy(identb[:], ident[:]))
            for mask, sign in ((mask_qk, 1), (mask_kq, -1)):
                setup(g.memset(a0_tok[:, 0:P], 0.0))
                setup(g.affine_select(out=a0_tok[:, 0:P], in_=a0_tok[:, 0:P], compare_op=ALU.is_ge, fill=NEG,
                                      base=0, pattern=[[-sign, P]], channel_multiplier=sign))
                setup(g.tensor_copy(mask[:], a0_tok[:, 0:P]))

            def rstd(base, wait, n_wait, first):
                pool.wait_ge(wait, n_wait)
                done = [0]

                def link(ins):
                    done[0] += 1
                    ins.then_inc(s["a_pool"], 1)
                    pool.wait_ge(s["a_pool"], base + done[0])
                var, mean = mv[:, :, 1], mv[:, :, 0]
                link(g.tensor_tensor(lnw[:, 0, :], var, eps[:], ALU.add))
                link(g.tensor_tensor(lnw[:, 1, :], lnw[:, 0, :], half[:], ALU.pow))
                if first:
                    link(g.tensor_tensor(lnw[:, 2, :], lnw[:, 1, :], lnw[:, 1, :], ALU.mult))
                    link(g.tensor_tensor(lnw[:, 3, :], lnw[:, 2, :], var, ALU.mult))
                    link(g.tensor_tensor(lnw[:, 4, :], lnw[:, 3, :], eps[:], ALU.add))
                    link(g.tensor_tensor(lnw[:, 5, :], lnw[:, 4, :], half[:], ALU.pow))
                    link(g.tensor_tensor(lnw[:, 6, :], lnw[:, 5, :], lnw[:, 1, :], ALU.mult))
                src = 6 if first else 1
                link(g.tensor_tensor(lnw[:, 7, :], mean, lnw[:, src, :], ALU.mult))
                link(g.tensor_tensor(lnw[:, 4, :], zeros[:], lnw[:, 7, :], ALU.subtract))
                return done[0]

            with pool.Fori(0, B) as b:
                n = rstd(b * PA, s["a_mv"], b * BLK + BLK, True)
                n += rstd(b * PA + n, s["a_mv5"], b * BLK + BLK, False)
                n += rstd(b * PA + n, s["a_mv9"], b * BLK + BLK, False)
                assert n == PA
                pool.wait_ge(s["split_hi"], b * 3 + 3)
                for m in range(3):
                    g.tensor_tensor(w_lo[m][:, bass.ds(b * S, S)], raw[m][:],
                                    w_hi[m][:, bass.ds(b * S, S)].bitcast(F32), ALU.subtract).then_inc(s["split_lo"], 1)


            def rstd4(f, n0):
                g.tensor_tensor(lnw[:, 0, 0:SUB], mv[:, 0:SUB, 1], eps[:, 0:SUB], ALU.add).then_inc(f["rs"], 1)
                pool.wait_ge(f["rs"], n0 + 1)
                g.tensor_tensor(lnw[:, 1, 0:SUB], lnw[:, 0, 0:SUB], half[:, 0:SUB], ALU.pow).then_inc(f["rs"], 1)

            def ffn(f):
                with pool.Fori(0, TILES) as t:
                    pool.wait_ge(f["mv"], t * SUB + SUB)
                    rstd4(f, t * 2)

            pool.wait_ge(s["split_lo"], 3 * B + 1)
            ffn(FS[0])

            def attention():
                ffn(G)
                pool.wait_ge(G["stored"], 16 * 3 * TILES)
                g.memset(vp[:], 0.0).then_inc(T["init"], 1)
                pool.wait_ge(T["init"], 1)
                g.memset(vp[:, :, :, :, HD:HD + 1], 1.0).then_inc(T["init"], 1)
                pool.wait_ge(T["init"], 2)

            attention()
            ffn(FS[1])

        @block.tensor
        def _(pe):
            def transpose4(dst, src):
                for j in range(SUB):
                    mm = pe.transpose(dst[:, j * P:(j + 1) * P], src[:, j * P:(j + 1) * P], ident[:])
                return mm

            pe.wait_ge(s["pool_setup"], 8)
            pe.wait_ge(s["small_loaded"], 16 * N_SMALL)
            for t in range(T_COUNT):
                src = convx[:, t - T_CONV, :] if T_CONV <= t < T_IN else wraw[:, (t if t < T_CONV else t - 4) * P:(t + 1 if t < T_CONV else t - 3) * P]
                mm = pe.transpose(bank(t // 4)[:, (t % 4) * P:(t % 4 + 1) * P], src, ident[:])
            mm.then_inc(s["wraw_T"], 1)
            pe.transpose(bank(5)[:, 0:PAR_ROWS], prow[:, :], ident[0:PAR_ROWS, 0:PAR_ROWS]).then_inc(s["par_T"], 1)
            pe.wait_ge(s["wt_ready"], 8)
            pe.wait_ge(s["par_ready"], 1)

            with pe.Fori(0, B) as b:
                pe.wait_ge(s["a_tokd"], b * BLK + BLK)
                pe.wait_ge(s["a_toka"], b * BLK + BLK)
                for u in range(2):
                    transpose4(bank(u), a0_tok[:, u * NT:(u + 1) * NT])
                    transpose4(bank(2 + u), hc_tok[:, u * NT:(u + 1) * NT]).then_inc(s["a_T"], 1)
                for u in range(2):
                    pe.wait_ge(s["a_hT"], b * 2 + u + 1)
                    for k in range(TAPS):
                        mm = pe.matmul(bank(4 + u), W(T_CONV + k), hT[:, u * NT + k:u * NT + k + NT],
                                       start=(k == 0), stop=(k == TAPS - 1))
                    mm.then_inc(s["a_conv"], 1)
                for u in range(2):
                    pe.wait_ge(s["a_a1"], b * 2 + u + 1)
                    transpose4(bank(u), a0T[:, u * NT:(u + 1) * NT]).then_inc(s["a_T5"], 1)
                for u in range(2):
                    pe.wait_ge(s["a_n5d" if u else "a_n5"], b * 4 + 4)
                    transpose4(bank(2 + u), a0_tok[:, u * NT:(u + 1) * NT]).then_inc(s["a_T7"], 1)
                for u in range(2):
                    pe.wait_ge(s["a_h2"], b * 2 + u + 1)
                    for m, bk in ((T_Q, 4 + u), (T_K, 6 + u), (T_V, 0 + u)):
                        pe.matmul(bank(bk), W(m), h2T[:, u * NT:(u + 1) * NT], start=True,
                                  stop=True).then_inc(s["a_qkv"], 1)
                for u in range(2):
                    pe.wait_ge(s["a_a2"], b * 2 + u + 1)
                    transpose4(bank(2 + u), a0T[:, u * NT:(u + 1) * NT]).then_inc(s["a_T9"], 1)
                for u in range(2):
                    pe.wait_ge(s["a_n9d" if u else "a_n9"], b * 4 + 4)
                    transpose4(bank(4 + u), a0_tok[:, u * NT:(u + 1) * NT]).then_inc(s["a_T10"], 1)
                pe.wait_ge(s["a_h3"], b * 2 + 2)
                for n in range(9):
                    if n < 8:
                        u, c = divmod(n, 4)
                        if n >= 2:
                            pe.wait_ge(s["a_gel"], b * 8 + n - 1)
                        pe.matmul(bank(6 + n % 2), W(T_BOOM + c), h2T[:, u * NT:(u + 1) * NT], start=True,
                                  stop=True).then_inc(s["a_up"], 1)
                    if n >= 1:
                        u, c = divmod(n - 1, 4)
                        pe.wait_ge(s["a_gel"], b * 8 + n)
                        pe.matmul(bank(u), W(T_DOWN + c), gel[:, (n - 1) % 2, :], start=(c == 0),
                                  stop=(c == 3)).then_inc(s["a_dn"], 1)
                for u in range(2):
                    pe.wait_ge(s["a_y"], b * 2 + u + 1)
                    transpose4(bank(2 + u), a0T[:, u * NT:(u + 1) * NT]).then_inc(s["a_T13"], 1)
                pe.wait_ge(s["a_x1"], b * 2 + 2)


            def ffn(f):
                def gate_up(h, c):
                    w = slice(c * P, (c + 1) * P)
                    for m, sig in ((0, "gate"), (1, "up")):
                        dst = bank(2 * m + c % 2)
                        pe.matmul(dst, w_hi[m][:, w], xn_hi[:, h, :], start=True, stop=False)
                        pe.matmul(dst, w_hi[m][:, w], xn_lo[:, h, :], start=False, stop=False)
                        pe.matmul(dst, w_lo[m][:, w], xn_hi[:, h, :], start=False, stop=True).then_inc(f[sig], 1)

                def down(h, c):
                    w = slice(c * P, (c + 1) * P)
                    dst = bank(4 + h)
                    pe.matmul(dst, w_hi[2][:, w], h_hi[:, c % 2, :], start=(c == 0), stop=False)
                    pe.matmul(dst, w_hi[2][:, w], h_lo[:, c % 2, :], start=False, stop=False)
                    mm = pe.matmul(dst, w_lo[2][:, w], h_hi[:, c % 2, :], start=False, stop=(c == CH - 1))
                    mm.then_inc(f["y_done"] if c == CH - 1 else f["dn"], 1)

                def pair(i, last):
                    for h in range(2):
                        t = i * 2 + h
                        end = last and h == 1
                        for c in range(CH):
                            k = i * (2 * CH) + (h * CH + c)
                            if not (end and c >= CH - 2):
                                if c == CH - 2:
                                    pe.wait_ge(f["xlo"], t + 2)
                                pe.wait_ge(f["silu"], k + 1)
                                pe.wait_ge(f["prod"], k + 1)
                                gate_up(h if c + 2 < CH else 1 - h, (c + 2) % CH)
                            pe.wait_ge(f["hhi"], k + 1)
                            pe.wait_ge(f["hlo"], k + 1)
                            down(h, c)
                            if c == 3:
                                pe.wait_ge(f["y_out"], t + 1)
                                transpose4(bank(7), yS).then_inc(f["yT"], 1)
                            if c == 16 and not end:
                                pe.wait_ge(f["xadd"], t + 1)
                                pe.wait_ge(f["norm"], t * SUB + 2 * SUB)
                                transpose4(bank(7), ntok).then_inc(f["xT"], 1)

                pe.wait_ge(f["norm"], SUB)
                transpose4(bank(7), ntok).then_inc(f["xT"], 1)
                pe.wait_ge(f["xlo"], 1)
                gate_up(0, 0)
                gate_up(0, 1)
                with pe.Fori(0, TILES // 2 - 1) as i:
                    pair(i, False)
                pair(TILES // 2 - 1, True)
                pe.wait_ge(f["y_out"], TILES + 1)
                transpose4(bank(7), yS).then_inc(f["yT"], 1)
                pe.wait_ge(f["xadd"], TILES + 1)

            def project():
                def tile(h, t, last):
                    pe.wait_ge(G["xlo"], t + 1)
                    for m in range(2):
                        w = slice(m * D, (m + 1) * D)
                        dst = bank(2 * m + h)
                        pe.matmul(dst, win_hi[:, w], xn_hi[:, h, :], start=True, stop=False)
                        pe.matmul(dst, win_hi[:, w], xn_lo[:, h, :], start=False, stop=False)
                        pe.matmul(dst, win_lo[:, w], xn_hi[:, h, :], start=False, stop=True).then_inc(G["qk"], 1)
                    w = slice(2 * D, 3 * D)
                    for j in range(SUB):
                        tok = slice(j * P, (j + 1) * P)
                        dst = bank(4 + h)[:, tok]
                        pe.matmul(dst, xn_hi[:, h, tok], win_hi[:, w], start=True, stop=False)
                        pe.matmul(dst, xn_lo[:, h, tok], win_hi[:, w], start=False, stop=False)
                        mm = pe.matmul(dst, xn_hi[:, h, tok], win_lo[:, w], start=False, stop=True)
                    mm.then_inc(G["v"], 1)
                    if not last:
                        pe.wait_ge(G["norm"], t * SUB + 2 * SUB)
                        transpose4(bank(7), ntok).then_inc(G["xT"], 1)
                        pe.wait_ge(G["third"], t * 2 + 2)
                        pe.wait_ge(G["vcopy"], t + 1)

                pe.wait_ge(G["norm"], SUB)
                transpose4(bank(7), ntok).then_inc(G["xT"], 1)
                with pe.Fori(0, TILES // 2 - 1) as i:
                    tile(0, i * 2, False)
                    tile(1, i * 2 + 1, False)
                tile(0, TILES - 2, False)
                tile(1, TILES - 1, True)

            def attention():
                def take_max(k, n_done, slot):
                    h, i = JOBS[k]
                    r = 2 * (k % 2)
                    keys = (i + 1) * P
                    if not (isinstance(n_done, int) and n_done + k < 2):
                        pe.wait_ge(T["reduced"], n_done + (k - 1))
                    lhs = qs[slot][0:K1, h, i * P:(i + 1) * P]
                    for lo in range(0, keys, NT):
                        w = min(NT, keys - lo)
                        diag = lo + w == keys
                        pe.matmul(ps[:, r + lo // NT, 0:w], lhs, ks[slot][0:K1, h, lo:lo + w],
                                  start=True, stop=not diag)
                    d = i * P % NT
                    pe.matmul(ps[:, r + i * P // NT, d:d + P], identb[:], mask_qk[:], start=False,
                              stop=True).then_inc(T["job"], 1)

                def maxima_T(c, n_red):
                    pe.wait_ge(T["reduced"], n_red)
                    pe.transpose(bank(7)[0:MROWS, 0:P], negm[:, c, :], ident[:]).then_inc(T["mT"], 1)

                def scores(n, slot, st, h):
                    c, j = STEPS[st]
                    k = st * HG + h
                    q0 = max(c * NT, j * P)
                    w = (c + 1) * NT - q0
                    if k >= 2:
                        pe.wait_ge(T["exp"], n * NST + (k - 1))
                    diag = j >= c * SUB
                    mm = pe.matmul(bank(4 + k % 2)[:, 0:w], ks[slot][:, h, j * P:(j + 1) * P],
                                   qs[slot][:, h, q0:q0 + w], start=True, stop=not diag)
                    if diag:
                        mm = pe.matmul(bank(4 + k % 2)[:, 0:P], identb[:], mask_kq[:], start=False, stop=True)
                    mm.then_inc(T["scores"], 1)

                def weigh(n, slot, st):
                    c, j = STEPS[st]
                    q0 = max(c * NT, j * P) - c * NT
                    pe.wait_ge(T["exp"], n * NST + (st * HG + HG))
                    if c == 1 and j == 0:
                        pe.wait_ge(T["o_out"], n * 2 + 1)
                    for h in range(HG):
                        mm = pe.matmul(ps[32 * h:32 * h + 32, 6, q0:NT], vp[:, slot, j, h, :],
                                       pr[:, st % 2, h, 0:NT - q0], start=(j == 0),
                                       stop=(j == SUB * c + SUB - 1))
                    if j == SUB * c + SUB - 1:
                        mm.then_inc(T["pv"], 1)

                def result_T(n, c):
                    pe.wait_ge(T["o_out"], n * 2 + c + 1)
                    transpose4(bank(7), ntok).then_inc(T["oT"], 1)

                def project_out(b):
                    for u in range(2):
                        transpose4(bank(7), ctxt[:, u * SUB:(u + 1) * SUB, :].rearrange("p j d -> p (j d)")
                                   ).then_inc(T["cT"], 1)
                        pe.wait_ge(T["c_out"], b * 2 + u + 1)
                        if u == 1:
                            pe.wait_ge(T["xadd"], b * 2 + 1)
                        for j in range(SUB):
                            mm = pe.matmul(bank(6)[:, j * P:(j + 1) * P], ntok[:, j * P:(j + 1) * P],
                                           wout[:], start=True, stop=True)
                        mm.then_inc(T["proj"], 1)
                    pe.wait_ge(T["xadd"], b * 2 + 2)

                pe.wait_ge(T["loaded0"], LOADS)
                for k in range(len(JOBS)):
                    take_max(k, 0, 0)
                maxima_T(0, MROWS)

                def batch(b, last):
                    for g in range(NG):
                        n = b * NG + g
                        slot = g % 2
                        k = 0
                        pe.wait_ge(T["m_loaded"], n * 32 + 16)
                        pe.wait_ge(T["vp"], n + 1)
                        for st in range(len(STEPS)):
                            if STEPS[st] == (1, 0):
                                pe.wait_ge(T["m_loaded"], n * 32 + 32)
                            n_jobs = 0 if last and g == NG - 1 else JOBS_AFTER[st]
                            for h in range(HG):
                                scores(n, slot, st, h)
                                for _ in range((n_jobs + HG - 1 - h) // HG):
                                    if k == 0:
                                        pe.wait_ge(T[f"loaded{1 - slot}"],
                                                   b * (2 * LOADS) + ((g + 1) // 2 + 1) * LOADS)
                                    take_max(k, n * len(JOBS) + len(JOBS), 1 - slot)
                                    k += 1
                            if st == 0:
                                maxima_T(1, n * len(JOBS) + len(JOBS))
                            if st >= 1:
                                weigh(n, slot, st - 1)
                            if st == 6:
                                pe.wait_ge(T["m_split"], n * 2 + 2)
                                result_T(n, 0)
                            if st == 9 and not (last and g == NG - 1):
                                pe.wait_ge(T["ctx"], n * 2 + 1)
                                maxima_T(0, n * len(JOBS) + (len(JOBS) + MROWS))
                        weigh(n, slot, len(STEPS) - 1)
                        if last and g == NG - 1:
                            pe.wait_ge(T["ctx"], n * 2 + 1)
                        else:
                            pe.wait_ge(T["m_split"], n * 2 + 3)
                        result_T(n, 1)
                        pe.wait_ge(T["ctx"], n * 2 + 2)
                    project_out(b)

                with pe.Fori(0, B - 1) as b:
                    batch(b, False)
                batch(B - 1, True)

            ffn(FS[0])
            project()
            pe.wait_ge(G["stored"], 16 * 3 * TILES)
            attention()
            ffn(FS[1])

        @block.scalar
        def _(act):
            a = nc.scalar
            load_small(act)
            act.wait_ge(s["wraw_T"], 1)
            for k in range(4):
                w = min(T_IN - 4 * k, 4) * P
                a.copy(wt[:, k * NT:k * NT + w], bank(k)[:, 0:w]).then_inc(s["wt_ready"], 1)
            for dst, src in w_in_blocks(win_hi):
                a.copy(dst, src).then_inc(s["wt_ready"], 1)
            a.copy(wout[:], bank(4)[:, 2 * P:3 * P]).then_inc(s["wt_ready"], 1)
            act.wait_ge(s["par_ready"], 1)

            def norm_blocks(src_banks, wait_sem, wait_n, mv_wait, scale_row, dst, done, which):
                for j in which:
                    a.activation(dst[:, j * P:(j + 1) * P], src_banks(j), ACT.Identity,
                                 bias=lnw[:, 4, j:j + 1], scale=lnw[:, scale_row, j:j + 1]).then_inc(done, 1)

            with act.Fori(0, B) as b:
                act.wait_ge(s["a_pool"], b * PA + 9)
                for j in range(BLK):
                    a.activation(hc_tok[:, j * P:(j + 1) * P], xs(b * BLK + j), ACT.Identity,
                                 bias=lnw[:, 4, j:j + 1], scale=lnw[:, 6, j:j + 1]).then_inc(s["a_toka"], 1)
                for u in range(2):
                    act.wait_ge(s["a_T"], b * 2 + u + 1)
                    a.activation(hT[:, TAPS - 1 + u * NT:TAPS - 1 + (u + 1) * NT], bank(2 + u), ACT.Identity,
                                 bias=col(R_CONV_B), scale=col(R_CONV_G)).then_inc(s["a_hT"], 1)
                act.wait_ge(s["raw_loaded"], b * 48 + 48)
                for m in range(3):
                    a.copy(w_hi[m][:, bass.ds(b * S, S)], raw[m][:]).then_inc(s["split_hi"], 1)
                act.wait_ge(s["a_pool"], b * PA + 13)
                for u in range(1):
                    for j in range(SUB):
                        a.activation(a0_tok[:, j * P:(j + 1) * P], bank(u)[:, (j % 4) * P:(j % 4 + 1) * P],
                                     ACT.Identity, bias=lnw[:, 4, j:j + 1],
                                     scale=lnw[:, 1, j:j + 1]).then_inc(s["a_n5"], 1)
                for u in range(2):
                    act.wait_ge(s["a_T7"], b * 2 + u + 1)
                    a.activation(h2T[:, u * NT:(u + 1) * NT], bank(2 + u), ACT.Identity,
                                 bias=col(R_ATTN_B), scale=col(R_ATTN_G)).then_inc(s["a_h2"], 1)
                act.wait_ge(s["a_pool"], b * PA + 17)
                for u in range(1):
                    for j in range(SUB):
                        a.activation(a0_tok[:, j * P:(j + 1) * P], bank(2 + u)[:, (j % 4) * P:(j % 4 + 1) * P],
                                     ACT.Identity, bias=lnw[:, 4, j:j + 1],
                                     scale=lnw[:, 1, j:j + 1]).then_inc(s["a_n9"], 1)
                for u in range(2):
                    act.wait_ge(s["a_T10"], b * 2 + u + 1)
                    a.activation(h2T[:, u * NT:(u + 1) * NT], bank(4 + u), ACT.Identity,
                                 bias=col(R_BOOM_B), scale=col(R_BOOM_G)).then_inc(s["a_h3"], 1)
                for n in range(8):
                    act.wait_ge(s["a_up"], b * 8 + n + 1)
                    if n >= 2:
                        act.wait_ge(s["a_dn"], b * 8 + n - 1)
                    a.activation(gel[:, n % 2, :], bank(6 + n % 2), ACT.Gelu,
                                 bias=col(R_BB + n % 4)).then_inc(s["a_gel"], 1)


            def ffn(f):
                def silu(c):
                    a.activation(sg[:, c % 2, :], bank(c % 2), ACT.Silu).then_inc(f["silu"], 1)

                def split_input(h):
                    a.copy(xn_hi[:, h, :], bank(7)).then_inc(f["xhi"], 1)

                def pair(i, last):
                    for h in range(2):
                        t = i * 2 + h
                        end = last and h == 1
                        for c in range(CH):
                            k = i * (2 * CH) + (h * CH + c)
                            if not (end and c == CH - 1):
                                act.wait_ge(f["gate"], k + 2)
                                silu((c + 1) % CH)
                            else:
                                act.wait_ge(f["dn"], (TILES * (CH - 1)) - 1)
                            act.wait_ge(f["prod"], k + 1)
                            a.copy(h_hi[:, c % 2, :], hid[:, c % 4, :]).then_inc(f["hhi"], 1)
                            if c == 1:
                                act.wait_ge(f["y_done"], t + 1)
                                a.copy(yS[:], bank(5 - h)).then_inc(f["y_out"], 1)
                            if c == 18 and not end:
                                act.wait_ge(f["xT"], t + 2)
                                split_input(1 - h)

                act.wait_ge(f["xT"], 1)
                split_input(0)
                act.wait_ge(f["gate"], 1)
                silu(0)
                with act.Fori(0, TILES // 2 - 1) as i:
                    pair(i, False)
                pair(TILES // 2 - 1, True)
                act.wait_ge(f["y_done"], TILES + 1)
                a.copy(yS[:], bank(5)).then_inc(f["y_out"], 1)

            def project():
                def tile(h, t, last):
                    for m in range(2):
                        act.wait_ge(G["qk"], t * 2 + m + 1)
                        a.activation(part(t, m, 0), bank(2 * m + h), ACT.Copy,
                                     scale=SCALE if m == 0 else 1.0).then_inc(G["first"], 1)
                    act.wait_ge(G["v"], t + 1)
                    a.copy(v_out[:, bass.ds(t, 1), :].rearrange("p a n -> p (a n)"), bank(4 + h)).then_inc(G["vcopy"], 1)
                    if not last:
                        act.wait_ge(G["xT"], t + 2)
                        a.copy(xn_hi[:, 1 - h, :], bank(7)).then_inc(G["xhi"], 1)
                    for m in range(2):
                        act.wait_ge(G["rest"], t * 2 + m + 1)
                        a.copy(part(t, m, 1), qkr[:, h, m, :]).then_inc(G["second"], 1)

                act.wait_ge(G["xT"], 1)
                a.copy(xn_hi[:, 0, :], bank(7)).then_inc(G["xhi"], 1)
                with act.Fori(0, TILES // 2 - 1) as i:
                    tile(0, i * 2, False)
                    tile(1, i * 2 + 1, False)
                tile(0, TILES - 2, False)
                tile(1, TILES - 1, True)

            def attention():
                def place_values(b, g):
                    act.wait_ge(T["v_loaded"], b * 16 + 16)
                    a.copy(vp[:, g % 2, :, :, 0:HD],
                           v_tok[:, :, g * HG * HD:(g + 1) * HG * HD].rearrange("p j (h d) -> p j h d", h=HG)
                           ).then_inc(T["vp"], 1)

                def result_out(n, c):
                    act.wait_ge(T["pv"], n * 2 + c + 1)
                    if c == 1:
                        act.wait_ge(T["oT"], n * 2 + 1)
                    a.copy(ntok[:], bank(6)).then_inc(T["o_out"], 1)

                def batch(b, last):
                    for g in range(NG):
                        n = b * NG + g
                        for st, (c, j) in enumerate(STEPS):
                            w = (c + 1) * NT - max(c * NT, j * P)
                            for h in range(HG):
                                k = st * HG + h
                                act.wait_ge(T["scores"], n * NST + (k + 1))
                                a.activation(pr[:, st % 2, h, 0:w], bank(4 + k % 2)[:, 0:w],
                                             ACT.Exp).then_inc(T["exp"], 1)
                            if st == SUB:
                                result_out(n, 0)
                                if not (last and g == NG - 1):
                                    place_values(b + (g + 1) // NG, (g + 1) % NG)
                        result_out(n, 1)
                    for u in range(2):
                        act.wait_ge(T["cT"], b * 2 + u + 1)
                        a.copy(ntok[:], bank(7)).then_inc(T["c_out"], 1)

                act.wait_ge(T["init"], 2)
                place_values(0, 0)
                with act.Fori(0, B - 1) as b:
                    batch(b, False)
                batch(B - 1, True)

            ffn(FS[0])
            project()
            attention()
            ffn(FS[1])

        @block.vector
        def _(dve):
            v = nc.vector
            v.memset(zcol[:], 0.0).then_inc(s["zeros"], 1)
            dve.wait_ge(s["zeros"], 1)
            dve.wait_ge(s["pool_setup"], 8)
            v.tensor_copy(cq[:], rinv[:].bitcast(I32)).then_inc(s["rinv_ready"], 1)
            dve.wait_ge(s["rinv_ready"], 1)
            v.reciprocal(rinv[:], cq[:]).then_inc(s["rinv_ready"], 1)
            dve.wait_ge(s["par_T"], 1)
            v.tensor_copy(par[:], bank(5)[:, 0:PAR_ROWS]).then_inc(s["par_ready"], 1)
            dve.wait_ge(s["wt_ready"], 8)
            for (dst, src), (hi, _) in zip(w_in_blocks(win_lo), w_in_blocks(win_hi)):
                v.tensor_tensor(dst, src, hi.bitcast(F32), ALU.subtract).then_inc(s["wt_ready"], 1)
            dve.wait_ge(s["x_loaded"], 16 * B)
            dve.wait_ge(s["par_ready"], 1)

            def stats(b, src, st_sem, mv_sem, waits):
                for j in range(BLK):
                    if j in waits:
                        dve.wait_ge(*waits[j])
                    v.bn_stats(st[:, j, :], src(j)).then_inc(st_sem, 1)
                dve.wait_ge(st_sem, b * BLK + BLK)
                v.memset(fence[:], 0.0)
                for j in range(BLK):
                    v.bn_aggr(mv[:, j, :], st[:, j, :]).then_inc(mv_sem, 1)

            with dve.Fori(0, B) as b:
                stats(b, lambda j: xs(b * BLK + j), s["a_st"], s["a_mv"], {})
                dve.wait_ge(s["a_pool"], b * PA + 9)
                for j in range(BLK):
                    v.tensor_scalar(a0_tok[:, j * P:(j + 1) * P], xs(b * BLK + j), mv[:, j, 0:1],
                                    lnw[:, 1, j:j + 1], ALU.subtract, ALU.mult).then_inc(s["a_tokd"], 1)
                for u in range(2):
                    dve.wait_ge(s["a_T"], b * 2 + u + 1)
                    v.tensor_copy(a0T[:, u * NT:(u + 1) * NT], bank(u)).then_inc(s["a_copyD"], 1)
                for u in range(2):
                    dve.wait_ge(s["a_conv"], b * 2 + u + 1)
                    dve.wait_ge(s["a_copyD"], b * 2 + u + 1)
                    v.scalar_tensor_tensor(a0T[:, u * NT:(u + 1) * NT], bank(4 + u), col(R_CONV_BIAS),
                                           a0T[:, u * NT:(u + 1) * NT], ALU.add, ALU.add).then_inc(s["a_a1"], 1)
                stats(b, lambda j: bank(j // 4)[:, (j % 4) * P:(j % 4 + 1) * P], s["a_st5"], s["a_mv5"],
                      {0: (s["a_T5"], b * 2 + 1), 4: (s["a_T5"], b * 2 + 2)})
                dve.wait_ge(s["a_pool"], b * PA + 13)
                for u in (1,):
                    for j in range(SUB, BLK):
                        v.tensor_scalar(a0_tok[:, j * P:(j + 1) * P], bank(u)[:, (j % 4) * P:(j % 4 + 1) * P],
                                        mv[:, j, 0:1], lnw[:, 1, j:j + 1], ALU.subtract, ALU.mult).then_inc(s["a_n5d"], 1)
                for u in range(2):
                    sl = slice(u * NT, (u + 1) * NT)
                    n0 = b * 12 + 6 * u
                    dve.wait_ge(s["a_qkv"], b * 6 + 3 * u + 1)
                    v.tensor_tensor_scan(cq[:, sl], bank(4 + u), col(R_BQ).to_broadcast([P, NT]),
                                         0.0 if u == 0 else cq[:, NT - 1:NT], ALU.add, ALU.add).then_inc(s["a_d8"], 1)
                    dve.wait_ge(s["a_d8"], n0 + 1)
                    v.tensor_tensor(pq[:, sl], cq[:, sl], rinv[:, sl], ALU.mult).then_inc(s["a_d8"], 1)
                    dve.wait_ge(s["a_d8"], n0 + 2)
                    dve.wait_ge(s["a_qkv"], b * 6 + 3 * u + 3)
                    v.scalar_tensor_tensor(pq[:, sl], bank(6 + u), col(R_BK), pq[:, sl], ALU.add,
                                           ALU.mult).then_inc(s["a_d8"], 1)
                    dve.wait_ge(s["a_d8"], n0 + 3)
                    v.tensor_tensor_scan(hc_tok[:, sl], pq[:, sl], zcol[:].to_broadcast([P, NT]),
                                         0.0 if u == 0 else hc_tok[:, NT - 1:NT], ALU.add, ALU.add).then_inc(s["a_d8"], 1)
                    dve.wait_ge(s["a_d8"], n0 + 4)
                    v.tensor_tensor(pq[:, sl], hc_tok[:, sl], rinv[:, sl], ALU.mult).then_inc(s["a_d8"], 1)
                    dve.wait_ge(s["a_d8"], n0 + 5)
                    v.scalar_tensor_tensor(pq[:, sl], bank(0 + u), col(R_BV), pq[:, sl], ALU.add,
                                           ALU.mult).then_inc(s["a_d8"], 1)
                    dve.wait_ge(s["a_d8"], n0 + 6)
                    v.tensor_tensor(a0T[:, sl], a0T[:, sl], pq[:, sl], ALU.add).then_inc(s["a_a2"], 1)
                stats(b, lambda j: bank(2 + j // 4)[:, (j % 4) * P:(j % 4 + 1) * P], s["a_st9"], s["a_mv9"],
                      {0: (s["a_T9"], b * 2 + 1), 4: (s["a_T9"], b * 2 + 2)})
                dve.wait_ge(s["a_pool"], b * PA + 17)
                for u in (1,):
                    for j in range(SUB, BLK):
                        v.tensor_scalar(a0_tok[:, j * P:(j + 1) * P], bank(2 + u)[:, (j % 4) * P:(j % 4 + 1) * P],
                                        mv[:, j, 0:1], lnw[:, 1, j:j + 1], ALU.subtract, ALU.mult).then_inc(s["a_n9d"], 1)
                for u in range(2):
                    sl = slice(u * NT, (u + 1) * NT)
                    dve.wait_ge(s["a_dn"], b * 8 + 4 * u + 4)
                    dve.wait_ge(s["a_a2"], b * 2 + u + 1)
                    v.scalar_tensor_tensor(a0T[:, sl], bank(u), col(R_BU), a0T[:, sl], ALU.add,
                                           ALU.add).then_inc(s["a_y"], 1)
                for u in range(2):
                    dve.wait_ge(s["a_T13"], b * 2 + u + 1)
                    v.tensor_tensor(xs(b * BLK + 4 * u, SUB), xs(b * BLK + 4 * u, SUB), bank(2 + u),
                                    ALU.add).then_inc(s["a_x1"], 1)

            def norm_steps(f):
                def stats4(t, n0):
                    for j in range(SUB):
                        v.bn_stats(st[:, j, :], xs(t * SUB + j)).then_inc(f["st"], 1)
                    dve.wait_ge(f["st"], n0 + SUB)
                    v.memset(fence[:], 0.0)
                    for j in range(SUB):
                        v.bn_aggr(mv[:, j, :], st[:, j, :]).then_inc(f["mv"], 1)

                def norm4(t):
                    for j in range(SUB):
                        v.tensor_scalar(ntok[:, j * P:(j + 1) * P], xs(t * SUB + j), mv[:, j, 0:1],
                                        lnw[:, 1, j:j + 1], ALU.subtract, ALU.mult).then_inc(f["norm"], 1)

                return stats4, norm4

            def ffn(f):
                stats4, norm4 = norm_steps(f)

                def product(c):
                    v.tensor_tensor(hid[:, c % 4, :], sg[:, c % 2, :], bank(2 + c % 2), ALU.mult).then_inc(f["prod"], 1)

                def split_input(h):
                    v.tensor_tensor(xn_lo[:, h, :], bank(7), xn_hi[:, h, :].bitcast(F32),
                                    ALU.subtract).then_inc(f["xlo"], 1)

                def pair(i, last):
                    for h in range(2):
                        t = i * 2 + h
                        end = last and h == 1
                        for c in range(CH):
                            k = i * (2 * CH) + (h * CH + c)
                            if not (end and c == CH - 1):
                                dve.wait_ge(f["up"], k + 2)
                                dve.wait_ge(f["silu"], k + 2)
                                product((c + 1) % CH)
                            dve.wait_ge(f["hhi"], k + 1)
                            v.tensor_tensor(h_lo[:, c % 2, :], hid[:, c % 4, :], h_hi[:, c % 2, :].bitcast(F32),
                                            ALU.subtract).then_inc(f["hlo"], 1)
                            if c == 5:
                                dve.wait_ge(f["yT"], t + 1)
                                v.tensor_tensor(xs(t * SUB - SUB, SUB), xs(t * SUB - SUB, SUB), bank(7),
                                                ALU.add).then_inc(f["xadd"], 1)
                            if end:
                                continue
                            if c == 7:
                                stats4(t + 1, t * SUB + SUB)
                            if c == 12:
                                dve.wait_ge(f["rs"], t * 2 + 4)
                                norm4(t + 1)
                            if c == 20:
                                dve.wait_ge(f["xhi"], t + 2)
                                split_input(1 - h)

                v.memset(x[:, 0:NT], 0.0)
                v.memset(bank(5), 0.0).then_inc(f["y_done"], 1)
                stats4(0, 0)
                dve.wait_ge(f["rs"], 2)
                norm4(0)
                dve.wait_ge(f["xhi"], 1)
                split_input(0)
                dve.wait_ge(f["up"], 1)
                dve.wait_ge(f["silu"], 1)
                product(0)
                with dve.Fori(0, TILES // 2 - 1) as i:
                    pair(i, False)
                pair(TILES // 2 - 1, True)
                dve.wait_ge(f["yT"], TILES + 1)
                v.tensor_tensor(xs(TILES * SUB - SUB, SUB), xs(TILES * SUB - SUB, SUB), bank(7),
                                ALU.add).then_inc(f["xadd"], 1)

            def project():
                stats4, norm4 = norm_steps(G)

                def split_input(t, h):
                    dve.wait_ge(G["xhi"], t + 1)
                    v.tensor_tensor(xn_lo[:, h, :], bank(7), xn_hi[:, h, :].bitcast(F32),
                                    ALU.subtract).then_inc(G["xlo"], 1)

                def tile(h, t, last):
                    if not last:
                        stats4(t + 1, t * SUB + SUB)
                    for m in range(2):
                        dve.wait_ge(G["first"], t * 2 + m + 1)
                        v.scalar_tensor_tensor(qkr[:, h, m, :], bank(2 * m + h), SCALE if m == 0 else 1.0,
                                               part(t, m, 0), ALU.mult, ALU.subtract).then_inc(G["rest"], 1)
                    if not last:
                        dve.wait_ge(G["rs"], t * 2 + 4)
                        norm4(t + 1)
                        split_input(t + 1, 1 - h)
                    for m in range(2):
                        dve.wait_ge(G["second"], t * 2 + m + 1)
                        v.tensor_tensor(part(t, m, 2), qkr[:, h, m, :], part(t, m, 1),
                                        ALU.subtract).then_inc(G["third"], 1)

                stats4(0, 0)
                dve.wait_ge(G["rs"], 2)
                norm4(0)
                split_input(0, 0)
                with dve.Fori(0, TILES // 2 - 1) as i:
                    tile(0, i * 2, False)
                    tile(1, i * 2 + 1, False)
                tile(0, TILES - 2, False)
                tile(1, TILES - 1, True)

            def attention():
                def reduce_job(k, n_done):
                    h, i = JOBS[k]
                    r = 2 * (k % 2)
                    c, col_ = divmod(k, MROWS)
                    dve.wait_ge(T["job"], n_done + (k + 1))
                    v.tensor_reduce(negm[:, c, col_:col_ + 1],
                                    ps[:, r:r + 2, :].rearrange("p a n -> p (a n)")[:, 0:(i + 1) * P],
                                    AX.X, ALU.max, negate=True).then_inc(T["reduced"], 1)

                def split_max(e, c):
                    src = bank(7)[0:MROWS, 0:P]
                    dve.wait_ge(T["mT"], e + 1)
                    v.tensor_copy(mpart[:, 0, :], src).then_inc(T["m_parts"], 1)
                    dve.wait_ge(T["m_parts"], e * 3 + 1)
                    v.tensor_tensor(mres[:, 0, :], src, mpart[:, 0, :], ALU.subtract).then_inc(T["m_split"], 1)
                    dve.wait_ge(T["m_split"], e + 1)
                    v.tensor_copy(mpart[:, 1, :], mres[:, 0, :]).then_inc(T["m_parts"], 1)
                    dve.wait_ge(T["m_parts"], e * 3 + 2)
                    v.tensor_tensor(mpart[:, 2, :], mres[:, 0, :], mpart[:, 1, :],
                                    ALU.subtract).then_inc(T["m_parts"], 1)

                def normalise(n, g, c):
                    src = bank(7).rearrange("p (t h w) -> p t h w", t=SUB, h=HG)
                    dve.wait_ge(T["oT"], n * 2 + c + 1)
                    v.reciprocal(rl[:], src[:, :, :, HD]).then_inc(T["onorm"], 1)
                    dve.wait_ge(T["onorm"], n * 2 + c + 1)
                    v.tensor_tensor(
                        ctxt[:, c * SUB:(c + 1) * SUB, g * HG * HD:(g + 1) * HG * HD].rearrange(
                            "p t (h d) -> p t h d", h=HG),
                        src[:, :, :, 0:HD], rl[:].unsqueeze(3).to_broadcast([P, SUB, HG, HD]),
                        ALU.mult).then_inc(T["ctx"], 1)

                for k in range(len(JOBS)):
                    reduce_job(k, 0)
                split_max(0, 0)

                def batch(b, last):
                    for g in range(NG):
                        n = b * NG + g
                        more = not (last and g == NG - 1)
                        k = 0
                        dve.wait_ge(T["m_stored"], n * 32 + 16)
                        split_max(n * 2 + 1, 1)
                        for st in range(len(STEPS)):
                            for _ in range(JOBS_AFTER[st] if more else 0):
                                reduce_job(k, n * len(JOBS) + len(JOBS))
                                k += 1
                            if st == 6:
                                normalise(n, g, 0)
                            if st == 9 and more:
                                dve.wait_ge(T["m_stored"], n * 32 + 32)
                                split_max(n * 2 + 2, 0)
                        normalise(n, g, 1)
                    for u in range(2):
                        dve.wait_ge(T["proj"], b * 2 + u + 1)
                        v.tensor_tensor(xs(b * BLK + u * SUB, SUB), xs(b * BLK + u * SUB, SUB), bank(6),
                                        ALU.add).then_inc(T["xadd"], 1)

                with dve.Fori(0, B - 1) as b:
                    batch(b, False)
                batch(B - 1, True)

            dve.wait_ge(s["a_x1"], TILES)
            ffn(FS[0])
            project()
            attention()
            ffn(FS[1])


LOADS = 16 * (PARTS + PARTS * PARTS + 2)
PA = 9 + 4 + 4


NAMES = {"hidden": "attn_a_hidden_states", "conv_w": "attn_a_conv_w", "conv_b": "attn_a_conv_b",
         "ln_conv_g": "attn_a_ln_conv_g", "ln_conv_b": "attn_a_ln_conv_b",
         "ln_attn_g": "attn_a_ln_attn_g", "ln_attn_b": "attn_a_ln_attn_b",
         "ln_boom_g": "attn_a_ln_boom_g", "ln_boom_b": "attn_a_ln_boom_b",
         "Wq": "attn_a_Wq", "Wk": "attn_a_Wk", "Wv": "attn_a_Wv", "bq": "attn_a_bq",
         "bk": "attn_a_bk", "bv": "attn_a_bv", "Wb": "attn_a_Wb", "bb": "attn_a_bb",
         "Wu": "attn_a_Wu", "bu": "attn_a_bu", "w_in": "attn_b_w_in", "w_out": "attn_b_w_out",
         "Wg": "ffn_Wg", "Wu8": "ffn_Wu", "Wd": "ffn_Wd"}


def bf16_parts(a, n):
    parts, rest = [], np.asarray(a, np.float64)
    for _ in range(n):
        p = rest.astype(BF16_NP)
        parts.append(p)
        rest = rest - p.astype(np.float64)
    return parts


def alibi_rows():
    slope = (2.0 ** (-8.0 / HEADS * (np.arange(HEADS, dtype=np.float32) + 1.0))).astype(np.float32)
    pos = np.arange(S)
    cut = [(pos // P * P).astype(BF16_NP), (pos % P).astype(BF16_NP)]
    k_rows = np.ones((AL_ROWS + PARTS, HEADS, S), BF16_NP)
    q_rows = np.zeros((AL_ROWS, HEADS, S), BF16_NP)
    r = 0
    for c in cut:
        for p in bf16_parts(slope, PARTS):
            k_rows[r], q_rows[r] = c[None, :], p[:, None]
            k_rows[r + 1], q_rows[r + 1] = -p[:, None], c[None, :]
            r += 2
    return k_rows, q_rows


def kernel(**inputs):
    import concourse.bacc as bacc
    from concourse.bass_utils import run_bass_kernel_spmd

    nc = bacc.Bacc("TRN2", target_bir_lowering=False, num_devices=1)
    arrays, aps = {}, {}
    for short, name in NAMES.items():
        arrays[f"in_{short}"] = np.ascontiguousarray(inputs["L0_" + name])
    arrays["in_al_k"], arrays["in_al_q"] = alibi_rows()
    for name, a in arrays.items():
        aps[name[3:]] = nc.dram_tensor(name, a.shape, mybir.dt.from_np(a.dtype), kind="ExternalInput").ap()
    aps["out"] = nc.dram_tensor("out_0", (B, S, D), F32, kind="ExternalOutput").ap()
    build(nc, aps)
    r = run_bass_kernel_spmd(nc, [arrays], core_ids=[0])
    return r.results[0]["out_0"]
```

```python
from contextlib import ExitStack

import concourse.bass as bass
import numpy as np
from concourse import mybir

F32 = mybir.dt.float32
F32R = mybir.dt.float32r
BF16 = mybir.dt.bfloat16
I32 = mybir.dt.int32
BF16_NP = mybir.dt.np(BF16)
ALU = mybir.AluOpType
ACT = mybir.ActivationFunctionType
AX = mybir.AxisListType

P = 128
D = 128
B, S = 4, 1024
TOK = B * S
NT = 512
TILES = TOK // NT
SUB = NT // P
BLK = S // P
EPS = 1e-5
TAPS, GROUPS = 4, 4
GW = D // GROUPS
EXPERTS, FFN = 8, 512
CH = EXPERTS * FFN // P
WCOLS = EXPERTS * FFN
HEADS, HD = 16, 8
HG = 4
NG = HEADS // HG
UNITS = B * NG
PARTS = 3
QK_ROWS = PARTS * PARTS * HD
AL_ROWS = 12
K1 = QK_ROWS + AL_ROWS
K2 = K1 + PARTS
MROWS = HG * SUB
SCALE = float(np.float32(1.0) / np.sqrt(np.float32(HD)))
STEPS = [(c, j) for c in range(2) for j in range(SUB * c + SUB)]
NST = len(STEPS) * HG
JOBS = [(h, i) for c in range(2) for h in range(HG) for i in range(SUB * c, SUB * c + SUB)]
JOBS_AFTER = [4, 4, 4, 4, 3, 3, 2, 2, 2, 2, 2, 0]
HEADS_FIRST = HG // 2
NEG = -1e30

(R_CONV_G, R_CONV_B, R_CONV_BIAS, R_ATTN_G, R_ATTN_B, R_BQ, R_BK, R_BV, R_BOOM_G, R_BOOM_B, R_BB,
 R_BU) = (0, 1, 2, 3, 4, 5, 6, 7, 8, 9, 10, 14)
PAR_ROWS = 15
T_Q, T_K, T_V, T_BOOM, T_DOWN, T_CONV, T_IN, T_OUT = 0, 1, 2, 3, 7, 11, 15, 18
T_COUNT = 19


def build(nc, ap):
    x_in, out = ap["hidden"], ap["out"]
    with ExitStack() as ctx:
        def sb(name, shape, dt=F32, stack=ctx):
            return stack.enter_context(nc.sbuf_tensor(name, shape, dt))

        def sem(name):
            return ctx.enter_context(nc.semaphore(name))

        x = sb("x", [P, (SUB + TOK // P) * P])
        w_hi = [sb(f"w_hi{m}", [P, WCOLS], F32R) for m in range(3)]
        w_lo = [sb(f"w_lo{m}", [P, WCOLS], F32R) for m in range(3)]
        xn_hi = sb("xn_hi", [P, 2, NT], F32R)
        xn_lo = sb("xn_lo", [P, 2, NT], F32R)
        ident = sb("ident", [P, P])
        identb = sb("identb", [P, P], BF16)
        mask_qk = sb("mask_qk", [P, P], BF16)
        mask_kq = sb("mask_kq", [P, P], BF16)
        par = sb("par", [P, PAR_ROWS])
        win_hi = sb("win_hi", [P, 3 * D], F32R)
        win_lo = sb("win_lo", [P, 3 * D], F32R)
        wout = sb("wout", [P, D])
        half = sb("half", [P, BLK])
        eps = sb("eps", [P, BLK])
        zeros = sb("zeros", [P, BLK])
        zcol = sb("zcol", [P, 1])
        fence = sb("fence", [P, 1])
        st = sb("st", [P, BLK, 6])
        mv = sb("mv", [P, BLK, 2])
        lnw = sb("lnw", [P, 8, BLK])
        ntok = sb("ntok", [P, NT])

        ps = ctx.enter_context(nc.psum_tensor("ps", [P, 8, NT], F32))

        with ExitStack() as pa:
            raw = [sb(f"raw{m}", [P, S], F32, pa) for m in range(3)]
            wt = sb("wt", [P, T_IN * P], F32, pa)
            prow = sb("prow", [PAR_ROWS, P], F32, pa)
            wraw = sb("wraw", [P, 15 * P], F32, pa)
            convraw = sb("convraw", [P, GW * TAPS], F32, pa)
            convx = sb("convx", [P, TAPS, P], F32, pa)
            rinv = sb("rinv", [P, S], F32, pa)
            a0_tok = sb("a0_tok", [P, S], F32, pa)
            hc_tok = sb("hc_tok", [P, S], F32, pa)
            a0T = sb("a0T", [P, S], F32, pa)
            hT = sb("hT", [P, TAPS - 1 + S], F32, pa)
            h2T = sb("h2T", [P, S], F32, pa)
            cq = sb("cq", [P, S], F32, pa)
            pq = sb("pq", [P, S], F32, pa)
            gel = sb("gel", [P, 2, NT], F32, pa)
        with ExitStack() as pf:
            sg = sb("sg", [P, 2, NT], F32, pf)
            hid = sb("hid", [P, 4, NT], F32, pf)
            h_hi = sb("h_hi", [P, 2, NT], F32R, pf)
            h_lo = sb("h_lo", [P, 2, NT], F32R, pf)
            yS = sb("yS", [P, NT], F32, pf)
        with ExitStack() as pt:
            qs = [sb(f"qs{i}", [K2, HG, S], BF16, pt) for i in range(2)]
            ks = [sb(f"ks{i}", [K2, HG, S], BF16, pt) for i in range(2)]
            vp = sb("vp", [P, 2, BLK, HG, 32], F32, pt)
            v_tok = sb("v_tok", [P, BLK, D], F32, pt)
            pr = sb("pr", [P, 2, HG, NT], F32, pt)
            ctxt = sb("ctxt", [P, BLK, D], F32, pt)
            rl = sb("rl", [P, SUB, HG], F32, pt)
            negm = sb("negm", [P, 2, MROWS], F32, pt)
            mpart = sb("mpart", [MROWS, PARTS, P], BF16, pt)
            mres = sb("mres", [MROWS, P], F32, pt)
            ctxT = sb("ctxT", [P, NT], F32, pt)
        with ExitStack() as pp:
            qkp = sb("qkp", [P, TILES, 2, PARTS, NT], BF16, pp)
            qkr = sb("qkr", [P, 2, 2, NT], F32, pp)
            v_out = sb("v_out", [P, TILES, NT], F32, pp)

        qkd = [nc.dram_tensor(n, (PARTS, D, TOK), BF16, kind="Internal").ap() for n in ("qd", "kd")]
        vd = nc.dram_tensor("vd", (TOK, D), F32, kind="Internal").ap()
        md = nc.dram_tensor("md", (2, 2, PARTS, MROWS, P), BF16, kind="Internal").ap()

        names = """x_loaded small_loaded zeros pool_setup conv_loaded
            wraw_T wt_ready par_T par_ready rinv_ready
            raw_loaded split_hi split_lo
            a_st a_mv a_pool a_tokd a_toka a_T a_copyD a_hT a_conv a_a1 a_T5 a_st5 a_mv5 a_n5 a_n5d
            a_T7 a_h2 a_qkv a_d8 a_a2 a_T9 a_st9 a_mv9 a_n9 a_n9d a_T10 a_h3 a_up a_gel a_dn a_y a_T13
            a_x1 stored""".split()
        s = {n: sem(n) for n in names}
        FF_NAMES = "st mv rs norm xT xhi xlo gate up silu prod hhi hlo dn y_done y_out yT xadd".split()
        FS = [{n: sem(f"ff{layer}_{n}") for n in FF_NAMES} for layer in range(2)]
        PREP_NAMES = "st mv rs norm xT xhi xlo qk v first rest second third vcopy stored".split()
        G = {n: sem(f"prep_{n}") for n in PREP_NAMES}
        ATT_NAMES = """init v_loaded loaded00 loaded01 loaded10 loaded11 m_loaded0 m_loaded1 vp scores exp pv o_out oT onorm ctx job reduced mT m_split
            m_parts m_stored cT c_out proj xadd""".split()
        T = {n: sem(f"att_{n}") for n in ATT_NAMES}
        block = ctx.enter_context(nc.Block())

        def bank(n):
            return ps[:, n, :]

        def xs(blk, n=1):
            return x[:, bass.ds(blk * P + NT, n * P)]

        def col(r):
            return par[:, r:r + 1]

        def W(slot, n=1):
            return wt[:, slot * P:(slot + n) * P]

        x_blk = x_in.rearrange("b s d -> (b s) d").rearrange("(n p) d -> p n d", p=P)
        o_blk = out.rearrange("b s d -> (b s) d").rearrange("(n p) d -> p n d", p=P)

        SMALL_ROWS = [("ln_conv_g", R_CONV_G), ("ln_conv_b", R_CONV_B), ("conv_b", R_CONV_BIAS),
                      ("ln_attn_g", R_ATTN_G), ("ln_attn_b", R_ATTN_B), ("bq", R_BQ), ("bk", R_BK),
                      ("bv", R_BV), ("ln_boom_g", R_BOOM_G), ("ln_boom_b", R_BOOM_B), ("bu", R_BU)]
        SMALL_MATS = [("Wq", T_Q), ("Wk", T_K), ("Wv", T_V)]
        N_SMALL = len(SMALL_ROWS) + 1 + len(SMALL_MATS) + 4

        def load_small(q):
            q.dma_start(convraw[:], ap["conv_w"].rearrange("o i k -> o (i k)")).then_inc(s["conv_loaded"], 16)
            for n, r in SMALL_ROWS:
                q.dma_start(prow[r:r + 1, :], ap[n].rearrange("(a d) -> a d", a=1)).then_inc(s["small_loaded"], 16)
            q.dma_start(prow[R_BB:R_BB + 4, :], ap["bb"].rearrange("(a d) -> a d", a=4)).then_inc(s["small_loaded"], 16)
            for n, t in SMALL_MATS:
                q.dma_start(wraw[:, t * P:(t + 1) * P], ap[n]).then_inc(s["small_loaded"], 16)
            q.dma_start(wraw[:, T_BOOM * P:(T_BOOM + 4) * P].rearrange("p (c d) -> p c d", c=4),
                        ap["Wb"].rearrange("(c p) d -> p c d", p=P)).then_inc(s["small_loaded"], 16)
            q.dma_start(wraw[:, T_DOWN * P:(T_DOWN + 4) * P], ap["Wu"]).then_inc(s["small_loaded"], 16)
            q.dma_start(wraw[:, 11 * P:14 * P].rearrange("p (c d) -> p c d", c=3),
                        ap["w_in"].rearrange("(c p) d -> p c d", p=P)).then_inc(s["small_loaded"], 16)
            q.dma_start(wraw[:, 14 * P:15 * P], ap["w_out"]).then_inc(s["small_loaded"], 16)

        ffn_src = [ap["Wg"].rearrange("e d f -> d e f"), ap["Wu8"].rearrange("e d f -> d e f"),
                   ap["Wd"].rearrange("e (m p) d -> p (e m) d", p=P)]

        def store_qkv(sp):
            with sp.Fori(0, TILES) as t:
                sp.wait_ge(G["third"], t * 2 + 2)
                sp.wait_ge(G["second"], t * 2 + 2)
                sp.wait_ge(G["first"], t * 2 + 2)
                for m in range(2):
                    sp.dma_start(qkd[m].rearrange("i f t -> f i t")[:, :, bass.ds(t * NT, NT)],
                                 qkp[:, bass.ds(t, 1), m, :, :].rearrange("p a i t -> p (a i) t")
                                 ).then_inc(G["stored"], 16)
                sp.wait_ge(G["vcopy"], t + 1)
                sp.dma_start(vd.rearrange("(n p) d -> p n d", p=P)[:, bass.ds(t * SUB, SUB), :],
                             v_out[:, bass.ds(t, 1), :].rearrange("p a (n d) -> p (a n) d", d=D)
                             ).then_inc(G["stored"], 16)
            sp.wait_ge(G["stored"], 16 * 3 * TILES)

        def attention_loads(sp):
            def load_half(b, g, c):
                hs, slot = slice(g * HG, (g + 1) * HG), g % 2
                tok, at = bass.ds(b * S + c * NT, NT), slice(c * NT, (c + 1) * NT)
                got = T[f"loaded{slot}{c}"]
                q_rows = qkd[0].rearrange("i (d h) t -> i d h t", h=HEADS)
                k_rows = qkd[1].rearrange("j (d h) t -> (j d) h t", h=HEADS)
                for i in range(PARTS):
                    r = i * PARTS * HD
                    sp.dma_start(ks[slot][r:r + PARTS * HD, :, at], k_rows[:, hs, tok]).then_inc(got, 16)
                    for j in range(PARTS):
                        sp.dma_start(qs[slot][r + j * HD:r + (j + 1) * HD, :, at],
                                     q_rows[i, :, hs, tok]).then_inc(got, 16)
                sp.dma_start(qs[slot][QK_ROWS:K1, :, at], ap["al_q"][:, hs, at]).then_inc(got, 16)
                sp.dma_start(ks[slot][QK_ROWS:K2, :, at], ap["al_k"][:, hs, at]).then_inc(got, 16)

            def load_v(b):
                sp.dma_start(v_tok[:], vd.rearrange("(n p) d -> p n d", p=P)[:, bass.ds(b * BLK, BLK), :]
                             ).then_inc(T["v_loaded"], 16)

            def unit(b, g, first=False, last=False):
                n = b * NG + g
                if not (last and g == NG - 1):
                    if not first:
                        sp.wait_ge(T["scores"], n * NST)
                    load_half(b + (g + 1) // NG, (g + 1) % NG, 1)
                if g == NG - 2 and not last:
                    sp.wait_ge(T["vp"], n + 2)
                    load_v(b + 1)
                if not (last and g >= NG - 2):
                    sp.wait_ge(T["scores"], n * NST + 2 * SUB * HG)
                    load_half(b + (g + 2) // NG, (g + 2) % NG, 0)

            load_half(0, 0, 0)
            load_half(0, 0, 1)
            load_v(0)
            load_half(0, 1, 0)
            unit(0, 0, first=True)
            with sp.Fori(0, B - 1) as b:
                for g in range(1, NG):
                    unit(b, g)
                unit(b + 1, 0)
            for g in range(1, NG):
                unit(B - 1, g, last=True)

        def w_in_blocks(dst):
            for m, src in enumerate((bank(3)[:, 3 * P:4 * P], bank(4)[:, 0:P], bank(4)[:, P:2 * P])):
                to = dst[:, m * D:(m + 1) * D]
                if m < 2:
                    to, src = to.rearrange("p (d h) -> p h d", h=HEADS), src.rearrange("p (h d) -> p h d", h=HEADS)
                yield to, src

        def job_bank(k):
            return k % 4 if k < MROWS else 2 * (k % 2)

        def part(t, m, i):
            return qkp[:, bass.ds(t, 1), m, i, :].rearrange("p a n -> p (a n)")

        @block.sync
        def _(sp):
            for b in range(B):
                sp.dma_start(x[:, (SUB + b * BLK) * P:(SUB + b * BLK + BLK) * P].rearrange("p (n d) -> p n d", d=D),
                             x_blk[:, b * BLK:(b + 1) * BLK, :]).then_inc(s["x_loaded"], 16)
            with sp.Fori(0, B) as b:
                sp.wait_ge(s["split_lo"], b * 3 + 1)
                for m in range(3):
                    n = 2 if m < 2 else BLK
                    sp.dma_start(raw[m][:, :].rearrange("p (n f) -> p n f", n=n),
                                 ffn_src[m][:, bass.ds(b * n, n), :]).then_inc(s["raw_loaded"], 16)
            sp.wait_ge(s["a_x1"], TILES)
            store_qkv(sp)
            attention_loads(sp)
            sp.wait_ge(T["xadd"], 2 * B)
            sp.wait_ge(FS[1]["xadd"], TILES + 1)
            sp.dma_start(o_blk, x[:, NT:].rearrange("p (n d) -> p n d", d=D)).then_inc(s["stored"], 16)
            sp.wait_ge(s["stored"], 16)

        @block.gpsimd
        def _(pool):
            g = nc.gpsimd
            steps = [0]

            def setup(ins):
                steps[0] += 1
                ins.then_inc(s["pool_setup"], 1)
                pool.wait_ge(s["pool_setup"], steps[0])

            setup(g.memset(ident[:], 0.0))
            setup(g.affine_select(out=ident[:], in_=ident[:], compare_op=ALU.not_equal, fill=1.0, base=0,
                                  pattern=[[-1, P]], channel_multiplier=1))
            setup(g.memset(convx[:], 0.0))
            pool.wait_ge(s["conv_loaded"], 16)
            for gr in range(GROUPS):
                r = slice(gr * GW, (gr + 1) * GW)
                setup(g.tensor_copy(convx[r, :, gr * GW:(gr + 1) * GW],
                                    convraw[r, :].rearrange("o (i k) -> o k i", k=TAPS)))
            setup(g.iota(rinv[:].bitcast(I32), pattern=[[1, S]], base=1, channel_multiplier=0))
            setup(g.memset(half[:], -0.5))
            setup(g.memset(eps[:], EPS))
            g.memset(zeros[:], 0.0).then_inc(s["split_lo"], 1)
            pool.wait_ge(s["split_lo"], 1)
            setup(g.memset(hT[:, 0:TAPS - 1], 0.0))
            setup(g.tensor_copy(identb[:], ident[:]))
            for mask, sign in ((mask_qk, 1), (mask_kq, -1)):
                setup(g.memset(a0_tok[:, 0:P], 0.0))
                setup(g.affine_select(out=a0_tok[:, 0:P], in_=a0_tok[:, 0:P], compare_op=ALU.is_ge, fill=NEG,
                                      base=0, pattern=[[-sign, P]], channel_multiplier=sign))
                setup(g.tensor_copy(mask[:], a0_tok[:, 0:P]))

            def rstd(base, wait, n_wait, first):
                pool.wait_ge(wait, n_wait)
                done = [0]

                def link(ins):
                    done[0] += 1
                    ins.then_inc(s["a_pool"], 1)
                    pool.wait_ge(s["a_pool"], base + done[0])
                var, mean = mv[:, :, 1], mv[:, :, 0]
                link(g.tensor_tensor(lnw[:, 0, :], var, eps[:], ALU.add))
                link(g.tensor_tensor(lnw[:, 1, :], lnw[:, 0, :], half[:], ALU.pow))
                if first:
                    link(g.tensor_tensor(lnw[:, 2, :], lnw[:, 1, :], lnw[:, 1, :], ALU.mult))
                    link(g.tensor_tensor(lnw[:, 3, :], lnw[:, 2, :], var, ALU.mult))
                    link(g.tensor_tensor(lnw[:, 4, :], lnw[:, 3, :], eps[:], ALU.add))
                    link(g.tensor_tensor(lnw[:, 5, :], lnw[:, 4, :], half[:], ALU.pow))
                    link(g.tensor_tensor(lnw[:, 6, :], lnw[:, 5, :], lnw[:, 1, :], ALU.mult))
                src = 6 if first else 1
                link(g.tensor_tensor(lnw[:, 7, :], mean, lnw[:, src, :], ALU.mult))
                link(g.tensor_tensor(lnw[:, 4, :], zeros[:], lnw[:, 7, :], ALU.subtract))
                return done[0]

            with pool.Fori(0, B) as b:
                n = rstd(b * PA, s["a_mv"], b * BLK + BLK, True)
                n += rstd(b * PA + n, s["a_mv5"], b * BLK + BLK, False)
                n += rstd(b * PA + n, s["a_mv9"], b * BLK + BLK, False)
                assert n == PA
                pool.wait_ge(s["split_hi"], b * 3 + 3)
                for m in range(3):
                    g.tensor_tensor(w_lo[m][:, bass.ds(b * S, S)], raw[m][:],
                                    w_hi[m][:, bass.ds(b * S, S)].bitcast(F32), ALU.subtract).then_inc(s["split_lo"], 1)


            def rstd4(f, n0):
                g.tensor_tensor(lnw[:, 0, 0:SUB], mv[:, 0:SUB, 1], eps[:, 0:SUB], ALU.add).then_inc(f["rs"], 1)
                pool.wait_ge(f["rs"], n0 + 1)
                g.tensor_tensor(lnw[:, 1, 0:SUB], lnw[:, 0, 0:SUB], half[:, 0:SUB], ALU.pow).then_inc(f["rs"], 1)

            def ffn(f):
                with pool.Fori(0, TILES) as t:
                    pool.wait_ge(f["mv"], t * SUB + SUB)
                    rstd4(f, t * 2)

            pool.wait_ge(s["split_lo"], 3 * B + 1)
            ffn(FS[0])

            def attention():
                ffn(G)
                pool.wait_ge(G["stored"], 16 * 3 * TILES)
                g.memset(vp[:], 0.0).then_inc(T["init"], 1)
                pool.wait_ge(T["init"], 1)
                g.memset(vp[:, :, :, :, HD:HD + 1], 1.0).then_inc(T["init"], 1)
                pool.wait_ge(T["init"], 2)

            attention()
            ffn(FS[1])

        @block.tensor
        def _(pe):
            def transpose4(dst, src):
                for j in range(SUB):
                    mm = pe.transpose(dst[:, j * P:(j + 1) * P], src[:, j * P:(j + 1) * P], ident[:])
                return mm

            pe.wait_ge(s["pool_setup"], 8)
            pe.wait_ge(s["small_loaded"], 16 * N_SMALL)
            for t in range(T_COUNT):
                src = convx[:, t - T_CONV, :] if T_CONV <= t < T_IN else wraw[:, (t if t < T_CONV else t - 4) * P:(t + 1 if t < T_CONV else t - 3) * P]
                mm = pe.transpose(bank(t // 4)[:, (t % 4) * P:(t % 4 + 1) * P], src, ident[:])
            mm.then_inc(s["wraw_T"], 1)
            pe.transpose(bank(5)[:, 0:PAR_ROWS], prow[:, :], ident[0:PAR_ROWS, 0:PAR_ROWS]).then_inc(s["par_T"], 1)
            pe.wait_ge(s["wt_ready"], 8)
            pe.wait_ge(s["par_ready"], 1)

            with pe.Fori(0, B) as b:
                pe.wait_ge(s["a_tokd"], b * BLK + BLK)
                pe.wait_ge(s["a_toka"], b * BLK + BLK)
                for u in range(2):
                    transpose4(bank(u), a0_tok[:, u * NT:(u + 1) * NT])
                    transpose4(bank(2 + u), hc_tok[:, u * NT:(u + 1) * NT]).then_inc(s["a_T"], 1)
                for u in range(2):
                    pe.wait_ge(s["a_hT"], b * 2 + u + 1)
                    for k in range(TAPS):
                        mm = pe.matmul(bank(4 + u), W(T_CONV + k), hT[:, u * NT + k:u * NT + k + NT],
                                       start=(k == 0), stop=(k == TAPS - 1))
                    mm.then_inc(s["a_conv"], 1)
                for u in range(2):
                    pe.wait_ge(s["a_a1"], b * 2 + u + 1)
                    transpose4(bank(u), a0T[:, u * NT:(u + 1) * NT]).then_inc(s["a_T5"], 1)
                for u in range(2):
                    pe.wait_ge(s["a_n5d" if u else "a_n5"], b * 4 + 4)
                    transpose4(bank(2 + u), a0_tok[:, u * NT:(u + 1) * NT]).then_inc(s["a_T7"], 1)
                for u in range(2):
                    pe.wait_ge(s["a_h2"], b * 2 + u + 1)
                    for m, bk in ((T_Q, 4 + u), (T_K, 6 + u), (T_V, 0 + u)):
                        pe.matmul(bank(bk), W(m), h2T[:, u * NT:(u + 1) * NT], start=True,
                                  stop=True).then_inc(s["a_qkv"], 1)
                for u in range(2):
                    pe.wait_ge(s["a_a2"], b * 2 + u + 1)
                    transpose4(bank(2 + u), a0T[:, u * NT:(u + 1) * NT]).then_inc(s["a_T9"], 1)
                for u in range(2):
                    pe.wait_ge(s["a_n9d" if u else "a_n9"], b * 4 + 4)
                    transpose4(bank(4 + u), a0_tok[:, u * NT:(u + 1) * NT]).then_inc(s["a_T10"], 1)
                pe.wait_ge(s["a_h3"], b * 2 + 2)
                for n in range(9):
                    if n < 8:
                        u, c = divmod(n, 4)
                        if n >= 2:
                            pe.wait_ge(s["a_gel"], b * 8 + n - 1)
                        pe.matmul(bank(6 + n % 2), W(T_BOOM + c), h2T[:, u * NT:(u + 1) * NT], start=True,
                                  stop=True).then_inc(s["a_up"], 1)
                    if n >= 1:
                        u, c = divmod(n - 1, 4)
                        pe.wait_ge(s["a_gel"], b * 8 + n)
                        pe.matmul(bank(u), W(T_DOWN + c), gel[:, (n - 1) % 2, :], start=(c == 0),
                                  stop=(c == 3)).then_inc(s["a_dn"], 1)
                for u in range(2):
                    pe.wait_ge(s["a_y"], b * 2 + u + 1)
                    transpose4(bank(2 + u), a0T[:, u * NT:(u + 1) * NT]).then_inc(s["a_T13"], 1)
                pe.wait_ge(s["a_x1"], b * 2 + 2)


            def ffn(f):
                def gate_up(h, c):
                    w = slice(c * P, (c + 1) * P)
                    for m, sig in ((0, "gate"), (1, "up")):
                        dst = bank(2 * m + c % 2)
                        pe.matmul(dst, w_hi[m][:, w], xn_hi[:, h, :], start=True, stop=False)
                        pe.matmul(dst, w_hi[m][:, w], xn_lo[:, h, :], start=False, stop=False)
                        pe.matmul(dst, w_lo[m][:, w], xn_hi[:, h, :], start=False, stop=True).then_inc(f[sig], 1)

                def down(h, c):
                    w = slice(c * P, (c + 1) * P)
                    dst = bank(4 + h)
                    pe.matmul(dst, w_hi[2][:, w], h_hi[:, c % 2, :], start=(c == 0), stop=False)
                    pe.matmul(dst, w_hi[2][:, w], h_lo[:, c % 2, :], start=False, stop=False)
                    mm = pe.matmul(dst, w_lo[2][:, w], h_hi[:, c % 2, :], start=False, stop=(c == CH - 1))
                    mm.then_inc(f["y_done"] if c == CH - 1 else f["dn"], 1)

                def pair(i, last):
                    for h in range(2):
                        t = i * 2 + h
                        end = last and h == 1
                        for c in range(CH):
                            k = i * (2 * CH) + (h * CH + c)
                            if not (end and c >= CH - 2):
                                if c == CH - 2:
                                    pe.wait_ge(f["xlo"], t + 2)
                                pe.wait_ge(f["silu"], k + 1)
                                pe.wait_ge(f["prod"], k + 1)
                                gate_up(h if c + 2 < CH else 1 - h, (c + 2) % CH)
                            pe.wait_ge(f["hhi"], k + 1)
                            pe.wait_ge(f["hlo"], k + 1)
                            down(h, c)
                            if c == 3:
                                pe.wait_ge(f["y_out"], t + 1)
                                transpose4(bank(7), yS).then_inc(f["yT"], 1)
                            if c == 16 and not end:
                                pe.wait_ge(f["xadd"], t + 1)
                                pe.wait_ge(f["norm"], t * SUB + 2 * SUB)
                                transpose4(bank(7), ntok).then_inc(f["xT"], 1)

                pe.wait_ge(f["norm"], SUB)
                transpose4(bank(7), ntok).then_inc(f["xT"], 1)
                pe.wait_ge(f["xlo"], 1)
                gate_up(0, 0)
                gate_up(0, 1)
                with pe.Fori(0, TILES // 2 - 1) as i:
                    pair(i, False)
                pair(TILES // 2 - 1, True)
                pe.wait_ge(f["y_out"], TILES + 1)
                transpose4(bank(7), yS).then_inc(f["yT"], 1)
                pe.wait_ge(f["xadd"], TILES + 1)

            def project():
                def tile(h, t, last):
                    pe.wait_ge(G["xlo"], t + 1)
                    for m in range(2):
                        w = slice(m * D, (m + 1) * D)
                        dst = bank(2 * m + h)
                        pe.matmul(dst, win_hi[:, w], xn_hi[:, h, :], start=True, stop=False)
                        pe.matmul(dst, win_hi[:, w], xn_lo[:, h, :], start=False, stop=False)
                        pe.matmul(dst, win_lo[:, w], xn_hi[:, h, :], start=False, stop=True).then_inc(G["qk"], 1)
                    w = slice(2 * D, 3 * D)
                    for j in range(SUB):
                        tok = slice(j * P, (j + 1) * P)
                        dst = bank(4 + h)[:, tok]
                        pe.matmul(dst, xn_hi[:, h, tok], win_hi[:, w], start=True, stop=False)
                        pe.matmul(dst, xn_lo[:, h, tok], win_hi[:, w], start=False, stop=False)
                        mm = pe.matmul(dst, xn_hi[:, h, tok], win_lo[:, w], start=False, stop=True)
                    mm.then_inc(G["v"], 1)
                    if not last:
                        pe.wait_ge(G["norm"], t * SUB + 2 * SUB)
                        transpose4(bank(7), ntok).then_inc(G["xT"], 1)
                        pe.wait_ge(G["third"], t * 2 + 2)
                        pe.wait_ge(G["vcopy"], t + 1)

                pe.wait_ge(G["norm"], SUB)
                transpose4(bank(7), ntok).then_inc(G["xT"], 1)
                with pe.Fori(0, TILES // 2 - 1) as i:
                    tile(0, i * 2, False)
                    tile(1, i * 2 + 1, False)
                tile(0, TILES - 2, False)
                tile(1, TILES - 1, True)

            def attention():
                def take_max(k, base, slot):
                    h, i = JOBS[k]
                    keys = (i + 1) * P
                    free = k // 2 - 1 if k < 4 else k - 3 if k < MROWS else MROWS - 2 if k == MROWS else k - 1
                    if not (isinstance(base, int) and base + free < 1):
                        pe.wait_ge(T["reduced"], base + free)
                    r = job_bank(k)
                    lhs = qs[slot][0:K1, h, i * P:(i + 1) * P]
                    for lo in range(0, keys, NT):
                        w = min(NT, keys - lo)
                        diag = lo + w == keys
                        pe.matmul(ps[:, r + lo // NT, 0:w], lhs, ks[slot][0:K1, h, lo:lo + w],
                                  start=True, stop=not diag)
                    d = i * P % NT
                    pe.matmul(ps[:, r + i * P // NT, d:d + P], identb[:], mask_qk[:], start=False,
                              stop=True).then_inc(T["job"], 1)

                def maxima_T(c, n_red):
                    pe.wait_ge(T["reduced"], n_red)
                    pe.transpose(bank(7)[0:MROWS, 0:P], negm[:, c, :], ident[:]).then_inc(T["mT"], 1)

                def scores(n, slot, st, h):
                    c, j = STEPS[st]
                    k = st * HG + h
                    q0 = max(c * NT, j * P)
                    w = (c + 1) * NT - q0
                    if not (isinstance(n, int) and n == 0 and k < 2):
                        pe.wait_ge(T["exp"], n * NST + (k - 1))
                    diag = j >= c * SUB
                    mm = pe.matmul(bank(4 + k % 2)[:, 0:w], ks[slot][:, h, j * P:(j + 1) * P],
                                   qs[slot][:, h, q0:q0 + w], start=True, stop=not diag)
                    if diag:
                        mm = pe.matmul(bank(4 + k % 2)[:, 0:P], identb[:], mask_kq[:], start=False, stop=True)
                    mm.then_inc(T["scores"], 1)

                def weigh(n, slot, st):
                    c, j = STEPS[st]
                    q0 = max(c * NT, j * P) - c * NT
                    pe.wait_ge(T["exp"], n * NST + (st * HG + HG))
                    if j == 0 and not (isinstance(n, int) and n * 2 + c == 0):
                        pe.wait_ge(T["o_out"], n * 2 + c)
                    for h in range(HG):
                        mm = pe.matmul(ps[32 * h:32 * h + 32, 6, q0:NT], vp[:, slot, j, h, :],
                                       pr[:, st % 2, h, 0:NT - q0], start=(j == 0),
                                       stop=(j == SUB * c + SUB - 1))
                    if j == SUB * c + SUB - 1:
                        mm.then_inc(T["pv"], 1)

                def result_T(n, c):
                    pe.wait_ge(T["o_out"], n * 2 + c + 1)
                    transpose4(bank(7), ntok).then_inc(T["oT"], 1)

                def context_T(b, u):
                    pe.wait_ge(T["ctx"], b * (2 * NG) + 2 * NG)
                    if u == 1:
                        pe.wait_ge(T["xadd"], b * 2 + 1)
                    transpose4(bank(7), ctxt[:, u * SUB:(u + 1) * SUB, :].rearrange("p j d -> p (j d)")
                               ).then_inc(T["cT"], 1)

                def project_out(b, u):
                    pe.wait_ge(T["c_out"], b * 2 + u + 1)
                    for j in range(SUB):
                        mm = pe.matmul(bank(7)[:, j * P:(j + 1) * P], ctxT[:, j * P:(j + 1) * P],
                                       wout[:], start=True, stop=True)
                    mm.then_inc(T["proj"], 1)

                def unit(b, g, first=False, last=False):
                    n = b * NG + g
                    slot = g % 2
                    more = not (last and g == NG - 1)
                    base = n * len(JOBS) + len(JOBS)
                    k = 0
                    for st in range(len(STEPS)):
                        if STEPS[st][1] == 0:
                            pe.wait_ge(T[f"m_loaded{STEPS[st][0]}"], n * 16 + 16)
                        n_jobs = JOBS_AFTER[st] if more else 0
                        for h in range(HG):
                            if h == HEADS_FIRST:
                                if st == 1:
                                    pe.wait_ge(T["vp"], n + 1)
                                if st >= 1:
                                    weigh(n, slot, st - 1)
                                elif not first:
                                    weigh(n - 1, 1 - slot, len(STEPS) - 1)
                            scores(n, slot, st, h)
                            for _ in range((h + 1) * n_jobs // HG - h * n_jobs // HG):
                                if k % MROWS == 0:
                                    pe.wait_ge(T[f"loaded{1 - slot}{k // MROWS}"],
                                               b * (2 * LOADS) + ((g + 1) // 2 + 1) * LOADS)
                                take_max(k, base, 1 - slot)
                                k += 1
                        if st == 1 and not first:
                            pe.wait_ge(T["m_split"], n * 2 + 2)
                            result_T(n - 1, 1)
                        if g == 0 and not first:
                            if st in (2, 4):
                                context_T(b - 1, st // 2 - 1)
                            if st in (3, 5):
                                project_out(b - 1, st // 2 - 1)
                        if st == 6 and more:
                            if first:
                                pe.wait_ge(T["m_split"], 2)
                            elif g == 0:
                                pe.wait_ge(T["xadd"], b * 2)
                            else:
                                pe.wait_ge(T["ctx"], n * 2)
                            maxima_T(0, base + MROWS)
                        if st == 7:
                            if more:
                                pe.wait_ge(T["m_split"], n * 2 + 3)
                            else:
                                pe.wait_ge(T["ctx"], n * 2)
                            result_T(n, 0)
                        if st == len(STEPS) - 1 and more:
                            pe.wait_ge(T["ctx"], n * 2 + 1)
                            maxima_T(1, base + len(JOBS))

                pe.wait_ge(T["loaded00"], LOADS)
                for k in range(len(JOBS)):
                    if k == MROWS:
                        pe.wait_ge(T["loaded01"], LOADS)
                    take_max(k, 0, 0)
                    if k == MROWS + 1:
                        maxima_T(0, MROWS)
                pe.wait_ge(T["m_split"], 1)
                maxima_T(1, len(JOBS))
                unit(0, 0, first=True)
                with pe.Fori(0, B - 1) as b:
                    for g in range(1, NG):
                        unit(b, g)
                    unit(b + 1, 0)
                for g in range(1, NG):
                    unit(B - 1, g, last=True)
                weigh(UNITS - 1, 1, len(STEPS) - 1)
                pe.wait_ge(T["ctx"], UNITS * 2 - 1)
                result_T(UNITS - 1, 1)
                for u in range(2):
                    context_T(B - 1, u)
                    project_out(B - 1, u)
                pe.wait_ge(T["xadd"], B * 2)

            ffn(FS[0])
            project()
            pe.wait_ge(G["stored"], 16 * 3 * TILES)
            attention()
            ffn(FS[1])

        @block.scalar
        def _(act):
            a = nc.scalar
            load_small(act)
            act.wait_ge(s["wraw_T"], 1)
            for k in range(4):
                w = min(T_IN - 4 * k, 4) * P
                a.copy(wt[:, k * NT:k * NT + w], bank(k)[:, 0:w]).then_inc(s["wt_ready"], 1)
            for dst, src in w_in_blocks(win_hi):
                a.copy(dst, src).then_inc(s["wt_ready"], 1)
            a.copy(wout[:], bank(4)[:, 2 * P:3 * P]).then_inc(s["wt_ready"], 1)
            act.wait_ge(s["par_ready"], 1)

            def norm_blocks(src_banks, wait_sem, wait_n, mv_wait, scale_row, dst, done, which):
                for j in which:
                    a.activation(dst[:, j * P:(j + 1) * P], src_banks(j), ACT.Identity,
                                 bias=lnw[:, 4, j:j + 1], scale=lnw[:, scale_row, j:j + 1]).then_inc(done, 1)

            with act.Fori(0, B) as b:
                act.wait_ge(s["a_pool"], b * PA + 9)
                for j in range(BLK):
                    a.activation(hc_tok[:, j * P:(j + 1) * P], xs(b * BLK + j), ACT.Identity,
                                 bias=lnw[:, 4, j:j + 1], scale=lnw[:, 6, j:j + 1]).then_inc(s["a_toka"], 1)
                for u in range(2):
                    act.wait_ge(s["a_T"], b * 2 + u + 1)
                    a.activation(hT[:, TAPS - 1 + u * NT:TAPS - 1 + (u + 1) * NT], bank(2 + u), ACT.Identity,
                                 bias=col(R_CONV_B), scale=col(R_CONV_G)).then_inc(s["a_hT"], 1)
                act.wait_ge(s["raw_loaded"], b * 48 + 48)
                for m in range(3):
                    a.copy(w_hi[m][:, bass.ds(b * S, S)], raw[m][:]).then_inc(s["split_hi"], 1)
                act.wait_ge(s["a_pool"], b * PA + 13)
                for u in range(1):
                    for j in range(SUB):
                        a.activation(a0_tok[:, j * P:(j + 1) * P], bank(u)[:, (j % 4) * P:(j % 4 + 1) * P],
                                     ACT.Identity, bias=lnw[:, 4, j:j + 1],
                                     scale=lnw[:, 1, j:j + 1]).then_inc(s["a_n5"], 1)
                for u in range(2):
                    act.wait_ge(s["a_T7"], b * 2 + u + 1)
                    a.activation(h2T[:, u * NT:(u + 1) * NT], bank(2 + u), ACT.Identity,
                                 bias=col(R_ATTN_B), scale=col(R_ATTN_G)).then_inc(s["a_h2"], 1)
                act.wait_ge(s["a_pool"], b * PA + 17)
                for u in range(1):
                    for j in range(SUB):
                        a.activation(a0_tok[:, j * P:(j + 1) * P], bank(2 + u)[:, (j % 4) * P:(j % 4 + 1) * P],
                                     ACT.Identity, bias=lnw[:, 4, j:j + 1],
                                     scale=lnw[:, 1, j:j + 1]).then_inc(s["a_n9"], 1)
                for u in range(2):
                    act.wait_ge(s["a_T10"], b * 2 + u + 1)
                    a.activation(h2T[:, u * NT:(u + 1) * NT], bank(4 + u), ACT.Identity,
                                 bias=col(R_BOOM_B), scale=col(R_BOOM_G)).then_inc(s["a_h3"], 1)
                for n in range(8):
                    act.wait_ge(s["a_up"], b * 8 + n + 1)
                    if n >= 2:
                        act.wait_ge(s["a_dn"], b * 8 + n - 1)
                    a.activation(gel[:, n % 2, :], bank(6 + n % 2), ACT.Gelu,
                                 bias=col(R_BB + n % 4)).then_inc(s["a_gel"], 1)


            def ffn(f):
                def silu(c):
                    a.activation(sg[:, c % 2, :], bank(c % 2), ACT.Silu).then_inc(f["silu"], 1)

                def split_input(h):
                    a.copy(xn_hi[:, h, :], bank(7)).then_inc(f["xhi"], 1)

                def pair(i, last):
                    for h in range(2):
                        t = i * 2 + h
                        end = last and h == 1
                        for c in range(CH):
                            k = i * (2 * CH) + (h * CH + c)
                            if not (end and c == CH - 1):
                                act.wait_ge(f["gate"], k + 2)
                                silu((c + 1) % CH)
                            else:
                                act.wait_ge(f["dn"], (TILES * (CH - 1)) - 1)
                            act.wait_ge(f["prod"], k + 1)
                            a.copy(h_hi[:, c % 2, :], hid[:, c % 4, :]).then_inc(f["hhi"], 1)
                            if c == 1:
                                act.wait_ge(f["y_done"], t + 1)
                                a.copy(yS[:], bank(5 - h)).then_inc(f["y_out"], 1)
                            if c == 18 and not end:
                                act.wait_ge(f["xT"], t + 2)
                                split_input(1 - h)

                act.wait_ge(f["xT"], 1)
                split_input(0)
                act.wait_ge(f["gate"], 1)
                silu(0)
                with act.Fori(0, TILES // 2 - 1) as i:
                    pair(i, False)
                pair(TILES // 2 - 1, True)
                act.wait_ge(f["y_done"], TILES + 1)
                a.copy(yS[:], bank(5)).then_inc(f["y_out"], 1)

            def project():
                def tile(h, t, last):
                    for m in range(2):
                        act.wait_ge(G["qk"], t * 2 + m + 1)
                        a.activation(part(t, m, 0), bank(2 * m + h), ACT.Copy,
                                     scale=SCALE if m == 0 else 1.0).then_inc(G["first"], 1)
                    act.wait_ge(G["v"], t + 1)
                    a.copy(v_out[:, bass.ds(t, 1), :].rearrange("p a n -> p (a n)"), bank(4 + h)).then_inc(G["vcopy"], 1)
                    if not last:
                        act.wait_ge(G["xT"], t + 2)
                        a.copy(xn_hi[:, 1 - h, :], bank(7)).then_inc(G["xhi"], 1)
                    for m in range(2):
                        act.wait_ge(G["rest"], t * 2 + m + 1)
                        a.copy(part(t, m, 1), qkr[:, h, m, :]).then_inc(G["second"], 1)

                act.wait_ge(G["xT"], 1)
                a.copy(xn_hi[:, 0, :], bank(7)).then_inc(G["xhi"], 1)
                with act.Fori(0, TILES // 2 - 1) as i:
                    tile(0, i * 2, False)
                    tile(1, i * 2 + 1, False)
                tile(0, TILES - 2, False)
                tile(1, TILES - 1, True)

            def attention():
                def place_values(b, g):
                    act.wait_ge(T["v_loaded"], b * 16 + 16)
                    a.copy(vp[:, g % 2, :, :, 0:HD],
                           v_tok[:, :, g * HG * HD:(g + 1) * HG * HD].rearrange("p j (h d) -> p j h d", h=HG)
                           ).then_inc(T["vp"], 1)

                def result_out(n, c):
                    act.wait_ge(T["pv"], n * 2 + c + 1)
                    if not (isinstance(n, int) and n * 2 + c == 0):
                        act.wait_ge(T["oT"], n * 2 + c)
                    a.copy(ntok[:], bank(6)).then_inc(T["o_out"], 1)

                def context_out(b, u):
                    act.wait_ge(T["cT"], b * 2 + u + 1)
                    if u == 1:
                        act.wait_ge(T["proj"], b * 2 + 1)
                    a.copy(ctxT[:], bank(7)).then_inc(T["c_out"], 1)

                def maxima_out(e, slot, c):
                    act.wait_ge(T["m_parts"], e * 3 + 3)
                    act.dma_start(md[slot, c].rearrange("i r q -> r i q"), mpart[:]).then_inc(T["m_stored"], 16)

                def maxima_in(e, slot, c):
                    act.wait_ge(T["m_stored"], e * 16 + 16)
                    act.dma_start(qs[slot][K1:K2, :, c * NT:(c + 1) * NT],
                                  md[slot, c].rearrange("i (h n) q -> i h (n q)", h=HG)
                                  ).then_inc(T[f"m_loaded{c}"], 16)

                def unit(b, g, first=False, last=False):
                    n = b * NG + g
                    more = not (last and g == NG - 1)
                    for st, (c, j) in enumerate(STEPS):
                        w = (c + 1) * NT - max(c * NT, j * P)
                        for h in range(HG):
                            k = st * HG + h
                            act.wait_ge(T["scores"], n * NST + (k + 1))
                            a.activation(pr[:, st % 2, h, 0:w], bank(4 + k % 2)[:, 0:w],
                                         ACT.Exp).then_inc(T["exp"], 1)
                        if st == 0 and not first:
                            result_out(n - 1, 1)
                            maxima_out(n * 2 + 1, g % 2, 1)
                        if st == 1 and not first:
                            maxima_in(n * 2 + 1, g % 2, 1)
                        if st == 8 and more:
                            maxima_out(n * 2 + 2, 1 - g % 2, 0)
                        if st == 9 and more:
                            maxima_in(n * 2 + 2, 1 - g % 2, 0)
                        if st == 1 and more:
                            place_values(b + (g + 1) // NG, (g + 1) % NG)
                        if g == 0 and not first and st in (2, 4):
                            context_out(b - 1, st // 2 - 1)
                        if st == SUB:
                            result_out(n, 0)

                for c in range(2):
                    maxima_out(c, 0, c)
                    maxima_in(c, 0, c)
                act.wait_ge(T["init"], 2)
                place_values(0, 0)
                unit(0, 0, first=True)
                with act.Fori(0, B - 1) as b:
                    for g in range(1, NG):
                        unit(b, g)
                    unit(b + 1, 0)
                for g in range(1, NG):
                    unit(B - 1, g, last=True)
                result_out(UNITS - 1, 1)
                for u in range(2):
                    context_out(B - 1, u)

            ffn(FS[0])
            project()
            attention()
            ffn(FS[1])

        @block.vector
        def _(dve):
            v = nc.vector
            v.memset(zcol[:], 0.0).then_inc(s["zeros"], 1)
            dve.wait_ge(s["zeros"], 1)
            dve.wait_ge(s["pool_setup"], 8)
            v.tensor_copy(cq[:], rinv[:].bitcast(I32)).then_inc(s["rinv_ready"], 1)
            dve.wait_ge(s["rinv_ready"], 1)
            v.reciprocal(rinv[:], cq[:]).then_inc(s["rinv_ready"], 1)
            dve.wait_ge(s["par_T"], 1)
            v.tensor_copy(par[:], bank(5)[:, 0:PAR_ROWS]).then_inc(s["par_ready"], 1)
            dve.wait_ge(s["wt_ready"], 8)
            for (dst, src), (hi, _) in zip(w_in_blocks(win_lo), w_in_blocks(win_hi)):
                v.tensor_tensor(dst, src, hi.bitcast(F32), ALU.subtract).then_inc(s["wt_ready"], 1)
            dve.wait_ge(s["x_loaded"], 16 * B)
            dve.wait_ge(s["par_ready"], 1)

            def stats(b, src, st_sem, mv_sem, waits):
                for j in range(BLK):
                    if j in waits:
                        dve.wait_ge(*waits[j])
                    v.bn_stats(st[:, j, :], src(j)).then_inc(st_sem, 1)
                dve.wait_ge(st_sem, b * BLK + BLK)
                v.memset(fence[:], 0.0)
                for j in range(BLK):
                    v.bn_aggr(mv[:, j, :], st[:, j, :]).then_inc(mv_sem, 1)

            with dve.Fori(0, B) as b:
                stats(b, lambda j: xs(b * BLK + j), s["a_st"], s["a_mv"], {})
                dve.wait_ge(s["a_pool"], b * PA + 9)
                for j in range(BLK):
                    v.tensor_scalar(a0_tok[:, j * P:(j + 1) * P], xs(b * BLK + j), mv[:, j, 0:1],
                                    lnw[:, 1, j:j + 1], ALU.subtract, ALU.mult).then_inc(s["a_tokd"], 1)
                for u in range(2):
                    dve.wait_ge(s["a_T"], b * 2 + u + 1)
                    v.tensor_copy(a0T[:, u * NT:(u + 1) * NT], bank(u)).then_inc(s["a_copyD"], 1)
                for u in range(2):
                    dve.wait_ge(s["a_conv"], b * 2 + u + 1)
                    dve.wait_ge(s["a_copyD"], b * 2 + u + 1)
                    v.scalar_tensor_tensor(a0T[:, u * NT:(u + 1) * NT], bank(4 + u), col(R_CONV_BIAS),
                                           a0T[:, u * NT:(u + 1) * NT], ALU.add, ALU.add).then_inc(s["a_a1"], 1)
                stats(b, lambda j: bank(j // 4)[:, (j % 4) * P:(j % 4 + 1) * P], s["a_st5"], s["a_mv5"],
                      {0: (s["a_T5"], b * 2 + 1), 4: (s["a_T5"], b * 2 + 2)})
                dve.wait_ge(s["a_pool"], b * PA + 13)
                for u in (1,):
                    for j in range(SUB, BLK):
                        v.tensor_scalar(a0_tok[:, j * P:(j + 1) * P], bank(u)[:, (j % 4) * P:(j % 4 + 1) * P],
                                        mv[:, j, 0:1], lnw[:, 1, j:j + 1], ALU.subtract, ALU.mult).then_inc(s["a_n5d"], 1)
                for u in range(2):
                    sl = slice(u * NT, (u + 1) * NT)
                    n0 = b * 12 + 6 * u
                    dve.wait_ge(s["a_qkv"], b * 6 + 3 * u + 1)
                    v.tensor_tensor_scan(cq[:, sl], bank(4 + u), col(R_BQ).to_broadcast([P, NT]),
                                         0.0 if u == 0 else cq[:, NT - 1:NT], ALU.add, ALU.add).then_inc(s["a_d8"], 1)
                    dve.wait_ge(s["a_d8"], n0 + 1)
                    v.tensor_tensor(pq[:, sl], cq[:, sl], rinv[:, sl], ALU.mult).then_inc(s["a_d8"], 1)
                    dve.wait_ge(s["a_d8"], n0 + 2)
                    dve.wait_ge(s["a_qkv"], b * 6 + 3 * u + 3)
                    v.scalar_tensor_tensor(pq[:, sl], bank(6 + u), col(R_BK), pq[:, sl], ALU.add,
                                           ALU.mult).then_inc(s["a_d8"], 1)
                    dve.wait_ge(s["a_d8"], n0 + 3)
                    v.tensor_tensor_scan(hc_tok[:, sl], pq[:, sl], zcol[:].to_broadcast([P, NT]),
                                         0.0 if u == 0 else hc_tok[:, NT - 1:NT], ALU.add, ALU.add).then_inc(s["a_d8"], 1)
                    dve.wait_ge(s["a_d8"], n0 + 4)
                    v.tensor_tensor(pq[:, sl], hc_tok[:, sl], rinv[:, sl], ALU.mult).then_inc(s["a_d8"], 1)
                    dve.wait_ge(s["a_d8"], n0 + 5)
                    v.scalar_tensor_tensor(pq[:, sl], bank(0 + u), col(R_BV), pq[:, sl], ALU.add,
                                           ALU.mult).then_inc(s["a_d8"], 1)
                    dve.wait_ge(s["a_d8"], n0 + 6)
                    v.tensor_tensor(a0T[:, sl], a0T[:, sl], pq[:, sl], ALU.add).then_inc(s["a_a2"], 1)
                stats(b, lambda j: bank(2 + j // 4)[:, (j % 4) * P:(j % 4 + 1) * P], s["a_st9"], s["a_mv9"],
                      {0: (s["a_T9"], b * 2 + 1), 4: (s["a_T9"], b * 2 + 2)})
                dve.wait_ge(s["a_pool"], b * PA + 17)
                for u in (1,):
                    for j in range(SUB, BLK):
                        v.tensor_scalar(a0_tok[:, j * P:(j + 1) * P], bank(2 + u)[:, (j % 4) * P:(j % 4 + 1) * P],
                                        mv[:, j, 0:1], lnw[:, 1, j:j + 1], ALU.subtract, ALU.mult).then_inc(s["a_n9d"], 1)
                for u in range(2):
                    sl = slice(u * NT, (u + 1) * NT)
                    dve.wait_ge(s["a_dn"], b * 8 + 4 * u + 4)
                    dve.wait_ge(s["a_a2"], b * 2 + u + 1)
                    v.scalar_tensor_tensor(a0T[:, sl], bank(u), col(R_BU), a0T[:, sl], ALU.add,
                                           ALU.add).then_inc(s["a_y"], 1)
                for u in range(2):
                    dve.wait_ge(s["a_T13"], b * 2 + u + 1)
                    v.tensor_tensor(xs(b * BLK + 4 * u, SUB), xs(b * BLK + 4 * u, SUB), bank(2 + u),
                                    ALU.add).then_inc(s["a_x1"], 1)

            def norm_steps(f):
                def stats4(t, n0):
                    for j in range(SUB):
                        v.bn_stats(st[:, j, :], xs(t * SUB + j)).then_inc(f["st"], 1)
                    dve.wait_ge(f["st"], n0 + SUB)
                    v.memset(fence[:], 0.0)
                    for j in range(SUB):
                        v.bn_aggr(mv[:, j, :], st[:, j, :]).then_inc(f["mv"], 1)

                def norm4(t):
                    for j in range(SUB):
                        v.tensor_scalar(ntok[:, j * P:(j + 1) * P], xs(t * SUB + j), mv[:, j, 0:1],
                                        lnw[:, 1, j:j + 1], ALU.subtract, ALU.mult).then_inc(f["norm"], 1)

                return stats4, norm4

            def ffn(f):
                stats4, norm4 = norm_steps(f)

                def product(c):
                    v.tensor_tensor(hid[:, c % 4, :], sg[:, c % 2, :], bank(2 + c % 2), ALU.mult).then_inc(f["prod"], 1)

                def split_input(h):
                    v.tensor_tensor(xn_lo[:, h, :], bank(7), xn_hi[:, h, :].bitcast(F32),
                                    ALU.subtract).then_inc(f["xlo"], 1)

                def pair(i, last):
                    for h in range(2):
                        t = i * 2 + h
                        end = last and h == 1
                        for c in range(CH):
                            k = i * (2 * CH) + (h * CH + c)
                            if not (end and c == CH - 1):
                                dve.wait_ge(f["up"], k + 2)
                                dve.wait_ge(f["silu"], k + 2)
                                product((c + 1) % CH)
                            dve.wait_ge(f["hhi"], k + 1)
                            v.tensor_tensor(h_lo[:, c % 2, :], hid[:, c % 4, :], h_hi[:, c % 2, :].bitcast(F32),
                                            ALU.subtract).then_inc(f["hlo"], 1)
                            if c == 5:
                                dve.wait_ge(f["yT"], t + 1)
                                v.tensor_tensor(xs(t * SUB - SUB, SUB), xs(t * SUB - SUB, SUB), bank(7),
                                                ALU.add).then_inc(f["xadd"], 1)
                            if end:
                                continue
                            if c == 7:
                                stats4(t + 1, t * SUB + SUB)
                            if c == 12:
                                dve.wait_ge(f["rs"], t * 2 + 4)
                                norm4(t + 1)
                            if c == 20:
                                dve.wait_ge(f["xhi"], t + 2)
                                split_input(1 - h)

                v.memset(x[:, 0:NT], 0.0)
                v.memset(bank(5), 0.0).then_inc(f["y_done"], 1)
                stats4(0, 0)
                dve.wait_ge(f["rs"], 2)
                norm4(0)
                dve.wait_ge(f["xhi"], 1)
                split_input(0)
                dve.wait_ge(f["up"], 1)
                dve.wait_ge(f["silu"], 1)
                product(0)
                with dve.Fori(0, TILES // 2 - 1) as i:
                    pair(i, False)
                pair(TILES // 2 - 1, True)
                dve.wait_ge(f["yT"], TILES + 1)
                v.tensor_tensor(xs(TILES * SUB - SUB, SUB), xs(TILES * SUB - SUB, SUB), bank(7),
                                ALU.add).then_inc(f["xadd"], 1)

            def project():
                stats4, norm4 = norm_steps(G)

                def split_input(t, h):
                    dve.wait_ge(G["xhi"], t + 1)
                    v.tensor_tensor(xn_lo[:, h, :], bank(7), xn_hi[:, h, :].bitcast(F32),
                                    ALU.subtract).then_inc(G["xlo"], 1)

                def tile(h, t, last):
                    if not last:
                        stats4(t + 1, t * SUB + SUB)
                    for m in range(2):
                        dve.wait_ge(G["first"], t * 2 + m + 1)
                        v.scalar_tensor_tensor(qkr[:, h, m, :], bank(2 * m + h), SCALE if m == 0 else 1.0,
                                               part(t, m, 0), ALU.mult, ALU.subtract).then_inc(G["rest"], 1)
                    if not last:
                        dve.wait_ge(G["rs"], t * 2 + 4)
                        norm4(t + 1)
                        split_input(t + 1, 1 - h)
                    for m in range(2):
                        dve.wait_ge(G["second"], t * 2 + m + 1)
                        v.tensor_tensor(part(t, m, 2), qkr[:, h, m, :], part(t, m, 1),
                                        ALU.subtract).then_inc(G["third"], 1)

                stats4(0, 0)
                dve.wait_ge(G["rs"], 2)
                norm4(0)
                split_input(0, 0)
                with dve.Fori(0, TILES // 2 - 1) as i:
                    tile(0, i * 2, False)
                    tile(1, i * 2 + 1, False)
                tile(0, TILES - 2, False)
                tile(1, TILES - 1, True)

            def attention():
                def reduce_job(k, base):
                    h, i = JOBS[k]
                    c, col_ = divmod(k, MROWS)
                    dve.wait_ge(T["job"], base + (k + 1))
                    v.tensor_reduce(negm[:, c, col_:col_ + 1],
                                    ps[:, job_bank(k):job_bank(k) + 1 + i // SUB, :].rearrange(
                                        "p a n -> p (a n)")[:, 0:(i + 1) * P],
                                    AX.X, ALU.max, negate=True).then_inc(T["reduced"], 1)

                def split_max(e):
                    src = bank(7)[0:MROWS, 0:P]
                    if not (isinstance(e, int) and e == 0):
                        dve.wait_ge(T["m_stored"], e * 16)
                    dve.wait_ge(T["mT"], e + 1)
                    v.tensor_copy(mpart[:, 0, :], src).then_inc(T["m_parts"], 1)
                    dve.wait_ge(T["m_parts"], e * 3 + 1)
                    v.tensor_tensor(mres[:], src, mpart[:, 0, :], ALU.subtract).then_inc(T["m_split"], 1)
                    dve.wait_ge(T["m_split"], e + 1)
                    v.tensor_copy(mpart[:, 1, :], mres[:]).then_inc(T["m_parts"], 1)
                    dve.wait_ge(T["m_parts"], e * 3 + 2)
                    v.tensor_tensor(mpart[:, 2, :], mres[:], mpart[:, 1, :],
                                    ALU.subtract).then_inc(T["m_parts"], 1)

                def normalise(n, g, c):
                    src = bank(7).rearrange("p (t h w) -> p t h w", t=SUB, h=HG)
                    dve.wait_ge(T["oT"], n * 2 + c + 1)
                    v.reciprocal(rl[:], src[:, :, :, HD]).then_inc(T["onorm"], 1)
                    dve.wait_ge(T["onorm"], n * 2 + c + 1)
                    v.tensor_tensor(
                        ctxt[:, c * SUB:(c + 1) * SUB, g * HG * HD:(g + 1) * HG * HD].rearrange(
                            "p t (h d) -> p t h d", h=HG),
                        src[:, :, :, 0:HD], rl[:].unsqueeze(3).to_broadcast([P, SUB, HG, HD]),
                        ALU.mult).then_inc(T["ctx"], 1)

                def add_projection(b, u):
                    dve.wait_ge(T["proj"], b * 2 + u + 1)
                    v.tensor_tensor(xs(b * BLK + u * SUB, SUB), xs(b * BLK + u * SUB, SUB), bank(7),
                                    ALU.add).then_inc(T["xadd"], 1)

                def unit(b, g, first=False, last=False):
                    n = b * NG + g
                    more = not (last and g == NG - 1)
                    k = 0
                    for st in range(len(STEPS)):
                        if st == 0 and not first:
                            split_max(n * 2 + 1)
                        if st == 2 and not first:
                            normalise(n - 1, (g - 1) % NG, 1)
                        if g == 0 and not first and st in (4, 6):
                            add_projection(b - 1, st // 2 - 2)
                        if st == 7 and more:
                            split_max(n * 2 + 2)
                        if st == 8:
                            normalise(n, g, 0)
                        for _ in range(JOBS_AFTER[st] if more else 0):
                            reduce_job(k, n * len(JOBS) + len(JOBS))
                            k += 1

                for k in range(len(JOBS)):
                    reduce_job(k, 0)
                    if k == MROWS + 1:
                        split_max(0)
                split_max(1)
                unit(0, 0, first=True)
                with dve.Fori(0, B - 1) as b:
                    for g in range(1, NG):
                        unit(b, g)
                    unit(b + 1, 0)
                for g in range(1, NG):
                    unit(B - 1, g, last=True)
                normalise(UNITS - 1, NG - 1, 1)
                for u in range(2):
                    add_projection(B - 1, u)

            dve.wait_ge(s["a_x1"], TILES)
            ffn(FS[0])
            project()
            attention()
            ffn(FS[1])


LOADS = 16 * (PARTS + PARTS * PARTS + 2)
PA = 9 + 4 + 4


NAMES = {"hidden": "attn_a_hidden_states", "conv_w": "attn_a_conv_w", "conv_b": "attn_a_conv_b",
         "ln_conv_g": "attn_a_ln_conv_g", "ln_conv_b": "attn_a_ln_conv_b",
         "ln_attn_g": "attn_a_ln_attn_g", "ln_attn_b": "attn_a_ln_attn_b",
         "ln_boom_g": "attn_a_ln_boom_g", "ln_boom_b": "attn_a_ln_boom_b",
         "Wq": "attn_a_Wq", "Wk": "attn_a_Wk", "Wv": "attn_a_Wv", "bq": "attn_a_bq",
         "bk": "attn_a_bk", "bv": "attn_a_bv", "Wb": "attn_a_Wb", "bb": "attn_a_bb",
         "Wu": "attn_a_Wu", "bu": "attn_a_bu", "w_in": "attn_b_w_in", "w_out": "attn_b_w_out",
         "Wg": "ffn_Wg", "Wu8": "ffn_Wu", "Wd": "ffn_Wd"}


def bf16_parts(a, n):
    parts, rest = [], np.asarray(a, np.float64)
    for _ in range(n):
        p = rest.astype(BF16_NP)
        parts.append(p)
        rest = rest - p.astype(np.float64)
    return parts


def alibi_rows():
    slope = (2.0 ** (-8.0 / HEADS * (np.arange(HEADS, dtype=np.float32) + 1.0))).astype(np.float32)
    pos = np.arange(S)
    cut = [(pos // P * P).astype(BF16_NP), (pos % P).astype(BF16_NP)]
    k_rows = np.ones((AL_ROWS + PARTS, HEADS, S), BF16_NP)
    q_rows = np.zeros((AL_ROWS, HEADS, S), BF16_NP)
    r = 0
    for c in cut:
        for p in bf16_parts(slope, PARTS):
            k_rows[r], q_rows[r] = c[None, :], p[:, None]
            k_rows[r + 1], q_rows[r + 1] = -p[:, None], c[None, :]
            r += 2
    return k_rows, q_rows


def kernel(**inputs):
    import concourse.bacc as bacc
    from concourse.bass_utils import run_bass_kernel_spmd

    nc = bacc.Bacc("TRN2", target_bir_lowering=False, num_devices=1)
    arrays, aps = {}, {}
    for short, name in NAMES.items():
        arrays[f"in_{short}"] = np.ascontiguousarray(inputs["L0_" + name])
    arrays["in_al_k"], arrays["in_al_q"] = alibi_rows()
    for name, a in arrays.items():
        aps[name[3:]] = nc.dram_tensor(name, a.shape, mybir.dt.from_np(a.dtype), kind="ExternalInput").ap()
    aps["out"] = nc.dram_tensor("out_0", (B, S, D), F32, kind="ExternalOutput").ap()
    build(nc, aps)
    r = run_bass_kernel_spmd(nc, [arrays], core_ids=[0])
    return r.results[0]["out_0"]
```

```python
from contextlib import ExitStack

import concourse.bass as bass
import numpy as np
from concourse import mybir

F32 = mybir.dt.float32
F32R = mybir.dt.float32r
BF16 = mybir.dt.bfloat16
I32 = mybir.dt.int32
BF16_NP = mybir.dt.np(BF16)
ALU = mybir.AluOpType
ACT = mybir.ActivationFunctionType
AX = mybir.AxisListType

P = 128
D = 128
B, S = 4, 1024
TOK = B * S
NT = 512
TILES = TOK // NT
SUB = NT // P
BLK = S // P
EPS = 1e-5
TAPS, GROUPS = 4, 4
GW = D // GROUPS
EXPERTS, FFN = 8, 512
CH = EXPERTS * FFN // P
WCOLS = EXPERTS * FFN
HEADS, HD = 16, 8
HG = 4
NG = HEADS // HG
UNITS = B * NG
PARTS = 3
QK_ROWS = PARTS * PARTS * HD
AL_ROWS = 12
K1 = QK_ROWS + AL_ROWS
K2 = K1 + PARTS
MROWS = HG * SUB
SCALE = float(np.float32(1.0) / np.sqrt(np.float32(HD)))
STEPS = [(c, j) for c in range(2) for j in range(SUB * c + SUB)]
WIDTH = [(c + 1) * NT - max(c * NT, j * P) for c, j in STEPS]
SHARE = [max(n for n in (1, 2, 4) if n * w <= NT) for w in WIDTH]
BEFORE = [sum(HG // n for n in SHARE[:st]) for st in range(len(STEPS) + 1)]
NST = BEFORE[-1]
JOBS = [(h, i) for c in range(2) for h in range(HG) for i in range(SUB * c, SUB * c + SUB)]
JOBS_AFTER = [4, 4, 4, 4, 3, 3, 2, 2, 2, 2, 2, 0]
PROJECT_STEPS, PROJECT_FROM = 9, 1
JOBS_BESIDE = [0, 4, 4, 4, 4, 4, 4, 4, 4]
RING = 3
HEADS_FIRST = HG // 2
NEG = -1e30

AT = {"tok": (0, 1), "T1": (2, 4), "copy": (2, 4), "conv": (5, 6), "a1": (6, 7), "T5": (7, 8),
      "stats5": (8, 9), "norm5": (11, 13), "T7": (12, 14), "h2": (12, 14),
      "q": (15, 18), "k": (16, 21), "v": (17, 20),
      "cumq": (15, 19), "kq": (17, 21), "cumk": (18, 22), "vq": (20, 24),
      "T9": (23, 26), "stats9": (23, 26), "norm9": (29, 30), "T10": (30, 31), "h3": (30, 31),
      "up": (32, 37), "gelu": (36, 41), "down": (42, 44), "y": (43, 45), "T13": (44, 46),
      "x1": (44, 46)}
UP_AT = [AT["up"][0] + c for c in range(4)] + [AT["up"][1]] * 4
DOWN_AT = [AT["down"][0]] * 4 + [AT["down"][1] + c // 2 for c in range(4)]
NORM_AT = (10, 16)
SPLIT_AT = (5, 10, 19, 27)

(R_CONV_G, R_CONV_B, R_CONV_BIAS, R_ATTN_G, R_ATTN_B, R_BQ, R_BK, R_BV, R_BOOM_G, R_BOOM_B, R_BB,
 R_BU) = (0, 1, 2, 3, 4, 5, 6, 7, 8, 9, 10, 14)
PAR_ROWS = 15
L_MEAN, L_RSTD, L_BOTH, L_BOTH_BIAS = 0, 1, 2, 3
T_Q, T_K, T_V, T_BOOM, T_DOWN, T_CONV, T_IN, T_OUT = 0, 1, 2, 3, 7, 11, 15, 18
T_COUNT = 19


def build(nc, ap):
    x_in, out = ap["hidden"], ap["out"]
    with ExitStack() as ctx:
        def sb(name, shape, dt=F32, stack=ctx):
            return stack.enter_context(nc.sbuf_tensor(name, shape, dt))

        def sem(name):
            return ctx.enter_context(nc.semaphore(name))

        x = sb("x", [P, (SUB + TOK // P) * P])
        w_hi = [sb(f"w_hi{m}", [P, WCOLS], F32R) for m in range(3)]
        w_lo = [sb(f"w_lo{m}", [P, WCOLS], F32R) for m in range(3)]
        xn_hi = sb("xn_hi", [P, 2, NT], F32R)
        xn_lo = sb("xn_lo", [P, 2, NT], F32R)
        ident = sb("ident", [P, P])
        identb = sb("identb", [P, P], BF16)
        mask_qk = sb("mask_qk", [P, P], BF16)
        mask_kq = sb("mask_kq", [P, P], BF16)
        par = sb("par", [P, PAR_ROWS])
        win_hi = sb("win_hi", [P, 3 * D], F32R)
        win_lo = sb("win_lo", [P, 3 * D], F32R)
        wout = sb("wout", [P, D])
        half = sb("half", [P, B * BLK])
        eps = sb("eps", [P, B * BLK])
        zeros = sb("zeros", [P, B * BLK])
        zcol = sb("zcol", [P, 1])
        fence = sb("fence", [P, 1])
        st = sb("st", [P, SUB, 6])
        mv = sb("mv", [P, SUB, 2])
        lnw = sb("lnw", [P, 2, SUB])
        ntok = sb("ntok", [P, NT])

        ps = ctx.enter_context(nc.psum_tensor("ps", [P, 8, NT], F32))

        stp = sb("stp", [P, SUB, 6])
        mvp = sb("mvp", [P, SUB, 2])
        lnp = sb("lnp", [P, 2, SUB])
        negm = sb("negm", [P, 2, MROWS])
        mpart = sb("mpart", [MROWS, PARTS, P], BF16)
        mres = sb("mres", [MROWS, P])

        convraw = sb("convraw", [P, GW * TAPS])
        with ExitStack() as one:
            raw0 = [sb(f"raw0{m}", [P, S], F32, one) for m in range(3)]
            prow = sb("prow", [PAR_ROWS, P], F32, one)
            wraw = sb("wraw", [P, 15 * P], F32, one)
            convx = sb("convx", [P, TAPS, P], F32, one)
        with ExitStack() as one:
            q1, k1 = (sb(n, [K2, HG, S], BF16, one) for n in ("qs1", "ks1"))
            v_tok = sb("v_tok", [P, BLK, D], F32, one)
            rl = sb("rl", [P, SUB, HG], F32, one)
        sg = sb("sg", [P, 2, NT])
        hid = sb("hid", [P, 4, NT])
        h_hi = sb("h_hi", [P, 2, NT], F32R)
        h_lo = sb("h_lo", [P, 2, NT], F32R)
        yS = sb("yS", [P, NT])
        with ExitStack() as two:
            wt = sb("wt", [P, T_IN * P], F32, two)
            rinv = sb("rinv", [P, S], F32, two)
            a0T = sb("a0T", [P, S], F32, two)
            hT = sb("hT", [P, TAPS - 1 + S], F32, two)
            h2T = sb("h2T", [P, S], F32, two)
            work = sb("work", [P, 4, S], F32, two)
            a0_tok, hc_tok, cq, pq = (work[:, i, :] for i in range(4))
            gel = work[:].rearrange("p i (a n) -> p (i a) n", n=NT)
            stx = sb("stx", [P, B * BLK, 6], F32, two)
            mvx = sb("mvx", [P, B * BLK, 2], F32, two)
            tmpx = sb("tmpx", [P, 4, B * BLK], F32, two)
            lnx = sb("lnx", [P, 4, B * BLK], F32, two)
            lns = sb("lns", [P, 4, BLK], F32, two)
            sta = sb("sta", [P, BLK, 6], F32, two)
            mva = sb("mva", [P, BLK, 2], F32, two)
            lna = sb("lna", [P, 4, BLK], F32, two)
            raw1 = [sb(f"raw1{m}", [P, S], F32, two) for m in range(3)]
        raw = (raw0, raw1)
        with ExitStack() as two:
            q0, k0 = (sb(n, [K2, HG, S], BF16, two) for n in ("qs0", "ks0"))
            with ExitStack() as gg:
                qkp = sb("qkp", [P, RING, 2, PARTS, NT], BF16, gg)
                qkr = sb("qkr", [P, 2, 2, NT], F32, gg)
                v_out = sb("v_out", [P, RING, NT], F32, gg)
                ntok2 = sb("ntok2", [P, NT], F32, gg)
                xp_hi = sb("xp_hi", [P, NT], F32R, gg)
                xp_lo = sb("xp_lo", [P, NT], F32R, gg)
            vp = sb("vp", [P, 2, BLK, HG, 32], F32, two)
            ctxt = sb("ctxt", [P, BLK, D], F32, two)
            ctxT = sb("ctxT", [P, NT], F32, two)
            pr = sb("pr", [P, 2, HG, NT], F32, two)
            qs, ks = (q0, q1), (k0, k1)
        qkd = [nc.dram_tensor(n, (PARTS, D, TOK), BF16, kind="Internal").ap() for n in ("qd", "kd")]
        vd = nc.dram_tensor("vd", (TOK, D), F32, kind="Internal").ap()
        md = nc.dram_tensor("md", (2, 2, PARTS, MROWS, P), BF16, kind="Internal").ap()

        names = """x_loaded x_rest_loaded small_loaded zeros pool_setup conv_loaded
            wraw_T wt_ready par_T par_ready rinv_ready
            raw_loaded0 raw_loaded1 split_hi split_lo
            a_stx a_mvx a_lnx a_lns a_pool a_tokd a_toka a_T a_copyD a_hT a_conv a_a1 a_T5 a_st5 a_mv5
            a_n5 a_T7 a_h2 a_q a_k a_v a_cumq a_meanq a_kq a_cumk a_meank a_vq a_a2 a_T9 a_st9 a_mv9
            a_n9 a_T10 a_h3 a_up a_hid0 a_hid1 a_gel a_dn a_y a_T13 a_x1 stored""".split()
        s = {n: sem(n) for n in names}
        FF_NAMES = "st mv rs norm xT xhi xlo gate up silu prod hhi hlo dn y_done y_out yT xadd".split()
        FS = [{n: sem(f"ff{layer}_{n}") for n in FF_NAMES} for layer in range(2)]
        PREP_NAMES = "st mv rs norm xT xhi xlo qk v first rest second third vcopy stored0 stored1 stored2".split()
        G = {n: sem(f"prep_{n}") for n in PREP_NAMES}
        ATT_NAMES = """init v_loaded loaded00 loaded01 loaded10 loaded11 m_loaded0 m_loaded1 vp
            scores exp pv o_out oT onorm ctx job reduced mT m_split
            m_parts m_stored cT c_out proj xadd""".split()
        T = {n: sem(f"att_{n}") for n in ATT_NAMES}
        block = ctx.enter_context(nc.Block())

        def bank(n):
            return ps[:, n, :]

        def xs(blk, n=1):
            return x[:, bass.ds(blk * P + NT, n * P)]

        def col(r):
            return par[:, r:r + 1]

        def W(slot, n=1):
            return wt[:, slot * P:(slot + n) * P]

        x_blk = x_in.rearrange("b s d -> (b s) d").rearrange("(n p) d -> p n d", p=P)
        o_blk = out.rearrange("b s d -> (b s) d").rearrange("(n p) d -> p n d", p=P)

        SMALL_ROWS = [("ln_conv_g", R_CONV_G), ("ln_conv_b", R_CONV_B), ("conv_b", R_CONV_BIAS),
                      ("ln_attn_g", R_ATTN_G), ("ln_attn_b", R_ATTN_B), ("bq", R_BQ), ("bk", R_BK),
                      ("bv", R_BV), ("ln_boom_g", R_BOOM_G), ("ln_boom_b", R_BOOM_B), ("bu", R_BU)]
        SMALL_MATS = [("Wq", T_Q), ("Wk", T_K), ("Wv", T_V)]
        N_SMALL = len(SMALL_ROWS) + 1 + len(SMALL_MATS) + 4

        def load_rows(q):
            q.dma_start(convraw[:], ap["conv_w"].rearrange("o i k -> o (i k)")).then_inc(s["conv_loaded"], 16)
            for n, r in SMALL_ROWS:
                q.dma_start(prow[r:r + 1, :], ap[n].rearrange("(a d) -> a d", a=1)).then_inc(s["small_loaded"], 16)
            q.dma_start(prow[R_BB:R_BB + 4, :], ap["bb"].rearrange("(a d) -> a d", a=4)).then_inc(s["small_loaded"], 16)

        def load_matrices(q):
            for n, t in SMALL_MATS:
                q.dma_start(wraw[:, t * P:(t + 1) * P], ap[n]).then_inc(s["small_loaded"], 16)
            q.dma_start(wraw[:, T_BOOM * P:(T_BOOM + 4) * P].rearrange("p (c d) -> p c d", c=4),
                        ap["Wb"].rearrange("(c p) d -> p c d", p=P)).then_inc(s["small_loaded"], 16)
            q.dma_start(wraw[:, T_DOWN * P:(T_DOWN + 4) * P], ap["Wu"]).then_inc(s["small_loaded"], 16)
            q.dma_start(wraw[:, 11 * P:14 * P].rearrange("p (c d) -> p c d", c=3),
                        ap["w_in"].rearrange("(c p) d -> p c d", p=P)).then_inc(s["small_loaded"], 16)
            q.dma_start(wraw[:, 14 * P:15 * P], ap["w_out"]).then_inc(s["small_loaded"], 16)

        ffn_src = [ap["Wg"].rearrange("e d f -> d e f"), ap["Wu8"].rearrange("e d f -> d e f"),
                   ap["Wd"].rearrange("e (m p) d -> p (e m) d", p=P)]

        def store_qkv(sp, t):
            done, tok = G[f"stored{t % RING}"], slice(t * NT, (t + 1) * NT)
            sp.wait_ge(G["third"], t * 2 + 2)
            sp.wait_ge(G["second"], t * 2 + 2)
            sp.wait_ge(G["first"], t * 2 + 2)
            for m in range(2):
                sp.dma_start(qkd[m].rearrange("i f t -> f i t")[:, :, tok], qkp[:, t % RING, m, :, :]).then_inc(done, 16)
            sp.wait_ge(G["vcopy"], t + 1)
            sp.dma_start(vd.rearrange("(n p) d -> p n d", p=P)[:, t * SUB:(t + 1) * SUB, :],
                         v_out[:, t % RING, :].rearrange("p (n d) -> p n d", d=D)).then_inc(done, 16)

        def wait_stored(engine):
            for slot in range(RING):
                engine.wait_ge(G[f"stored{slot}"], 48 * len(range(slot, TILES, RING)))

        def attention_loads(sp):
            def load_half(b, g, c):
                hs, slot = slice(g * HG, (g + 1) * HG), g % 2
                tok, at = bass.ds(b * S + c * NT, NT), slice(c * NT, (c + 1) * NT)
                got = T[f"loaded{slot}{c}"]
                q_rows = qkd[0].rearrange("i (d h) t -> i d h t", h=HEADS)
                k_rows = qkd[1].rearrange("j (d h) t -> (j d) h t", h=HEADS)
                for i in range(PARTS):
                    r = i * PARTS * HD
                    sp.dma_start(ks[slot][r:r + PARTS * HD, :, at], k_rows[:, hs, tok]).then_inc(got, 16)
                    for j in range(PARTS):
                        sp.dma_start(qs[slot][r + j * HD:r + (j + 1) * HD, :, at],
                                     q_rows[i, :, hs, tok]).then_inc(got, 16)
                sp.dma_start(qs[slot][QK_ROWS:K1, :, at], ap["al_q"][:, hs, at]).then_inc(got, 16)
                sp.dma_start(ks[slot][QK_ROWS:K2, :, at], ap["al_k"][:, hs, at]).then_inc(got, 16)

            def load_v(b):
                sp.dma_start(v_tok[:], vd.rearrange("(n p) d -> p n d", p=P)[:, bass.ds(b * BLK, BLK), :]
                             ).then_inc(T["v_loaded"], 16)

            def unit(b, g, first=False, last=False):
                n = b * NG + g
                if not (last and g == NG - 1):
                    if not first:
                        sp.wait_ge(T["scores"], n * NST)
                    load_half(b + (g + 1) // NG, (g + 1) % NG, 1)
                if g == NG - 2 and not last:
                    sp.wait_ge(T["vp"], n + 2)
                    load_v(b + 1)
                if not (last and g >= NG - 2):
                    sp.wait_ge(T["scores"], n * NST + BEFORE[2 * SUB])
                    load_half(b + (g + 2) // NG, (g + 2) % NG, 0)

            for t in range(TILES):
                if t == TILES - 1:
                    sp.wait_ge(FS[0]["xadd"], TILES + 1)
                    load_half(0, 1, 0)
                    load_v(0)
                store_qkv(sp, t)
                if t == 1:
                    sp.wait_ge(G["stored0"], 48)
                    sp.wait_ge(G["stored1"], 48)
                    load_half(0, 0, 0)
                if t == 2:
                    load_half(0, 0, 1)
            wait_stored(sp)
            unit(0, 0, first=True)
            with sp.Fori(0, B - 1) as b:
                for g in range(1, NG):
                    unit(b, g)
                unit(b + 1, 0)
            for g in range(1, NG):
                unit(B - 1, g, last=True)

        def w_in_blocks(dst):
            for m, src in enumerate((bank(3)[:, 3 * P:4 * P], bank(4)[:, 0:P], bank(4)[:, P:2 * P])):
                to = dst[:, m * D:(m + 1) * D]
                if m < 2:
                    to, src = to.rearrange("p (d h) -> p h d", h=HEADS), src.rearrange("p (h d) -> p h d", h=HEADS)
                yield to, src

        def job_bank(k):
            return k % 4 if k < MROWS else 2 * (k % 2)

        def part(t, m, i):
            return qkp[:, t % RING, m, i, :]

        @block.sync
        def _(sp):
            for b in range(B):
                sp.dma_start(x[:, (SUB + b * BLK) * P:(SUB + b * BLK + BLK) * P].rearrange("p (n d) -> p n d", d=D),
                             x_blk[:, b * BLK:(b + 1) * BLK, :]).then_inc(s["x_loaded" if b == 0 else "x_rest_loaded"], 16)
            load_matrices(sp)
            for r in range(4):
                if r >= 2:
                    sp.wait_ge(s["split_lo"], (r - 1) * 3)
                for m in range(3):
                    n = 2 if m < 2 else BLK
                    sp.dma_start(raw[r % 2][m][:, :].rearrange("p (n f) -> p n f", n=n),
                                 ffn_src[m][:, r * n:(r + 1) * n, :]).then_inc(s[f"raw_loaded{r % 2}"], 16)
            attention_loads(sp)
            with sp.Fori(0, TILES) as t:
                sp.wait_ge(FS[1]["xadd"], t + 2)
                sp.dma_start(o_blk[:, bass.ds(t * SUB, SUB), :],
                             xs(t * SUB, SUB).rearrange("p (n d) -> p n d", d=D)).then_inc(s["stored"], 16)
            sp.wait_ge(s["stored"], 16 * TILES)

        @block.gpsimd
        def _(pool):
            g = nc.gpsimd
            steps = [0]

            def setup(ins):
                steps[0] += 1
                ins.then_inc(s["pool_setup"], 1)
                pool.wait_ge(s["pool_setup"], steps[0])

            setup(g.memset(ident[:], 0.0))
            setup(g.affine_select(out=ident[:], in_=ident[:], compare_op=ALU.not_equal, fill=1.0, base=0,
                                  pattern=[[-1, P]], channel_multiplier=1))
            setup(g.memset(half[:], -0.5))
            setup(g.memset(eps[:], EPS))
            setup(g.memset(zeros[:], 0.0))
            setup(g.memset(hT[:, 0:TAPS - 1], 0.0))
            setup(g.memset(convx[:], 0.0))
            pool.wait_ge(s["conv_loaded"], 16)
            for gr in range(GROUPS):
                r = slice(gr * GW, (gr + 1) * GW)
                setup(g.tensor_copy(convx[r, :, gr * GW:(gr + 1) * GW],
                                    convraw[r, :].rearrange("o (i k) -> o k i", k=TAPS)))
            assert steps[0] == SETUP_MATRICES

            def late_setup():
                setup(g.iota(rinv[:].bitcast(I32), pattern=[[1, S]], base=1, channel_multiplier=0))
                setup(g.tensor_copy(identb[:], ident[:]))
                setup(g.memset(pq[:, 0:P], 0.0))
                setup(g.affine_select(out=pq[:, 0:P], in_=pq[:, 0:P], compare_op=ALU.is_ge, fill=NEG,
                                      base=0, pattern=[[-1, P]], channel_multiplier=1))
                setup(g.tensor_copy(mask_qk[:], pq[:, 0:P]))
                setup(g.memset(pq[:, 0:P], 0.0))
                setup(g.affine_select(out=pq[:, 0:P], in_=pq[:, 0:P], compare_op=ALU.is_ge, fill=NEG,
                                      base=0, pattern=[[1, P]], channel_multiplier=-1))
                setup(g.tensor_copy(mask_kq[:], pq[:, 0:P]))

            def norms_of_input(lo, hi):
                pool.wait_ge(s["a_mvx"], hi)
                done = [10 if lo else 0]

                def link(ins):
                    done[0] += 1
                    ins.then_inc(s["a_lnx"], 1)
                    pool.wait_ge(s["a_lnx"], done[0])

                e, h, z = eps[:, lo:hi], half[:, lo:hi], zeros[:, lo:hi]
                mean, var = mvx[:, lo:hi, 0], mvx[:, lo:hi, 1]
                tmp = [tmpx[:, i, lo:hi] for i in range(4)]
                L = [lnx[:, i, lo:hi] for i in range(4)]
                link(g.tensor_tensor(tmp[0], var, e, ALU.add))
                link(g.tensor_tensor(L[L_RSTD], tmp[0], h, ALU.pow))
                link(g.tensor_tensor(tmp[1], L[L_RSTD], L[L_RSTD], ALU.mult))
                link(g.tensor_tensor(tmp[2], tmp[1], var, ALU.mult))
                link(g.tensor_tensor(tmp[3], tmp[2], e, ALU.add))
                link(g.tensor_tensor(tmp[0], tmp[3], h, ALU.pow))
                link(g.tensor_tensor(L[L_BOTH], tmp[0], L[L_RSTD], ALU.mult))
                link(g.tensor_tensor(tmp[1], mean, L[L_BOTH], ALU.mult))
                link(g.tensor_tensor(L[L_BOTH_BIAS], z, tmp[1], ALU.subtract))
                link(g.tensor_tensor(L[L_MEAN], mean, z, ALU.add))

            def inner_norm(base, got, n_got, u):
                sl, one = slice(u * SUB, (u + 1) * SUB), slice(0, SUB)
                pool.wait_ge(got, n_got)
                done = [0]

                def link(ins):
                    done[0] += 1
                    ins.then_inc(s["a_pool"], 1)
                    pool.wait_ge(s["a_pool"], base + done[0])

                link(g.tensor_tensor(lna[:, 0, sl], mva[:, sl, 1], eps[:, one], ALU.add))
                link(g.tensor_tensor(lna[:, 1, sl], lna[:, 0, sl], half[:, one], ALU.pow))
                link(g.tensor_tensor(lna[:, 2, sl], mva[:, sl, 0], lna[:, 1, sl], ALU.mult))
                link(g.tensor_tensor(lna[:, 3, sl], zeros[:, one], lna[:, 2, sl], ALU.subtract))

            def sequence_step(b, p):
                for u in range(2):
                    if p == AT["stats5"][u]:
                        inner_norm(b * 16 + 4 * u, s["a_mv5"], b * BLK + SUB * (u + 1), u)
                    if p == AT["stats9"][u]:
                        inner_norm(b * 16 + 4 * u + 8, s["a_mv9"], b * BLK + SUB * (u + 1), u)
                    sl = slice(u * NT, (u + 1) * NT)
                    if p == AT["cumq"][u]:
                        pool.wait_ge(s["a_cumq"], b * 2 + u + 1)
                        g.tensor_tensor(pq[:, sl], cq[:, sl], rinv[:, sl], ALU.mult).then_inc(s["a_meanq"], 1)
                    if p == AT["cumk"][u]:
                        pool.wait_ge(s["a_cumk"], b * 2 + u + 1)
                        g.tensor_tensor(pq[:, sl], hc_tok[:, sl], rinv[:, sl], ALU.mult).then_inc(s["a_meank"], 1)
                    if p == AT["vq"][u]:
                        pool.wait_ge(s["a_vq"], b * 2 + u + 1)
                        g.tensor_tensor(a0T[:, sl], a0T[:, sl], pq[:, sl], ALU.add).then_inc(s["a_a2"], 1)

            norms_of_input(0, BLK)
            late_setup()
            for p in range(2 * CH):
                if p == AT["cumq"][0]:
                    pool.wait_ge(s["rinv_ready"], 2)
                sequence_step(0, p)
                if p in SPLIT_AT[:3]:
                    r = SPLIT_AT.index(p)
                    pool.wait_ge(s["split_hi"], r * 3 + 3)
                    for m in range(3):
                        g.tensor_tensor(w_lo[m][:, r * S:(r + 1) * S], raw[r % 2][m][:],
                                        w_hi[m][:, r * S:(r + 1) * S].bitcast(F32),
                                        ALU.subtract).then_inc(s["split_lo"], 1)
            norms_of_input(BLK, B * BLK)

            def rstd4(f, n0, mv=mv, lnw=lnw):
                g.tensor_tensor(lnw[:, 0, :], mv[:, :, 1], eps[:, 0:SUB], ALU.add).then_inc(f["rs"], 1)
                pool.wait_ge(f["rs"], n0 + 1)
                g.tensor_tensor(lnw[:, 1, :], lnw[:, 0, :], half[:, 0:SUB], ALU.pow).then_inc(f["rs"], 1)

            def project_step(t, r):
                if r == 0:
                    pool.wait_ge(G["mv"], (t + 1) * SUB)
                    rstd4(G, t * 2, mvp, lnp)
                if r == 8:
                    for m in range(2):
                        pool.wait_ge(G["second"], t * 2 + m + 1)
                        g.tensor_tensor(part(t, m, 2), qkr[:, t % 2, m, :], part(t, m, 1),
                                        ALU.subtract).then_inc(G["third"], 1)

            def ffn(f):
                with pool.Fori(0, TILES) as t:
                    pool.wait_ge(f["mv"], t * SUB + SUB)
                    rstd4(f, t * 2)

            def ffn_beside_sequences(f):
                def norm(t):
                    pool.wait_ge(f["mv"], t * SUB + SUB)
                    rstd4(f, t * 2)

                norm(0)
                with pool.Fori(0, TILES // 2 - 1) as i:
                    for p in range(2 * CH):
                        sequence_step(i + 1, p)
                        if p % CH == NORM_AT[p // CH]:
                            norm(i * 2 + (p // CH + 1))
                for p in range(2 * CH):
                    if p == NORM_AT[0]:
                        norm(TILES - 1)
                    if p >= PROJECT_FROM:
                        project_step(*divmod(p - PROJECT_FROM, PROJECT_STEPS))

            ffn_beside_sequences(FS[0])

            def attention():
                for r in range(PROJECT_STEPS):
                    project_step(TILES - 1, r)
                wait_stored(pool)
                g.memset(vp[:], 0.0).then_inc(T["init"], 1)
                pool.wait_ge(T["init"], 1)
                g.memset(vp[:, :, :, :, HD:HD + 1], 1.0).then_inc(T["init"], 1)
                pool.wait_ge(T["init"], 2)

            attention()
            ffn(FS[1])

        @block.tensor
        def _(pe):
            def transpose4(dst, src):
                for j in range(SUB):
                    mm = pe.transpose(dst[:, j * P:(j + 1) * P], src[:, j * P:(j + 1) * P], ident[:])
                return mm

            def sequence_step(b, p, first=False):
                for u in range(2):
                    dst, sl = bank(5 + u), slice(u * NT, (u + 1) * NT)
                    if p == AT["T1"][u]:
                        pe.wait_ge(s["a_tokd"], b * BLK + SUB * (u + 1))
                        pe.wait_ge(s["a_toka"], b * BLK + SUB * (u + 1))
                        if u == 1:
                            pe.wait_ge(s["a_copyD"], b * 2 + 1)
                            pe.wait_ge(s["a_hT"], b * 2 + 1)
                        elif not first:
                            pe.wait_ge(s["a_x1"], b * 2)
                        transpose4(bank(5), a0_tok[:, sl])
                        transpose4(bank(6), hc_tok[:, sl]).then_inc(s["a_T"], 1)
                    if p == AT["conv"][u]:
                        pe.wait_ge(s["a_hT"], b * 2 + 1 + u)
                        if u == 0:
                            pe.wait_ge(s["a_copyD"], b * 2 + 2)
                        for k in range(TAPS):
                            mm = pe.matmul(dst, W(T_CONV + k), hT[:, u * NT + k:u * NT + k + NT],
                                           start=(k == 0), stop=(k == TAPS - 1))
                        mm.then_inc(s["a_conv"], 1)
                    if p == AT["T5"][u]:
                        pe.wait_ge(s["a_a1"], b * 2 + u + 1)
                        transpose4(dst, a0T[:, sl]).then_inc(s["a_T5"], 1)
                    if p == AT["T7"][u]:
                        pe.wait_ge(s["a_n5"], b * BLK + SUB * (u + 1))
                        transpose4(dst, a0_tok[:, sl]).then_inc(s["a_T7"], 1)
                    if p == AT["q"][u]:
                        pe.wait_ge(s["a_h2"], b * 2 + u + 1)
                        if u == 1:
                            pe.wait_ge(s["a_kq"], b * 2 + 1)
                        pe.matmul(dst, W(T_Q), h2T[:, sl], start=True, stop=True).then_inc(s["a_q"], 1)
                    if p == AT["k"][u]:
                        if u == 0:
                            pe.wait_ge(s["a_h2"], b * 2 + 2)
                        else:
                            pe.wait_ge(s["a_vq"], b * 2 + 1)
                        pe.matmul(bank(6 - u), W(T_K), h2T[:, sl], start=True, stop=True).then_inc(s["a_k"], 1)
                    if p == AT["v"][u]:
                        pe.wait_ge(s["a_cumq"], b * 2 + u + 1)
                        pe.matmul(dst, W(T_V), h2T[:, sl], start=True, stop=True).then_inc(s["a_v"], 1)
                    if p == AT["T9"][u]:
                        pe.wait_ge(s["a_a2"], b * 2 + u + 1)
                        if u == 0:
                            pe.wait_ge(s["a_kq"], b * 2 + 2)
                        transpose4(dst, a0T[:, sl]).then_inc(s["a_T9"], 1)
                    if p == AT["T10"][u]:
                        pe.wait_ge(s["a_n9"], b * BLK + SUB * (u + 1))
                        transpose4(dst, a0_tok[:, sl]).then_inc(s["a_T10"], 1)
                    for c in range(4):
                        n = u * 4 + c
                        if p == UP_AT[n]:
                            if n < 2:
                                pe.wait_ge(s["a_h3"], b * 2 + n + 1)
                            elif n < 6:
                                pe.wait_ge(s["a_hid0"], b * 4 + n - 1)
                            else:
                                pe.wait_ge(s["a_hid1"], b * 4 + n - 5)
                            pe.matmul(bank(5 + n % 2), W(T_BOOM + c), h2T[:, sl], start=True,
                                      stop=True).then_inc(s["a_up"], 1)
                    for c in range(4):
                        if p == DOWN_AT[u * 4 + c]:
                            if c == 0:
                                pe.wait_ge(s["a_gel"], b * 2 + u + 1)
                                pe.wait_ge(s["a_hid1"], b * 4 + 4)
                            mm = pe.matmul(dst, W(T_DOWN + c), gel[:, u * 4 + c, :], start=(c == 0), stop=(c == 3))
                            if c == 3:
                                mm.then_inc(s["a_dn"], 1)
                    if p == AT["T13"][u]:
                        pe.wait_ge(s["a_y"], b * 2 + u + 1)
                        transpose4(dst, a0T[:, sl]).then_inc(s["a_T13"], 1)

            pe.wait_ge(s["pool_setup"], SETUP_MATRICES)
            for p in range(AT["T1"][0] + 1):
                sequence_step(0, p, first=True)
            pe.wait_ge(s["pool_setup"], SETUP_MATRICES)
            pe.wait_ge(s["small_loaded"], 16 * N_SMALL)
            for t in range(T_COUNT):
                if T_CONV <= t < T_IN:
                    src = convx[:, t - T_CONV, :]
                else:
                    r = t if t < T_CONV else t - TAPS
                    src = wraw[:, r * P:(r + 1) * P]
                mm = pe.transpose(bank(t // 4)[:, (t % 4) * P:(t % 4 + 1) * P], src, ident[:])
            mm.then_inc(s["wraw_T"], 1)
            pe.transpose(bank(7)[:, 0:PAR_ROWS], prow[:, :], ident[0:PAR_ROWS, 0:PAR_ROWS]).then_inc(s["par_T"], 1)
            pe.wait_ge(s["wt_ready"], 8)
            pe.wait_ge(s["par_ready"], 1)

            for p in range(AT["T1"][0] + 1, 2 * CH):
                sequence_step(0, p, first=True)

            def project_step(t, r):
                if r == 3:
                    pe.wait_ge(G["norm"], (t + 1) * SUB)
                    if t:
                        pe.wait_ge(G["vcopy"], t)
                    transpose4(bank(5), ntok2).then_inc(G["xT"], 1)
                if r == 5:
                    pe.wait_ge(G["xlo"], t + 1)
                    for m in range(2):
                        w, dst = slice(m * D, (m + 1) * D), bank(5 + m)
                        if m and t:
                            pe.wait_ge(G["rest"], t * 2)
                        pe.matmul(dst, win_hi[:, w], xp_hi[:], start=True, stop=False)
                        pe.matmul(dst, win_hi[:, w], xp_lo[:], start=False, stop=False)
                        pe.matmul(dst, win_lo[:, w], xp_hi[:], start=False, stop=True).then_inc(G["qk"], 1)
                if r == 7:
                    w = slice(2 * D, 3 * D)
                    pe.wait_ge(G["rest"], t * 2 + 1)
                    for j in range(SUB):
                        tok = slice(j * P, (j + 1) * P)
                        pe.matmul(bank(5)[:, tok], xp_hi[:, tok], win_hi[:, w], start=True, stop=False)
                        pe.matmul(bank(5)[:, tok], xp_lo[:, tok], win_hi[:, w], start=False, stop=False)
                        mm = pe.matmul(bank(5)[:, tok], xp_hi[:, tok], win_lo[:, w], start=False, stop=True)
                    mm.then_inc(G["v"], 1)

            def ffn(f, sequences):
                def gate_up(h, c):
                    w = slice(c * P, (c + 1) * P)
                    for m, sig in ((0, "gate"), (1, "up")):
                        dst = bank(2 * m + c % 2)
                        pe.matmul(dst, w_hi[m][:, w], xn_hi[:, h, :], start=True, stop=False)
                        pe.matmul(dst, w_hi[m][:, w], xn_lo[:, h, :], start=False, stop=False)
                        pe.matmul(dst, w_lo[m][:, w], xn_hi[:, h, :], start=False, stop=True).then_inc(f[sig], 1)

                def down(h, c):
                    w = slice(c * P, (c + 1) * P)
                    dst = bank(4)
                    pe.matmul(dst, w_hi[2][:, w], h_hi[:, c % 2, :], start=(c == 0), stop=False)
                    pe.matmul(dst, w_hi[2][:, w], h_lo[:, c % 2, :], start=False, stop=False)
                    mm = pe.matmul(dst, w_lo[2][:, w], h_hi[:, c % 2, :], start=False, stop=(c == CH - 1))
                    mm.then_inc(f["y_done"] if c == CH - 1 else f["dn"], 1)

                def pair(i, last):
                    for h in range(2):
                        t = i * 2 + h
                        end = last and h == 1
                        for c in range(CH):
                            k = i * (2 * CH) + (h * CH + c)
                            if sequences and not last:
                                sequence_step(i + 1, h * CH + c)
                            if sequences and last and h * CH + c >= PROJECT_FROM:
                                project_step(*divmod(h * CH + c - PROJECT_FROM, PROJECT_STEPS))
                            if c == NORM_AT[h] + 4 and not end:
                                pe.wait_ge(f["xadd"], t + 1)
                                pe.wait_ge(f["norm"], t * SUB + 2 * SUB)
                                transpose4(bank(7), ntok).then_inc(f["xT"], 1)
                            if not (end and c >= CH - 2):
                                if c == CH - 2:
                                    pe.wait_ge(f["xlo"], t + 2)
                                pe.wait_ge(f["silu"], k + 1)
                                pe.wait_ge(f["prod"], k + 1)
                                gate_up(h if c + 2 < CH else 1 - h, (c + 2) % CH)
                            pe.wait_ge(f["hhi"], k + 1)
                            pe.wait_ge(f["hlo"], k + 1)
                            if c == 0:
                                pe.wait_ge(f["y_out"], t + 1)
                            down(h, c)
                            if c == 3:
                                transpose4(bank(7), yS).then_inc(f["yT"], 1)

                if sequences:
                    pe.wait_ge(f["norm"], SUB)
                    transpose4(bank(7), ntok).then_inc(f["xT"], 1)
                pe.wait_ge(f["xlo"], 1)
                gate_up(0, 0)
                gate_up(0, 1)
                with pe.Fori(0, TILES // 2 - 1) as i:
                    pair(i, False)
                pair(TILES // 2 - 1, True)
                pe.wait_ge(f["y_out"], TILES + 1)
                transpose4(bank(7), yS).then_inc(f["yT"], 1)
                if not sequences:
                    pe.wait_ge(f["xadd"], TILES + 1)

            def attention():
                def take_max(k, base, slot):
                    h, i = JOBS[k]
                    keys = (i + 1) * P
                    free = k // 2 - 1 if k < 4 else k - 3 if k < MROWS else MROWS - 2 if k == MROWS else k - 1
                    if not (isinstance(base, int) and base + free < 1):
                        pe.wait_ge(T["reduced"], base + free)
                    r = job_bank(k)
                    lhs = qs[slot][0:K1, h, i * P:(i + 1) * P]
                    for lo in range(0, keys, NT):
                        w = min(NT, keys - lo)
                        diag = lo + w == keys
                        pe.matmul(ps[:, r + lo // NT, 0:w], lhs, ks[slot][0:K1, h, lo:lo + w],
                                  start=True, stop=not diag)
                    d = i * P % NT
                    pe.matmul(ps[:, r + i * P // NT, d:d + P], identb[:], mask_qk[:], start=False,
                              stop=True).then_inc(T["job"], 1)

                def maxima_T(c, n_red):
                    pe.wait_ge(T["reduced"], n_red)
                    pe.transpose(bank(7)[0:MROWS, 0:P], negm[:, c, :], ident[:]).then_inc(T["mT"], 1)

                def scores(n, slot, st, h):
                    c, j = STEPS[st]
                    w, share = WIDTH[st], SHARE[st]
                    k = BEFORE[st] + h // share
                    q0 = max(c * NT, j * P)
                    if h % share == 0 and not (isinstance(n, int) and n == 0 and k < 2):
                        pe.wait_ge(T["exp"], n * NST + (k - 1))
                    diag = j >= c * SUB
                    dst = bank(4 + k % 2)[:, h % share * w:(h % share + 1) * w]
                    mm = pe.matmul(dst, ks[slot][:, h, j * P:(j + 1) * P], qs[slot][:, h, q0:q0 + w],
                                   start=True, stop=not diag)
                    if diag:
                        mm = pe.matmul(dst[:, 0:P], identb[:], mask_kq[:], start=False, stop=True)
                    if h % share == share - 1:
                        mm.then_inc(T["scores"], 1)

                def weigh(n, slot, st):
                    c, j = STEPS[st]
                    q0 = max(c * NT, j * P) - c * NT
                    pe.wait_ge(T["exp"], n * NST + BEFORE[st + 1])
                    if j == 0 and not (isinstance(n, int) and n * 2 + c == 0):
                        pe.wait_ge(T["o_out"], n * 2 + c)
                    for h in range(HG):
                        mm = pe.matmul(ps[32 * h:32 * h + 32, 6, q0:NT], vp[:, slot, j, h, :],
                                       pr[:, st % 2, h, 0:NT - q0], start=(j == 0),
                                       stop=(j == SUB * c + SUB - 1))
                    if j == SUB * c + SUB - 1:
                        mm.then_inc(T["pv"], 1)

                def result_T(n, c):
                    pe.wait_ge(T["o_out"], n * 2 + c + 1)
                    transpose4(bank(7), ntok).then_inc(T["oT"], 1)

                def context_T(b, u):
                    pe.wait_ge(T["ctx"], b * (2 * NG) + 2 * NG)
                    if u == 1:
                        pe.wait_ge(T["xadd"], b * 2 + 1)
                    transpose4(bank(7), ctxt[:, u * SUB:(u + 1) * SUB, :].rearrange("p j d -> p (j d)")
                               ).then_inc(T["cT"], 1)

                def project_out(b, u):
                    pe.wait_ge(T["c_out"], b * 2 + u + 1)
                    for j in range(SUB):
                        mm = pe.matmul(bank(7)[:, j * P:(j + 1) * P], ctxT[:, j * P:(j + 1) * P],
                                       wout[:], start=True, stop=True)
                    mm.then_inc(T["proj"], 1)

                def unit(b, g, first=False, last=False):
                    n = b * NG + g
                    slot = g % 2
                    more = not (last and g == NG - 1)
                    base = n * len(JOBS) + len(JOBS)
                    k = 0
                    for st in range(len(STEPS)):
                        if STEPS[st][1] == 0:
                            pe.wait_ge(T[f"m_loaded{STEPS[st][0]}"], n * 16 + 16)
                        n_jobs = JOBS_AFTER[st] if more else 0
                        for h in range(HG):
                            if h == HEADS_FIRST:
                                if st == 1:
                                    pe.wait_ge(T["vp"], n + 1)
                                if st >= 1:
                                    weigh(n, slot, st - 1)
                                elif not first:
                                    weigh(n - 1, 1 - slot, len(STEPS) - 1)
                            scores(n, slot, st, h)
                            for _ in range((h + 1) * n_jobs // HG - h * n_jobs // HG):
                                if k % MROWS == 0:
                                    pe.wait_ge(T[f"loaded{1 - slot}{k // MROWS}"],
                                               b * (2 * LOADS) + ((g + 1) // 2 + 1) * LOADS)
                                take_max(k, base, 1 - slot)
                                k += 1
                        if st == 1 and not first:
                            pe.wait_ge(T["m_split"], n * 2 + 2)
                            result_T(n - 1, 1)
                        if g == 0 and not first:
                            if st in (2, 4):
                                context_T(b - 1, st // 2 - 1)
                            if st in (3, 5):
                                project_out(b - 1, st // 2 - 1)
                        if st == 6 and more:
                            if first:
                                pe.wait_ge(T["m_split"], 2)
                            elif g == 0:
                                pe.wait_ge(T["xadd"], b * 2)
                            else:
                                pe.wait_ge(T["ctx"], n * 2)
                            maxima_T(0, base + MROWS)
                        if st == 7:
                            if more:
                                pe.wait_ge(T["m_split"], n * 2 + 3)
                            else:
                                pe.wait_ge(T["ctx"], n * 2)
                            result_T(n, 0)
                        if st == len(STEPS) - 1:
                            pe.wait_ge(T["ctx"], n * 2 + 1)
                            if more:
                                maxima_T(1, base + len(JOBS))
                            else:
                                pe.wait_ge(FS[1]["norm"], SUB)
                                transpose4(bank(7), ntok).then_inc(FS[1]["xT"], 1)

                k = 0
                for r in range(PROJECT_STEPS):
                    project_step(TILES - 1, r)
                    for _ in range(JOBS_BESIDE[r]):
                        if k % MROWS == 0:
                            pe.wait_ge(T[f"loaded0{k // MROWS}"], LOADS)
                        take_max(k, 0, 0)
                        k += 1
                    if r == 5:
                        pe.wait_ge(FS[0]["xadd"], TILES + 1)
                        maxima_T(0, MROWS)
                pe.wait_ge(T["m_split"], 1)
                maxima_T(1, len(JOBS))
                wait_stored(pe)
                unit(0, 0, first=True)
                with pe.Fori(0, B - 1) as b:
                    for g in range(1, NG):
                        unit(b, g)
                    unit(b + 1, 0)
                for g in range(1, NG):
                    unit(B - 1, g, last=True)
                weigh(UNITS - 1, 1, len(STEPS) - 1)
                pe.wait_ge(FS[1]["xlo"], 1)
                result_T(UNITS - 1, 1)
                for u in range(2):
                    context_T(B - 1, u)
                    project_out(B - 1, u)
                pe.wait_ge(T["xadd"], B * 2)

            pe.wait_ge(s["split_lo"], 12)
            ffn(FS[0], True)
            attention()
            ffn(FS[1], False)

        @block.scalar
        def _(act):
            a = nc.scalar
            load_rows(act)
            def small_matrices():
                act.wait_ge(s["wraw_T"], 1)
                for k in range(4):
                    w = min(T_IN - 4 * k, 4) * P
                    a.copy(wt[:, k * NT:k * NT + w], bank(k)[:, 0:w]).then_inc(s["wt_ready"], 1)
                for dst, src in w_in_blocks(win_hi):
                    a.copy(dst, src).then_inc(s["wt_ready"], 1)
                a.copy(wout[:], bank(4)[:, 2 * P:3 * P]).then_inc(s["wt_ready"], 1)
                act.wait_ge(s["par_ready"], 1)

            def sequence_step(b, p, first=False):
                for u in range(2):
                    src, sl = bank(5 + u), slice(u * NT, (u + 1) * NT)
                    blocks = range(SUB * u, SUB * (u + 1))
                    if p == AT["tok"][u]:
                        act.wait_ge(s["a_lns"], b + 1)
                        if not first:
                            act.wait_ge(s["a_dn"], b * 2)
                        for j in blocks:
                            a.activation(hc_tok[:, j * P:(j + 1) * P], xs(b * BLK + j), ACT.Identity,
                                         bias=lns[:, L_BOTH_BIAS, j:j + 1],
                                         scale=lns[:, L_BOTH, j:j + 1]).then_inc(s["a_toka"], 1)
                    if p == AT["copy"][u]:
                        act.wait_ge(s["a_T"], b * 2 + u + 1)
                        a.activation(hT[:, TAPS - 1 + u * NT:TAPS - 1 + (u + 1) * NT], bank(6), ACT.Identity,
                                     bias=col(R_CONV_B), scale=col(R_CONV_G)).then_inc(s["a_hT"], 1)
                    for name, got, done in (("norm5", "a_pool", "a_n5"), ("norm9", "a_pool", "a_n9")):
                        if p == AT[name][u]:
                            act.wait_ge(s[got], b * 16 + 4 * u + (4 if name == "norm5" else 12))
                            for j in blocks:
                                a.activation(a0_tok[:, j * P:(j + 1) * P], src[:, (j % SUB) * P:(j % SUB + 1) * P],
                                             ACT.Identity, bias=lna[:, 3, j:j + 1],
                                             scale=lna[:, 1, j:j + 1]).then_inc(s[done], 1)
                    for name, got, done, bias, scale in (("h2", "a_T7", "a_h2", R_ATTN_B, R_ATTN_G),
                                                         ("h3", "a_T10", "a_h3", R_BOOM_B, R_BOOM_G)):
                        if p == AT[name][u]:
                            act.wait_ge(s[got], b * 2 + u + 1)
                            a.activation(h2T[:, sl], src, ACT.Identity, bias=col(bias),
                                         scale=col(scale)).then_inc(s[done], 1)
                    if u == 0 and p in UP_AT[0:4]:
                        n = UP_AT.index(p)
                        act.wait_ge(s["a_up"], b * 8 + n + 1)
                        a.activation(gel[:, n, :], bank(5 + n % 2), ACT.Identity,
                                     bias=col(R_BB + n)).then_inc(s["a_hid0"], 1)
                    if p == AT["gelu"][u]:
                        act.wait_ge(s[f"a_hid{u}"], b * 4 + 4)
                        a.activation(gel[:, 4 * u:4 * u + 4, :], gel[:, 4 * u:4 * u + 4, :],
                                     ACT.Gelu).then_inc(s["a_gel"], 1)

            for p in range(2 * CH):
                if p == AT["copy"][0]:
                    small_matrices()
                sequence_step(0, p, first=True)
                if p in SPLIT_AT:
                    r = SPLIT_AT.index(p)
                    act.wait_ge(s[f"raw_loaded{r % 2}"], (r // 2 + 1) * 48)
                    for m in range(3):
                        a.copy(w_hi[m][:, r * S:(r + 1) * S], raw[r % 2][m][:]).then_inc(s["split_hi"], 1)

            def project_step(t, r):
                if r == 3:
                    act.wait_ge(G["xT"], t + 1)
                    a.copy(xp_hi[:], bank(5)).then_inc(G["xhi"], 1)
                if r == 5:
                    if t >= RING:
                        act.wait_ge(G[f"stored{t % RING}"], 48 * (t // RING))
                    for m in range(2):
                        act.wait_ge(G["qk"], t * 2 + m + 1)
                        a.activation(part(t, m, 0), bank(5 + m), ACT.Copy,
                                     scale=SCALE if m == 0 else 1.0).then_inc(G["first"], 1)
                if r == 7:
                    act.wait_ge(G["v"], t + 1)
                    a.copy(v_out[:, t % RING, :], bank(5)).then_inc(G["vcopy"], 1)
                if r == 8:
                    for m in range(2):
                        act.wait_ge(G["rest"], t * 2 + m + 1)
                        a.copy(part(t, m, 1), qkr[:, t % 2, m, :]).then_inc(G["second"], 1)

            def ffn(f, sequences):
                def silu(c):
                    a.activation(sg[:, c % 2, :], bank(c % 2), ACT.Silu).then_inc(f["silu"], 1)

                def split_input(h):
                    a.copy(xn_hi[:, h, :], bank(7)).then_inc(f["xhi"], 1)

                def pair(i, last):
                    for h in range(2):
                        t = i * 2 + h
                        end = last and h == 1
                        for c in range(CH):
                            k = i * (2 * CH) + (h * CH + c)
                            if not (end and c == CH - 1):
                                act.wait_ge(f["gate"], k + 2)
                                silu((c + 1) % CH)
                            else:
                                act.wait_ge(f["dn"], (TILES * (CH - 1)) - 1)
                            act.wait_ge(f["prod"], k + 1)
                            a.copy(h_hi[:, c % 2, :], hid[:, c % 4, :]).then_inc(f["hhi"], 1)
                            if c == 0:
                                act.wait_ge(f["y_done"], t + 1)
                                a.copy(yS[:], bank(4)).then_inc(f["y_out"], 1)
                            if c == NORM_AT[h] + 4 and not end:
                                act.wait_ge(f["xT"], t + 2)
                                split_input(1 - h)
                            if sequences and not last:
                                sequence_step(i + 1, h * CH + c)
                            if sequences and last and h * CH + c >= PROJECT_FROM:
                                project_step(*divmod(h * CH + c - PROJECT_FROM, PROJECT_STEPS))

                if sequences:
                    act.wait_ge(f["xT"], 1)
                    split_input(0)
                act.wait_ge(f["gate"], 1)
                silu(0)
                with act.Fori(0, TILES // 2 - 1) as i:
                    pair(i, False)
                pair(TILES // 2 - 1, True)
                act.wait_ge(f["y_done"], TILES + 1)
                a.copy(yS[:], bank(4)).then_inc(f["y_out"], 1)

            def attention():
                def place_values(b, g):
                    act.wait_ge(T["v_loaded"], b * 16 + 16)
                    a.copy(vp[:, g % 2, :, :, 0:HD],
                           v_tok[:, :, g * HG * HD:(g + 1) * HG * HD].rearrange("p j (h d) -> p j h d", h=HG)
                           ).then_inc(T["vp"], 1)

                def result_out(n, c):
                    act.wait_ge(T["pv"], n * 2 + c + 1)
                    if not (isinstance(n, int) and n * 2 + c == 0):
                        act.wait_ge(T["oT"], n * 2 + c)
                    a.copy(ntok[:], bank(6)).then_inc(T["o_out"], 1)

                def context_out(b, u):
                    act.wait_ge(T["cT"], b * 2 + u + 1)
                    if u == 1:
                        act.wait_ge(T["proj"], b * 2 + 1)
                    a.copy(ctxT[:], bank(7)).then_inc(T["c_out"], 1)

                def maxima_out(e, slot, c):
                    act.wait_ge(T["m_parts"], e * 3 + 3)
                    act.dma_start(md[slot, c].rearrange("i r q -> r i q"), mpart[:]).then_inc(T["m_stored"], 16)

                def maxima_in(e, slot, c):
                    act.wait_ge(T["m_stored"], e * 16 + 16)
                    act.dma_start(qs[slot][K1:K2, :, c * NT:(c + 1) * NT],
                                  md[slot, c].rearrange("i (h n) q -> i h (n q)", h=HG)
                                  ).then_inc(T[f"m_loaded{c}"], 16)

                def unit(b, g, first=False, last=False):
                    n = b * NG + g
                    more = not (last and g == NG - 1)
                    for st, (c, j) in enumerate(STEPS):
                        w, share = WIDTH[st], SHARE[st]
                        for h in range(0, HG, share):
                            k = BEFORE[st] + h // share
                            act.wait_ge(T["scores"], n * NST + (k + 1))
                            a.activation(pr[:, st % 2, h:h + share, 0:w],
                                         bank(4 + k % 2)[:, 0:share * w].rearrange("p (h q) -> p h q", h=share),
                                         ACT.Exp).then_inc(T["exp"], 1)
                        if st == 0:
                            if not first:
                                result_out(n - 1, 1)
                            maxima_out(n * 2 + 1, g % 2, 1)
                            if first:
                                act.wait_ge(T["init"], 2)
                                place_values(0, 0)
                        if st == 1:
                            maxima_in(n * 2 + 1, g % 2, 1)
                        if st == 8 and more:
                            maxima_out(n * 2 + 2, 1 - g % 2, 0)
                        if st == 9 and more:
                            maxima_in(n * 2 + 2, 1 - g % 2, 0)
                        if st == 1 and more:
                            place_values(b + (g + 1) // NG, (g + 1) % NG)
                        if g == 0 and not first and st in (2, 4):
                            context_out(b - 1, st // 2 - 1)
                        if st == SUB:
                            result_out(n, 0)
                        if st == len(STEPS) - 1 and not more:
                            act.wait_ge(FS[1]["xT"], 1)
                            a.copy(xn_hi[:, 0, :], bank(7)).then_inc(FS[1]["xhi"], 1)

                for r in range(PROJECT_STEPS):
                    project_step(TILES - 1, r)
                    if r == 7:
                        maxima_out(0, 0, 0)
                maxima_in(0, 0, 0)
                unit(0, 0, first=True)
                with act.Fori(0, B - 1) as b:
                    for g in range(1, NG):
                        unit(b, g)
                    unit(b + 1, 0)
                for g in range(1, NG):
                    unit(B - 1, g, last=True)
                result_out(UNITS - 1, 1)
                for u in range(2):
                    context_out(B - 1, u)

            ffn(FS[0], True)
            attention()
            ffn(FS[1], False)

        @block.vector
        def _(dve):
            v = nc.vector
            v.memset(zcol[:], 0.0).then_inc(s["zeros"], 1)
            dve.wait_ge(s["zeros"], 1)

            def parameters():
                dve.wait_ge(s["par_T"], 1)
                v.tensor_copy(par[:], bank(7)[:, 0:PAR_ROWS]).then_inc(s["par_ready"], 1)
                dve.wait_ge(s["wt_ready"], 8)
                for (dst, src), (hi, _) in zip(w_in_blocks(win_lo), w_in_blocks(win_hi)):
                    v.tensor_tensor(dst, src, hi.bitcast(F32), ALU.subtract).then_inc(s["wt_ready"], 1)

            def positions():
                dve.wait_ge(s["pool_setup"], SETUP_MATRICES + 1)
                v.tensor_copy(cq[:], rinv[:].bitcast(I32)).then_inc(s["rinv_ready"], 1)
                dve.wait_ge(s["rinv_ready"], 1)
                v.reciprocal(rinv[:], cq[:]).then_inc(s["rinv_ready"], 1)

            def norm_steps(f, st=st, mv=mv, lnw=lnw, ntok=ntok):
                def stats4(t, n0):
                    for j in range(SUB):
                        v.bn_stats(st[:, j, :], xs(t * SUB + j)).then_inc(f["st"], 1)
                    dve.wait_ge(f["st"], n0 + SUB)
                    v.memset(fence[:], 0.0)
                    for j in range(SUB):
                        v.bn_aggr(mv[:, j, :], st[:, j, :]).then_inc(f["mv"], 1)

                def norm4(t):
                    for j in range(SUB):
                        v.tensor_scalar(ntok[:, j * P:(j + 1) * P], xs(t * SUB + j), mv[:, j, 0:1],
                                        lnw[:, 1, j:j + 1], ALU.subtract, ALU.mult).then_inc(f["norm"], 1)

                return stats4, norm4

            def first_norm(f, step):
                stats4, norm4 = norm_steps(f)
                if step == 0:
                    stats4(0, 0)
                if step == 3:
                    dve.wait_ge(f["rs"], 2)
                    norm4(0)
                if step == 5:
                    dve.wait_ge(f["xhi"], 1)
                    v.tensor_tensor(xn_lo[:, 0, :], bank(7), xn_hi[:, 0, :].bitcast(F32),
                                    ALU.subtract).then_inc(f["xlo"], 1)

            def stats_of_input(lo, hi):
                for j in range(lo, hi):
                    v.bn_stats(stx[:, j, :], xs(j)).then_inc(s["a_stx"], 1)
                dve.wait_ge(s["a_stx"], hi)
                for j in range(lo, hi):
                    v.bn_aggr(mvx[:, j, :], stx[:, j, :]).then_inc(s["a_mvx"], 1)

            def inner_stats(b, u, T_, st_, mv_):
                dve.wait_ge(s[T_], b * 2 + u + 1)
                for j in range(SUB):
                    v.bn_stats(sta[:, u * SUB + j, :], bank(5 + u)[:, j * P:(j + 1) * P]).then_inc(s[st_], 1)
                dve.wait_ge(s[st_], b * BLK + SUB * (u + 1))
                v.memset(fence[:], 0.0)
                for j in range(u * SUB, (u + 1) * SUB):
                    v.bn_aggr(mva[:, j, :], sta[:, j, :]).then_inc(s[mv_], 1)

            def sequence_step(b, p):
                if p == AT["tok"][0]:
                    v.tensor_copy(lns[:], lnx[:, :, bass.ds(b * BLK, BLK)]).then_inc(s["a_lns"], 1)
                    dve.wait_ge(s["a_lns"], b + 1)
                for u in range(2):
                    sl = slice(u * NT, (u + 1) * NT)
                    if p == AT["tok"][u]:
                        for j in range(SUB * u, SUB * (u + 1)):
                            v.tensor_scalar(a0_tok[:, j * P:(j + 1) * P], xs(b * BLK + j), lns[:, L_MEAN, j:j + 1],
                                            lns[:, L_RSTD, j:j + 1], ALU.subtract, ALU.mult).then_inc(s["a_tokd"], 1)
                    if p == AT["copy"][u]:
                        dve.wait_ge(s["a_T"], b * 2 + u + 1)
                        v.tensor_copy(a0T[:, sl], bank(5)).then_inc(s["a_copyD"], 1)
                    if p == AT["a1"][u]:
                        dve.wait_ge(s["a_conv"], b * 2 + u + 1)
                        dve.wait_ge(s["a_copyD"], b * 2 + u + 1)
                        v.scalar_tensor_tensor(a0T[:, sl], bank(5 + u), col(R_CONV_BIAS), a0T[:, sl],
                                               ALU.add, ALU.add).then_inc(s["a_a1"], 1)
                    if p == AT["stats5"][u]:
                        inner_stats(b, u, "a_T5", "a_st5", "a_mv5")
                    if p == AT["cumq"][u]:
                        dve.wait_ge(s["a_q"], b * 2 + u + 1)
                        if u == 1:
                            dve.wait_ge(s["a_cumq"], b * 2 + 1)
                        v.tensor_tensor_scan(cq[:, sl], bank(5 + u), col(R_BQ).to_broadcast([P, NT]),
                                             0.0 if u == 0 else cq[:, NT - 1:NT], ALU.add, ALU.add
                                             ).then_inc(s["a_cumq"], 1)
                    if p == AT["kq"][u]:
                        dve.wait_ge(s["a_k"], b * 2 + u + 1)
                        dve.wait_ge(s["a_meanq"], b * 2 + u + 1)
                        v.scalar_tensor_tensor(pq[:, sl], bank(6 - u), col(R_BK), pq[:, sl], ALU.add,
                                               ALU.mult).then_inc(s["a_kq"], 1)
                    if p == AT["cumk"][u]:
                        dve.wait_ge(s["a_kq"], b * 2 + u + 1)
                        if u == 1:
                            dve.wait_ge(s["a_cumk"], b * 2 + 1)
                        v.tensor_tensor_scan(hc_tok[:, sl], pq[:, sl], zcol[:].to_broadcast([P, NT]),
                                             0.0 if u == 0 else hc_tok[:, NT - 1:NT], ALU.add, ALU.add
                                             ).then_inc(s["a_cumk"], 1)
                    if p == AT["vq"][u]:
                        dve.wait_ge(s["a_v"], b * 2 + u + 1)
                        dve.wait_ge(s["a_meank"], b * 2 + u + 1)
                        v.scalar_tensor_tensor(pq[:, sl], bank(5 + u), col(R_BV), pq[:, sl], ALU.add,
                                               ALU.mult).then_inc(s["a_vq"], 1)
                    if p == AT["stats9"][u]:
                        inner_stats(b, u, "a_T9", "a_st9", "a_mv9")
                    if u == 1 and p == UP_AT[4] - 1:
                        for n in range(4, 8):
                            dve.wait_ge(s["a_up"], b * 8 + n + 1)
                            v.tensor_scalar(gel[:, n, :], bank(5 + n % 2), col(R_BB + n - 4), None,
                                            ALU.add).then_inc(s["a_hid1"], 1)
                    if p == AT["y"][u]:
                        dve.wait_ge(s["a_dn"], b * 2 + u + 1)
                        v.scalar_tensor_tensor(a0T[:, sl], bank(5 + u), col(R_BU), a0T[:, sl], ALU.add,
                                               ALU.add).then_inc(s["a_y"], 1)
                    if p == AT["x1"][u]:
                        dve.wait_ge(s["a_T13"], b * 2 + u + 1)
                        v.tensor_tensor(xs(b * BLK + SUB * u, SUB), xs(b * BLK + SUB * u, SUB), bank(5 + u),
                                        ALU.add).then_inc(s["a_x1"], 1)

            dve.wait_ge(s["x_loaded"], 16)
            stats_of_input(0, BLK)
            dve.wait_ge(s["a_lnx"], 10)
            for p in range(2 * CH):
                if p == AT["copy"][0]:
                    parameters()
                    dve.wait_ge(s["par_ready"], 1)
                if p == AT["cumq"][0]:
                    dve.wait_ge(s["rinv_ready"], 2)
                sequence_step(0, p)
                if p == AT["stats5"][1]:
                    positions()
                if p == AT["stats9"][1]:
                    dve.wait_ge(s["x_rest_loaded"], 16 * (B - 1))
                    stats_of_input(BLK, B * BLK)
                if p == AT["x1"][0]:
                    dve.wait_ge(s["a_x1"], 1)
                    first_norm(FS[0], 0)
                if p == AT["x1"][1]:
                    first_norm(FS[0], 3)
                if p == SPLIT_AT[3]:
                    dve.wait_ge(s["split_hi"], 12)
                    for m in range(3):
                        v.tensor_tensor(w_lo[m][:, 3 * S:], raw[1][m][:], w_hi[m][:, 3 * S:].bitcast(F32),
                                        ALU.subtract).then_inc(s["split_lo"], 1)
            dve.wait_ge(s["a_lnx"], 20)

            def project_step(t, r):
                stats4, norm4 = norm_steps(G, stp, mvp, lnp, ntok2)
                if r == 0:
                    dve.wait_ge(FS[0]["xadd"], t + 2)
                    stats4(t, t * SUB)
                if r == 2:
                    dve.wait_ge(G["rs"], t * 2 + 2)
                    norm4(t)
                if r == 3:
                    dve.wait_ge(G["xhi"], t + 1)
                    v.tensor_tensor(xp_lo[:], bank(5), xp_hi[:].bitcast(F32), ALU.subtract).then_inc(G["xlo"], 1)
                if r in (6, 7):
                    m = r - 6
                    dve.wait_ge(G["first"], t * 2 + m + 1)
                    if t >= 2:
                        dve.wait_ge(G["third"], t * 2 - 3 + m)
                    v.scalar_tensor_tensor(qkr[:, t % 2, m, :], bank(5 + m), SCALE if m == 0 else 1.0,
                                           part(t, m, 0), ALU.mult, ALU.subtract).then_inc(G["rest"], 1)

            def ffn(f, sequences):
                stats4, norm4 = norm_steps(f)

                def product(c):
                    v.tensor_tensor(hid[:, c % 4, :], sg[:, c % 2, :], bank(2 + c % 2), ALU.mult).then_inc(f["prod"], 1)

                def split_input(h):
                    v.tensor_tensor(xn_lo[:, h, :], bank(7), xn_hi[:, h, :].bitcast(F32),
                                    ALU.subtract).then_inc(f["xlo"], 1)

                def pair(i, last):
                    for h in range(2):
                        t = i * 2 + h
                        end = last and h == 1
                        for c in range(CH):
                            k = i * (2 * CH) + (h * CH + c)
                            if not (end and c == CH - 1):
                                dve.wait_ge(f["up"], k + 2)
                                dve.wait_ge(f["silu"], k + 2)
                                product((c + 1) % CH)
                            dve.wait_ge(f["hhi"], k + 1)
                            v.tensor_tensor(h_lo[:, c % 2, :], hid[:, c % 4, :], h_hi[:, c % 2, :].bitcast(F32),
                                            ALU.subtract).then_inc(f["hlo"], 1)
                            if c == 5:
                                dve.wait_ge(f["yT"], t + 1)
                                v.tensor_tensor(xs(t * SUB - SUB, SUB), xs(t * SUB - SUB, SUB), bank(7),
                                                ALU.add).then_inc(f["xadd"], 1)
                            if end:
                                if sequences:
                                    project_step(*divmod(h * CH + c - PROJECT_FROM, PROJECT_STEPS))
                                continue
                            if sequences and not last:
                                sequence_step(i + 1, h * CH + c)
                            if c == NORM_AT[h]:
                                if sequences:
                                    dve.wait_ge(s["a_x1"], t + 2)
                                stats4(t + 1, t * SUB + SUB)
                            if c == NORM_AT[h] + 3:
                                dve.wait_ge(f["rs"], t * 2 + 4)
                                norm4(t + 1)
                            if c == NORM_AT[h] + 5:
                                dve.wait_ge(f["xhi"], t + 2)
                                split_input(1 - h)
                            if sequences and last and c >= PROJECT_FROM:
                                project_step(*divmod(c - PROJECT_FROM, PROJECT_STEPS))

                v.memset(x[:, 0:NT], 0.0)
                v.memset(bank(4), 0.0).then_inc(f["y_done"], 1)
                if sequences:
                    first_norm(f, 5)
                dve.wait_ge(f["up"], 1)
                dve.wait_ge(f["silu"], 1)
                product(0)
                with dve.Fori(0, TILES // 2 - 1) as i:
                    pair(i, False)
                pair(TILES // 2 - 1, True)
                dve.wait_ge(f["yT"], TILES + 1)
                v.tensor_tensor(xs(TILES * SUB - SUB, SUB), xs(TILES * SUB - SUB, SUB), bank(7),
                                ALU.add).then_inc(f["xadd"], 1)

            def attention():
                def reduce_job(k, base):
                    h, i = JOBS[k]
                    c, col_ = divmod(k, MROWS)
                    dve.wait_ge(T["job"], base + (k + 1))
                    v.tensor_reduce(negm[:, c, col_:col_ + 1],
                                    ps[:, job_bank(k):job_bank(k) + 1 + i // SUB, :].rearrange(
                                        "p a n -> p (a n)")[:, 0:(i + 1) * P],
                                    AX.X, ALU.max, negate=True).then_inc(T["reduced"], 1)

                def split_max(e):
                    src = bank(7)[0:MROWS, 0:P]
                    if not (isinstance(e, int) and e == 0):
                        dve.wait_ge(T["m_stored"], e * 16)
                    dve.wait_ge(T["mT"], e + 1)
                    v.tensor_copy(mpart[:, 0, :], src).then_inc(T["m_parts"], 1)
                    dve.wait_ge(T["m_parts"], e * 3 + 1)
                    v.tensor_tensor(mres[:], src, mpart[:, 0, :], ALU.subtract).then_inc(T["m_split"], 1)
                    dve.wait_ge(T["m_split"], e + 1)
                    v.tensor_copy(mpart[:, 1, :], mres[:]).then_inc(T["m_parts"], 1)
                    dve.wait_ge(T["m_parts"], e * 3 + 2)
                    v.tensor_tensor(mpart[:, 2, :], mres[:], mpart[:, 1, :],
                                    ALU.subtract).then_inc(T["m_parts"], 1)

                def normalise(n, g, c):
                    src = bank(7).rearrange("p (t h w) -> p t h w", t=SUB, h=HG)
                    dve.wait_ge(T["oT"], n * 2 + c + 1)
                    v.reciprocal(rl[:], src[:, :, :, HD]).then_inc(T["onorm"], 1)
                    dve.wait_ge(T["onorm"], n * 2 + c + 1)
                    v.tensor_tensor(
                        ctxt[:, c * SUB:(c + 1) * SUB, g * HG * HD:(g + 1) * HG * HD].rearrange(
                            "p t (h d) -> p t h d", h=HG),
                        src[:, :, :, 0:HD], rl[:].unsqueeze(3).to_broadcast([P, SUB, HG, HD]),
                        ALU.mult).then_inc(T["ctx"], 1)

                def add_projection(b, u):
                    dve.wait_ge(T["proj"], b * 2 + u + 1)
                    v.tensor_tensor(xs(b * BLK + u * SUB, SUB), xs(b * BLK + u * SUB, SUB), bank(7),
                                    ALU.add).then_inc(T["xadd"], 1)

                def unit(b, g, first=False, last=False):
                    n = b * NG + g
                    more = not (last and g == NG - 1)
                    k = 0
                    for st in range(len(STEPS)):
                        if st == 0 and not first:
                            split_max(n * 2 + 1)
                        if st == 2 and not first:
                            normalise(n - 1, (g - 1) % NG, 1)
                        if g == 0 and not first and st in (4, 6):
                            add_projection(b - 1, st // 2 - 2)
                        if st == 7 and more:
                            split_max(n * 2 + 2)
                        if st == 8:
                            normalise(n, g, 0)
                        if not more and st >= 8:
                            first_norm(FS[1], st - 8)
                        for _ in range(JOBS_AFTER[st] if more else 0):
                            reduce_job(k, n * len(JOBS) + len(JOBS))
                            k += 1

                k = 0
                for r in range(PROJECT_STEPS):
                    project_step(TILES - 1, r)
                    for _ in range(JOBS_BESIDE[r]):
                        reduce_job(k, 0)
                        k += 1
                    if r == 5:
                        split_max(0)
                split_max(1)
                unit(0, 0, first=True)
                with dve.Fori(0, B - 1) as b:
                    for g in range(1, NG):
                        unit(b, g)
                    unit(b + 1, 0)
                for g in range(1, NG):
                    unit(B - 1, g, last=True)
                first_norm(FS[1], 5)
                normalise(UNITS - 1, NG - 1, 1)
                for u in range(2):
                    add_projection(B - 1, u)

            ffn(FS[0], True)
            attention()
            ffn(FS[1], False)


LOADS = 16 * (PARTS + PARTS * PARTS + 2)


SETUP_MATRICES = 11


NAMES = {"hidden": "attn_a_hidden_states", "conv_w": "attn_a_conv_w", "conv_b": "attn_a_conv_b",
         "ln_conv_g": "attn_a_ln_conv_g", "ln_conv_b": "attn_a_ln_conv_b",
         "ln_attn_g": "attn_a_ln_attn_g", "ln_attn_b": "attn_a_ln_attn_b",
         "ln_boom_g": "attn_a_ln_boom_g", "ln_boom_b": "attn_a_ln_boom_b",
         "Wq": "attn_a_Wq", "Wk": "attn_a_Wk", "Wv": "attn_a_Wv", "bq": "attn_a_bq",
         "bk": "attn_a_bk", "bv": "attn_a_bv", "Wb": "attn_a_Wb", "bb": "attn_a_bb",
         "Wu": "attn_a_Wu", "bu": "attn_a_bu", "w_in": "attn_b_w_in", "w_out": "attn_b_w_out",
         "Wg": "ffn_Wg", "Wu8": "ffn_Wu", "Wd": "ffn_Wd"}


def bf16_parts(a, n):
    parts, rest = [], np.asarray(a, np.float64)
    for _ in range(n):
        p = rest.astype(BF16_NP)
        parts.append(p)
        rest = rest - p.astype(np.float64)
    return parts


def alibi_rows():
    slope = (2.0 ** (-8.0 / HEADS * (np.arange(HEADS, dtype=np.float32) + 1.0))).astype(np.float32)
    pos = np.arange(S)
    cut = [(pos // P * P).astype(BF16_NP), (pos % P).astype(BF16_NP)]
    k_rows = np.ones((AL_ROWS + PARTS, HEADS, S), BF16_NP)
    q_rows = np.zeros((AL_ROWS, HEADS, S), BF16_NP)
    r = 0
    for c in cut:
        for p in bf16_parts(slope, PARTS):
            k_rows[r], q_rows[r] = c[None, :], p[:, None]
            k_rows[r + 1], q_rows[r + 1] = -p[:, None], c[None, :]
            r += 2
    return k_rows, q_rows


def kernel(**inputs):
    import concourse.bacc as bacc
    from concourse.bass_utils import run_bass_kernel_spmd

    nc = bacc.Bacc("TRN2", target_bir_lowering=False, num_devices=1)
    arrays, aps = {}, {}
    for short, name in NAMES.items():
        arrays[f"in_{short}"] = np.ascontiguousarray(inputs["L0_" + name])
    arrays["in_al_k"], arrays["in_al_q"] = alibi_rows()
    for name, a in arrays.items():
        aps[name[3:]] = nc.dram_tensor(name, a.shape, mybir.dt.from_np(a.dtype), kind="ExternalInput").ap()
    aps["out"] = nc.dram_tensor("out_0", (B, S, D), F32, kind="ExternalOutput").ap()
    build(nc, aps)
    r = run_bass_kernel_spmd(nc, [arrays], core_ids=[0])
    return r.results[0]["out_0"]
```
